# Optimizing a Trainium2 kernel written in Bass

```python
import numpy as np
import jax
import jax.numpy as jnp

def _softmax(x, axis=-1):
    return jax.nn.softmax(x, axis=axis)

def _gelu(x):
    return jax.nn.gelu(x, approximate=True)

def _silu(x):
    return jax.nn.silu(x)

def _sigmoid(x):
    return jax.nn.sigmoid(x)

def _layernorm(x, axis=-1, eps=1e-05):
    m = jnp.mean(x, axis=axis, keepdims=True)
    v = jnp.var(x, axis=axis, keepdims=True)
    return (x - m) / jnp.sqrt(v + eps)

def _scatter_add(tgt, idx, src, axis=0):
    return tgt.at[idx].add(src)

def _segment_sum(src, seg, n):
    return jax.ops.segment_sum(src, seg, n)
kernel_name = 'mk_decoder_preln_d2_seqx_r8_949e3b'

def setup_inputs(seed: int=0):
    np.random.seed(seed)
    _w = jnp.asarray

    def _rec_inputs():
        import jax
        import jax.numpy as jnp
        _rk = jax.random.key(seed)
        x = 0.000341 + 1 * jax.random.normal(jax.random.fold_in(_rk, 1), (16, 128, 256), jnp.float32)
        _lenS = 128 - jax.random.randint(jax.random.fold_in(_rk, 7), (16,), 0, max(1, 128 // 4) + 1, jnp.int32)
        _lenS2 = 128 - jax.random.randint(jax.random.fold_in(_rk, 8), (16,), 0, max(1, 128 // 4) + 1, jnp.int32)
        _ctx_2048P = jax.random.normal(jax.random.fold_in(_rk, 11), (16, 16, 256), jnp.float32)
        _ctx_2048c = jax.random.dirichlet(jax.random.fold_in(_rk, 511), 0.3 * jnp.ones((16,), jnp.float32), (16, 128))
        _ctx_2048t = jnp.einsum('bsk,bkd->bsd', _ctx_2048c, _ctx_2048P)
        _ctx_2048t = _ctx_2048t * jax.lax.rsqrt(jnp.mean(jnp.square(_ctx_2048t)) + 1e-12) * 0.953939
        ctx_2048 = -1.47943e-05 + 1.00017 * (_ctx_2048t + 0.3 * jax.random.normal(jax.random.fold_in(_rk, 611), (16, 128, 256), jnp.float32))
        return (x, ctx_2048)
    x, ctx_2048 = _rec_inputs()

    def _L0_attn_setup():
        import jax, jax.numpy as jnp
        import numpy as np
        from jax import lax
        D_MODEL = 256
        D_STATE = 64
        D_CONV = 4
        EXPAND = 2
        HEADDIM = 64
        D_INNER = D_MODEL * EXPAND
        NHEADS = D_INNER // HEADDIM
        CONV_DIM = D_INNER + 2 * D_STATE
        D_IN_PROJ = 2 * D_INNER + 2 * D_STATE + NHEADS
        NUM_EXPERTS = 8
        TOP_K = 2
        D_FF = 4 * D_MODEL
        BATCH = 2
        SEQ = 64
        EPS = 1e-06

        def rmsnorm(x, w):
            return x * lax.rsqrt(jnp.mean(x * x, axis=-1, keepdims=True) + EPS) * w

        def silu(x):
            return x * jax.nn.sigmoid(x)

        def mamba2(x, in_proj_w, conv_w, conv_b, dt_bias, A_log, Dp, ssm_norm_w, out_proj_w):
            Bsz, L, _ = x.shape
            zxbcdt = x @ in_proj_w.T
            z, xBC, dt = jnp.split(zxbcdt, [D_INNER, D_INNER + CONV_DIM], axis=-1)
            xBC = lax.conv_general_dilated(xBC.transpose(0, 2, 1), conv_w[:, None, :], (1,), [(D_CONV - 1, 0)], feature_group_count=CONV_DIM)
            xBC = silu((xBC + conv_b[None, :, None]).transpose(0, 2, 1))
            xs, Bm, Cm = jnp.split(xBC, [D_INNER, D_INNER + D_STATE], axis=-1)
            dt = jax.nn.softplus(dt + dt_bias)
            A = -jnp.exp(A_log)
            xh = xs.reshape(Bsz, L, NHEADS, HEADDIM)

            def step(h, inp):
                dt_t, x_t, B_t, C_t = inp
                dA = jnp.exp(dt_t * A)
                h = h * dA[:, :, None, None] + dt_t[:, :, None, None] * x_t[..., None] * B_t[:, None, None, :]
                y = jnp.einsum('bhpn,bn->bhp', h, C_t)
                return (h, y)
            h0 = jnp.zeros((Bsz, NHEADS, HEADDIM, D_STATE), x.dtype)
            _, ys = lax.scan(step, h0, (dt.transpose(1, 0, 2), xh.transpose(1, 0, 2, 3), Bm.transpose(1, 0, 2), Cm.transpose(1, 0, 2)))
            y = ys.transpose(1, 0, 2, 3) + Dp[None, None, :, None] * xh
            y = y.reshape(Bsz, L, D_INNER)
            y = rmsnorm(y * silu(z), ssm_norm_w)
            return y @ out_proj_w.T

        def moe(x, gate_w, w1, w2):
            T = x.shape[0] * x.shape[1]
            xf = x.reshape(T, D_MODEL)
            logits = xf @ gate_w.T
            vals, idx = lax.top_k(logits, TOP_K)
            wts = jax.nn.softmax(vals, axis=-1)
            combine = jnp.sum(jax.nn.one_hot(idx, NUM_EXPERTS, dtype=x.dtype) * wts[..., None], axis=1)
            h = silu(jnp.einsum('td,efd->tef', xf, w1))
            eo = jnp.einsum('tef,edf->ted', h, w2)
            out = jnp.einsum('ted,te->td', eo, combine)
            probs = jax.nn.softmax(logits, axis=-1)
            lb = NUM_EXPERTS * jnp.sum(jnp.mean(probs, axis=0) ** 2)
            return (out.reshape(x.shape), lb)

        def safety(x, sp1_w, sp1_b, sp2_w, sp2_b, harm_w, harm_b, unc_w, unc_b, tox_w, tox_b):
            f = silu(x @ sp1_w.T + sp1_b) @ sp2_w.T + sp2_b
            harm = f @ harm_w.T + harm_b
            unc = jax.nn.sigmoid(f @ unc_w.T + unc_b)[..., 0]
            tox = jax.nn.sigmoid(f @ tox_w.T + tox_b)[..., 0]
            hs = jax.nn.sigmoid(harm)
            return (hs.max(-1), jnp.argmax(hs, -1), unc, tox, harm)

        def _reference_tuple_inner(x, in_proj_w, conv_w, conv_b, dt_bias, A_log, D, ssm_norm_w, out_proj_w, norm_mamba_w, norm_moe_w, gate_w, w1, w2, sp1_w, sp1_b, sp2_w, sp2_b, harm_w, harm_b, unc_w, unc_b, tox_w, tox_b):
            residual = x
            h = rmsnorm(x, norm_mamba_w)
            h = mamba2(h, in_proj_w, conv_w, conv_b, dt_bias, A_log, D, ssm_norm_w, out_proj_w) + residual
            x_moe, lb_loss = moe(rmsnorm(h, norm_moe_w), gate_w, w1, w2)
            h = h + x_moe
            risk_vals, risk_idx, unc, tox, harm = safety(h, sp1_w, sp1_b, sp2_w, sp2_b, harm_w, harm_b, unc_w, unc_b, tox_w, tox_b)
            return (h, risk_vals, risk_idx, unc, tox, harm, lb_loss)
        ks = jax.random.split(jax.random.key(seed), 24)
        s = 0.02
        n = lambda k, shape, sc=s: jax.random.normal(k, shape, jnp.float32) * sc
        return {'x': jax.random.normal(ks[0], (BATCH, SEQ, D_MODEL), jnp.float32), 'in_proj_w': n(ks[1], (D_IN_PROJ, D_MODEL)), 'conv_w': n(ks[2], (CONV_DIM, D_CONV), 0.1), 'conv_b': n(ks[3], (CONV_DIM,), 0.01), 'dt_bias': n(ks[4], (NHEADS,), 0.1), 'A_log': jnp.log(jax.random.uniform(ks[5], (NHEADS,), jnp.float32, 1.0, 16.0)), 'D': jnp.ones((NHEADS,), jnp.float32), 'ssm_norm_w': jnp.ones((D_INNER,), jnp.float32), 'out_proj_w': n(ks[6], (D_MODEL, D_INNER)), 'norm_mamba_w': jnp.ones((D_MODEL,), jnp.float32), 'norm_moe_w': jnp.ones((D_MODEL,), jnp.float32), 'gate_w': n(ks[7], (NUM_EXPERTS, D_MODEL)), 'w1': n(ks[8], (NUM_EXPERTS, D_FF, D_MODEL)), 'w2': n(ks[9], (NUM_EXPERTS, D_MODEL, D_FF)), 'sp1_w': n(ks[10], (D_MODEL // 2, D_MODEL)), 'sp1_b': jnp.zeros((D_MODEL // 2,), jnp.float32), 'sp2_w': n(ks[11], (128, D_MODEL // 2)), 'sp2_b': jnp.zeros((128,), jnp.float32), 'harm_w': n(ks[12], (5, 128)), 'harm_b': jnp.zeros((5,), jnp.float32), 'unc_w': n(ks[13], (1, 128)), 'unc_b': jnp.zeros((1,), jnp.float32), 'tox_w': n(ks[14], (1, 128)), 'tox_b': jnp.zeros((1,), jnp.float32)}
    _L0_attn_all = _L0_attn_setup()
    _L0_attn_in = {k: v for k, v in _L0_attn_all.items() if k in ('in_proj_w', 'conv_w', 'conv_b', 'dt_bias', 'A_log', 'D', 'ssm_norm_w', 'out_proj_w', 'norm_mamba_w', 'norm_moe_w', 'gate_w', 'w1', 'w2', 'sp1_w', 'sp1_b', 'sp2_w', 'sp2_b', 'harm_w', 'harm_b', 'unc_w', 'unc_b', 'tox_w', 'tox_b')}
    del _L0_attn_all

    def _L0_xattn_setup():
        import jax, jax.numpy as jnp
        import numpy as np

        def _wkv(time_decay, time_first, k, v):
            w = -jnp.exp(time_decay)
            u = time_first
            B, T, C = k.shape
            aa = jnp.zeros((B, C), dtype=k.dtype)
            bb = jnp.zeros((B, C), dtype=k.dtype)
            pp = jnp.full((B, C), -1e+38, dtype=k.dtype)

            def step(carry, kv_t):
                aa, bb, pp = carry
                kt, vt = kv_t
                ww = u + kt
                q = jnp.maximum(pp, ww)
                e1 = jnp.exp(pp - q)
                e2 = jnp.exp(ww - q)
                y_t = (e1 * aa + e2 * vt) / (e1 * bb + e2)
                ww2 = pp + w
                q2 = jnp.maximum(ww2, kt)
                e1b = jnp.exp(ww2 - q2)
                e2b = jnp.exp(kt - q2)
                new_carry = (e1b * aa + e2b * vt, e1b * bb + e2b, q2)
                return (new_carry, y_t)
            ks = jnp.transpose(k, (1, 0, 2))
            vs = jnp.transpose(v, (1, 0, 2))
            _, ys = jax.lax.scan(step, (aa, bb, pp), (ks, vs))
            return jnp.transpose(ys, (1, 0, 2))
        key = jax.random.key(seed)
        k1, k2, k3, k4 = jax.random.split(key, 4)
        B, T, C = (8, 128, 256)
        return {'batch_size': B, 'seq_len': T, 'embedding_dim': C, 'time_decay': jax.random.normal(k1, (C,), dtype=jnp.float32), 'time_first': jax.random.normal(k2, (C,), dtype=jnp.float32), 'k': jax.random.normal(k3, (B, T, C), dtype=jnp.float32), 'v': jax.random.normal(k4, (B, T, C), dtype=jnp.float32)}
    _L0_xattn_all = _L0_xattn_setup()
    _L0_xattn_in = {k: v for k, v in _L0_xattn_all.items() if k in ('time_decay', 'time_first')}
    del _L0_xattn_all

    def _L0_ffn_setup():
        import jax, jax.numpy as jnp
        import numpy as np
        E = 8
        K = 2
        CAP = 64
        H = 256
        F = 1024
        key = jax.random.key(seed)
        ks = jax.random.split(key, 6)
        inp = {'hidden_states': jax.random.normal(ks[0], (2, 128, H), jnp.float32), 'router_w': jax.random.normal(ks[1], (E, H), jnp.float32) * (0.01 / np.sqrt(H)), 'w1': jax.random.normal(ks[2], (F, H), jnp.float32) * (1.0 / np.sqrt(H)), 'b1': jax.random.normal(ks[3], (F,), jnp.float32) * 0.01, 'w2': jax.random.normal(ks[4], (H, F), jnp.float32) * (1.0 / np.sqrt(F)), 'b2': jax.random.normal(ks[5], (H,), jnp.float32) * 0.01}
        return inp
    _L0_ffn_all = _L0_ffn_setup()
    _L0_ffn_in = {k: v for k, v in _L0_ffn_all.items() if k in ('router_w', 'w1', 'b1', 'w2', 'b2')}
    del _L0_ffn_all

    def _L1_attn_setup():
        import jax, jax.numpy as jnp
        import numpy as np
        B, L, D, H = (2, 512, 256, 16)
        K = D // H
        V = D // H
        EPS = 1e-05

        def _gla_recurrence(q, k, v, g):
            qs = jnp.moveaxis(q, 1, 0)
            ks = jnp.moveaxis(k, 1, 0)
            vs = jnp.moveaxis(v, 1, 0)
            gs = jnp.moveaxis(g, 1, 0)

            def step(S, inp):
                qt, kt, vt, gt = inp
                S = S * jnp.exp(gt)[..., None] + kt[..., None] * vt[..., None, :]
                yt = jnp.einsum('bhk,bhkv->bhv', qt, S)
                return (S, yt)
            S0 = jnp.zeros((q.shape[0], H, K, V), q.dtype)
            S_final, ys = jax.lax.scan(step, S0, (qs, ks, vs, gs))
            return (jnp.moveaxis(ys, 0, 1), S_final)

        def _layernorm(x, gamma, beta):
            mu = jnp.mean(x, axis=-1, keepdims=True)
            var = jnp.mean(jnp.square(x - mu), axis=-1, keepdims=True)
            return (x - mu) * jax.lax.rsqrt(var + EPS) * gamma + beta

        def _reference_tuple_inner(x, Wq, Wk, Wv, Wg, Wo, gamma, beta):
            b, l, d = x.shape
            q = (x @ Wq.T).reshape(b, l, H, K) * K ** (-0.5)
            k = (x @ Wk.T).reshape(b, l, H, K)
            v = (x @ Wv.T).reshape(b, l, H, V)
            g = jax.nn.log_sigmoid(x @ Wg.T).reshape(b, l, H, K)
            y, final_state = _gla_recurrence(q, k, v, g)
            y = y.reshape(b, l, d)
            o = _layernorm(y, gamma, beta) @ Wo.T
            return (o, final_state)
        key = jax.random.key(seed)
        ks = jax.random.split(key, 7)
        s = D ** (-0.5)
        return {'x': jax.random.normal(ks[0], (B, L, D), jnp.float32), 'Wq': jax.random.normal(ks[1], (D, D), jnp.float32) * s, 'Wk': jax.random.normal(ks[2], (D, D), jnp.float32) * s, 'Wv': jax.random.normal(ks[3], (D, D), jnp.float32) * s, 'Wg': jax.random.normal(ks[4], (D, D), jnp.float32) * s, 'Wo': jax.random.normal(ks[5], (D, D), jnp.float32) * s, 'gamma': jnp.ones((D,), jnp.float32), 'beta': jnp.zeros((D,), jnp.float32)}
    _L1_attn_all = _L1_attn_setup()
    _L1_attn_in = {k: v for k, v in _L1_attn_all.items() if k in ('Wq', 'Wk', 'Wv', 'Wg', 'Wo', 'gamma', 'beta')}
    del _L1_attn_all

    def _L1_xattn_setup():
        import jax, jax.numpy as jnp
        import numpy as np
        BS, S, DK = (8, 64, 256)
        key = jax.random.key(seed)
        kq, kk, kv = jax.random.split(key, 3)
        q = jax.random.normal(kq, (BS, S, DK), dtype=jnp.float32)
        k = jax.random.normal(kk, (BS, S, DK), dtype=jnp.float32)
        v = jax.random.normal(kv, (BS, S, DK), dtype=jnp.float32)
        return {'q': q, 'k': k, 'v': v}
    _L1_xattn_all = _L1_xattn_setup()
    _L1_xattn_in = {k: v for k, v in _L1_xattn_all.items() if k in ()}
    del _L1_xattn_all

    def _L1_ffn_setup():
        import jax, jax.numpy as jnp
        import numpy as np
        B, S, D, H = (4, 256, 256, 1024)

        def fwht(x):
            orig_shape = x.shape
            n = orig_shape[-1]
            x = x.reshape(-1, n)
            h = 1
            while h < n:
                xb = x.reshape(-1, n // (2 * h), 2, h)
                a = xb[:, :, 0, :]
                b = xb[:, :, 1, :]
                x = jnp.stack([a + b, a - b], axis=2).reshape(-1, n)
                h *= 2
            scale = jnp.asarray(1.0 / np.sqrt(n), dtype=x.dtype)
            return (x * scale).reshape(orig_shape)
        key = jax.random.key(seed)
        kx, k1, k2, k3 = jax.random.split(key, 4)
        x = jax.random.normal(kx, (B, S, D), dtype=jnp.float32)
        W1 = jax.random.normal(k1, (H, D), dtype=jnp.float32) * (1.0 / np.sqrt(D))
        W2 = jax.random.normal(k2, (D, H), dtype=jnp.float32) * (1.0 / np.sqrt(H))
        W3 = jax.random.normal(k3, (H, D), dtype=jnp.float32) * (1.0 / np.sqrt(D))
        return {'x': x, 'W1': W1, 'W2': W2, 'W3': W3}
    _L1_ffn_all = _L1_ffn_setup()
    _L1_ffn_in = {k: v for k, v in _L1_ffn_all.items() if k in ('W1', 'W2', 'W3')}
    del _L1_ffn_all
    return {'x': x, 'ctx_2048': ctx_2048, 'L0_attn_in_proj_w': _L0_attn_in['in_proj_w'], 'L0_attn_conv_w': _L0_attn_in['conv_w'], 'L0_attn_conv_b': _L0_attn_in['conv_b'], 'L0_attn_dt_bias': _L0_attn_in['dt_bias'], 'L0_attn_A_log': _L0_attn_in['A_log'], 'L0_attn_D': _L0_attn_in['D'], 'L0_attn_ssm_norm_w': _L0_attn_in['ssm_norm_w'], 'L0_attn_out_proj_w': _L0_attn_in['out_proj_w'], 'L0_attn_norm_mamba_w': _L0_attn_in['norm_mamba_w'], 'L0_attn_norm_moe_w': _L0_attn_in['norm_moe_w'], 'L0_attn_gate_w': _L0_attn_in['gate_w'], 'L0_attn_w1': _L0_attn_in['w1'], 'L0_attn_w2': _L0_attn_in['w2'], 'L0_attn_sp1_w': _L0_attn_in['sp1_w'], 'L0_attn_sp1_b': _L0_attn_in['sp1_b'], 'L0_attn_sp2_w': _L0_attn_in['sp2_w'], 'L0_attn_sp2_b': _L0_attn_in['sp2_b'], 'L0_attn_harm_w': _L0_attn_in['harm_w'], 'L0_attn_harm_b': _L0_attn_in['harm_b'], 'L0_attn_unc_w': _L0_attn_in['unc_w'], 'L0_attn_unc_b': _L0_attn_in['unc_b'], 'L0_attn_tox_w': _L0_attn_in['tox_w'], 'L0_attn_tox_b': _L0_attn_in['tox_b'], 'L0_xattn_time_decay': _L0_xattn_in['time_decay'], 'L0_xattn_time_first': _L0_xattn_in['time_first'], 'L0_ffn_router_w': _L0_ffn_in['router_w'], 'L0_ffn_w1': _L0_ffn_in['w1'], 'L0_ffn_b1': _L0_ffn_in['b1'], 'L0_ffn_w2': _L0_ffn_in['w2'], 'L0_ffn_b2': _L0_ffn_in['b2'], 'L1_attn_Wq': _L1_attn_in['Wq'], 'L1_attn_Wk': _L1_attn_in['Wk'], 'L1_attn_Wv': _L1_attn_in['Wv'], 'L1_attn_Wg': _L1_attn_in['Wg'], 'L1_attn_Wo': _L1_attn_in['Wo'], 'L1_attn_gamma': _L1_attn_in['gamma'], 'L1_attn_beta': _L1_attn_in['beta'], 'L1_ffn_W1': _L1_ffn_in['W1'], 'L1_ffn_W2': _L1_ffn_in['W2'], 'L1_ffn_W3': _L1_ffn_in['W3']}

def reference(x, ctx_2048, L0_attn_in_proj_w, L0_attn_conv_w, L0_attn_conv_b, L0_attn_dt_bias, L0_attn_A_log, L0_attn_D, L0_attn_ssm_norm_w, L0_attn_out_proj_w, L0_attn_norm_mamba_w, L0_attn_norm_moe_w, L0_attn_gate_w, L0_attn_w1, L0_attn_w2, L0_attn_sp1_w, L0_attn_sp1_b, L0_attn_sp2_w, L0_attn_sp2_b, L0_attn_harm_w, L0_attn_harm_b, L0_attn_unc_w, L0_attn_unc_b, L0_attn_tox_w, L0_attn_tox_b, L0_xattn_time_decay, L0_xattn_time_first, L0_ffn_router_w, L0_ffn_w1, L0_ffn_b1, L0_ffn_w2, L0_ffn_b2, L1_attn_Wq, L1_attn_Wk, L1_attn_Wv, L1_attn_Wg, L1_attn_Wo, L1_attn_gamma, L1_attn_beta, L1_ffn_W1, L1_ffn_W2, L1_ffn_W3):
    import jax
    import jax.numpy as jnp

    def _L0_attn_ref(x, in_proj_w, conv_w, conv_b, dt_bias, A_log, D, ssm_norm_w, out_proj_w, norm_mamba_w, norm_moe_w, gate_w, w1, w2, sp1_w, sp1_b, sp2_w, sp2_b, harm_w, harm_b, unc_w, unc_b, tox_w, tox_b):
        import jax, jax.numpy as jnp
        import numpy as np
        from jax import lax
        D_MODEL = 256
        D_STATE = 64
        D_CONV = 4
        EXPAND = 2
        HEADDIM = 64
        D_INNER = D_MODEL * EXPAND
        NHEADS = D_INNER // HEADDIM
        CONV_DIM = D_INNER + 2 * D_STATE
        D_IN_PROJ = 2 * D_INNER + 2 * D_STATE + NHEADS
        NUM_EXPERTS = 8
        TOP_K = 2
        D_FF = 4 * D_MODEL
        BATCH = 2
        SEQ = 64
        EPS = 1e-06

        def rmsnorm(x, w):
            return x * lax.rsqrt(jnp.mean(x * x, axis=-1, keepdims=True) + EPS) * w

        def silu(x):
            return x * jax.nn.sigmoid(x)

        def mamba2(x, in_proj_w, conv_w, conv_b, dt_bias, A_log, Dp, ssm_norm_w, out_proj_w):
            Bsz, L, _ = x.shape
            zxbcdt = x @ in_proj_w.T
            z, xBC, dt = jnp.split(zxbcdt, [D_INNER, D_INNER + CONV_DIM], axis=-1)
            xBC = lax.conv_general_dilated(xBC.transpose(0, 2, 1), conv_w[:, None, :], (1,), [(D_CONV - 1, 0)], feature_group_count=CONV_DIM)
            xBC = silu((xBC + conv_b[None, :, None]).transpose(0, 2, 1))
            xs, Bm, Cm = jnp.split(xBC, [D_INNER, D_INNER + D_STATE], axis=-1)
            dt = jax.nn.softplus(dt + dt_bias)
            A = -jnp.exp(A_log)
            xh = xs.reshape(Bsz, L, NHEADS, HEADDIM)

            def step(h, inp):
                dt_t, x_t, B_t, C_t = inp
                dA = jnp.exp(dt_t * A)
                h = h * dA[:, :, None, None] + dt_t[:, :, None, None] * x_t[..., None] * B_t[:, None, None, :]
                y = jnp.einsum('bhpn,bn->bhp', h, C_t)
                return (h, y)
            h0 = jnp.zeros((Bsz, NHEADS, HEADDIM, D_STATE), x.dtype)
            _, ys = lax.scan(step, h0, (dt.transpose(1, 0, 2), xh.transpose(1, 0, 2, 3), Bm.transpose(1, 0, 2), Cm.transpose(1, 0, 2)))
            y = ys.transpose(1, 0, 2, 3) + Dp[None, None, :, None] * xh
            y = y.reshape(Bsz, L, D_INNER)
            y = rmsnorm(y * silu(z), ssm_norm_w)
            return y @ out_proj_w.T

        def moe(x, gate_w, w1, w2):
            T = x.shape[0] * x.shape[1]
            xf = x.reshape(T, D_MODEL)
            logits = xf @ gate_w.T
            vals, idx = lax.top_k(logits, TOP_K)
            wts = jax.nn.softmax(vals, axis=-1)
            combine = jnp.sum(jax.nn.one_hot(idx, NUM_EXPERTS, dtype=x.dtype) * wts[..., None], axis=1)
            h = silu(jnp.einsum('td,efd->tef', xf, w1))
            eo = jnp.einsum('tef,edf->ted', h, w2)
            out = jnp.einsum('ted,te->td', eo, combine)
            probs = jax.nn.softmax(logits, axis=-1)
            lb = NUM_EXPERTS * jnp.sum(jnp.mean(probs, axis=0) ** 2)
            return (out.reshape(x.shape), lb)

        def safety(x, sp1_w, sp1_b, sp2_w, sp2_b, harm_w, harm_b, unc_w, unc_b, tox_w, tox_b):
            f = silu(x @ sp1_w.T + sp1_b) @ sp2_w.T + sp2_b
            harm = f @ harm_w.T + harm_b
            unc = jax.nn.sigmoid(f @ unc_w.T + unc_b)[..., 0]
            tox = jax.nn.sigmoid(f @ tox_w.T + tox_b)[..., 0]
            hs = jax.nn.sigmoid(harm)
            return (hs.max(-1), jnp.argmax(hs, -1), unc, tox, harm)

        def _reference_tuple_inner(x, in_proj_w, conv_w, conv_b, dt_bias, A_log, D, ssm_norm_w, out_proj_w, norm_mamba_w, norm_moe_w, gate_w, w1, w2, sp1_w, sp1_b, sp2_w, sp2_b, harm_w, harm_b, unc_w, unc_b, tox_w, tox_b):
            residual = x
            h = rmsnorm(x, norm_mamba_w)
            h = mamba2(h, in_proj_w, conv_w, conv_b, dt_bias, A_log, D, ssm_norm_w, out_proj_w) + residual
            x_moe, lb_loss = moe(rmsnorm(h, norm_moe_w), gate_w, w1, w2)
            h = h + x_moe
            risk_vals, risk_idx, unc, tox, harm = safety(h, sp1_w, sp1_b, sp2_w, sp2_b, harm_w, harm_b, unc_w, unc_b, tox_w, tox_b)
            return (h, risk_vals, risk_idx, unc, tox, harm, lb_loss)
        return _reference_tuple_inner(x, in_proj_w, conv_w, conv_b, dt_bias, A_log, D, ssm_norm_w, out_proj_w, norm_mamba_w, norm_moe_w, gate_w, w1, w2, sp1_w, sp1_b, sp2_w, sp2_b, harm_w, harm_b, unc_w, unc_b, tox_w, tox_b)[0]

    def _L0_xattn_ref(batch_size, seq_len, embedding_dim, time_decay, time_first, k, v):
        import jax, jax.numpy as jnp
        import numpy as np

        def _wkv(time_decay, time_first, k, v):
            w = -jnp.exp(time_decay)
            u = time_first
            B, T, C = k.shape
            aa = jnp.zeros((B, C), dtype=k.dtype)
            bb = jnp.zeros((B, C), dtype=k.dtype)
            pp = jnp.full((B, C), -1e+38, dtype=k.dtype)

            def step(carry, kv_t):
                aa, bb, pp = carry
                kt, vt = kv_t
                ww = u + kt
                q = jnp.maximum(pp, ww)
                e1 = jnp.exp(pp - q)
                e2 = jnp.exp(ww - q)
                y_t = (e1 * aa + e2 * vt) / (e1 * bb + e2)
                ww2 = pp + w
                q2 = jnp.maximum(ww2, kt)
                e1b = jnp.exp(ww2 - q2)
                e2b = jnp.exp(kt - q2)
                new_carry = (e1b * aa + e2b * vt, e1b * bb + e2b, q2)
                return (new_carry, y_t)
            ks = jnp.transpose(k, (1, 0, 2))
            vs = jnp.transpose(v, (1, 0, 2))
            _, ys = jax.lax.scan(step, (aa, bb, pp), (ks, vs))
            return jnp.transpose(ys, (1, 0, 2))
        assert seq_len <= 128
        return _wkv(time_decay, time_first, k, v)

    def _L0_ffn_ref(hidden_states, router_w, w1, b1, w2, b2):
        import jax, jax.numpy as jnp
        import numpy as np
        E = 8
        K = 2
        CAP = 64
        H = 256
        F = 1024
        orig_shape = hidden_states.shape
        x = hidden_states.reshape(-1, H)
        N = x.shape[0]
        logits = x @ router_w.T
        probs = jax.nn.softmax(logits, axis=-1)
        top_p, top_i = jax.lax.top_k(probs, K)
        expert_flat = top_i.T.reshape(-1)
        probs_flat = top_p.T.reshape(-1)
        token_idx = jnp.tile(jnp.arange(N), K)
        onehot = (expert_flat[:, None] == jnp.arange(E)[None, :]).astype(jnp.int32)
        pos = jnp.take_along_axis(jnp.cumsum(onehot, axis=0), expert_flat[:, None], axis=1)[:, 0] - 1
        keep = pos < CAP
        dest = expert_flat * CAP + pos
        dest_m = jnp.where(keep, dest, E * CAP)
        buf = jnp.zeros((E * CAP, H), x.dtype).at[dest_m].set(x[token_idx], mode='drop')
        h = jax.nn.gelu(buf @ w1.T + b1, approximate=False) @ w2.T + b2
        gathered = jnp.where(keep[:, None], h[jnp.where(keep, dest, 0)], 0.0) * probs_flat[:, None]
        out = jnp.zeros_like(x).at[token_idx].add(gathered)
        return out.reshape(orig_shape)

    def _L1_attn_ref(x, Wq, Wk, Wv, Wg, Wo, gamma, beta):
        import jax, jax.numpy as jnp
        import numpy as np
        B, L, D, H = (2, 512, 256, 16)
        K = D // H
        V = D // H
        EPS = 1e-05

        def _gla_recurrence(q, k, v, g):
            qs = jnp.moveaxis(q, 1, 0)
            ks = jnp.moveaxis(k, 1, 0)
            vs = jnp.moveaxis(v, 1, 0)
            gs = jnp.moveaxis(g, 1, 0)

            def step(S, inp):
                qt, kt, vt, gt = inp
                S = S * jnp.exp(gt)[..., None] + kt[..., None] * vt[..., None, :]
                yt = jnp.einsum('bhk,bhkv->bhv', qt, S)
                return (S, yt)
            S0 = jnp.zeros((q.shape[0], H, K, V), q.dtype)
            S_final, ys = jax.lax.scan(step, S0, (qs, ks, vs, gs))
            return (jnp.moveaxis(ys, 0, 1), S_final)

        def _layernorm(x, gamma, beta):
            mu = jnp.mean(x, axis=-1, keepdims=True)
            var = jnp.mean(jnp.square(x - mu), axis=-1, keepdims=True)
            return (x - mu) * jax.lax.rsqrt(var + EPS) * gamma + beta

        def _reference_tuple_inner(x, Wq, Wk, Wv, Wg, Wo, gamma, beta):
            b, l, d = x.shape
            q = (x @ Wq.T).reshape(b, l, H, K) * K ** (-0.5)
            k = (x @ Wk.T).reshape(b, l, H, K)
            v = (x @ Wv.T).reshape(b, l, H, V)
            g = jax.nn.log_sigmoid(x @ Wg.T).reshape(b, l, H, K)
            y, final_state = _gla_recurrence(q, k, v, g)
            y = y.reshape(b, l, d)
            o = _layernorm(y, gamma, beta) @ Wo.T
            return (o, final_state)
        return _reference_tuple_inner(x, Wq, Wk, Wv, Wg, Wo, gamma, beta)[0]

    def _L1_xattn_ref(q, k, v):
        import jax, jax.numpy as jnp
        import numpy as np
        BS, S, DK = (8, 64, 256)
        dk = q.shape[-1]
        scale = 1.0 / jnp.sqrt(jnp.asarray(dk, dtype=q.dtype))
        scaled = jnp.einsum('bsd,bse->bde', q, k) * scale
        attn = jax.nn.softmax(scaled, axis=1)
        out = jnp.einsum('bde,bse->bsd', attn, v)
        return out

    def _L1_ffn_ref(x, W1, W2, W3):
        import jax, jax.numpy as jnp
        import numpy as np
        B, S, D, H = (4, 256, 256, 1024)

        def fwht(x):
            orig_shape = x.shape
            n = orig_shape[-1]
            x = x.reshape(-1, n)
            h = 1
            while h < n:
                xb = x.reshape(-1, n // (2 * h), 2, h)
                a = xb[:, :, 0, :]
                b = xb[:, :, 1, :]
                x = jnp.stack([a + b, a - b], axis=2).reshape(-1, n)
                h *= 2
            scale = jnp.asarray(1.0 / np.sqrt(n), dtype=x.dtype)
            return (x * scale).reshape(orig_shape)
        up_gate = jnp.einsum('bsd,hd->bsh', x, W1)
        up_lin = jnp.einsum('bsd,hd->bsh', x, W3)
        hidden = jax.nn.silu(up_gate) * up_lin
        hidden = fwht(hidden)
        out = jnp.einsum('bsh,dh->bsd', hidden, W2)
        return out
    x = x + _L0_attn_ref(_layernorm(x, axis=-1), L0_attn_in_proj_w, L0_attn_conv_w, L0_attn_conv_b, L0_attn_dt_bias, L0_attn_A_log, L0_attn_D, L0_attn_ssm_norm_w, L0_attn_out_proj_w, L0_attn_norm_mamba_w, L0_attn_norm_moe_w, L0_attn_gate_w, L0_attn_w1, L0_attn_w2, L0_attn_sp1_w, L0_attn_sp1_b, L0_attn_sp2_w, L0_attn_sp2_b, L0_attn_harm_w, L0_attn_harm_b, L0_attn_unc_w, L0_attn_unc_b, L0_attn_tox_w, L0_attn_tox_b)
    x = x + _L0_xattn_ref(16, 128, 256, L0_xattn_time_decay, L0_xattn_time_first, _layernorm(x, axis=-1), ctx_2048)
    x = x + _L0_ffn_ref(_layernorm(x, axis=-1), L0_ffn_router_w, L0_ffn_w1, L0_ffn_b1, L0_ffn_w2, L0_ffn_b2)
    x = x + _L1_attn_ref(_layernorm(x, axis=-1), L1_attn_Wq, L1_attn_Wk, L1_attn_Wv, L1_attn_Wg, L1_attn_Wo, L1_attn_gamma, L1_attn_beta)
    x = x + _L1_xattn_ref(_layernorm(x, axis=-1), ctx_2048, ctx_2048)
    x = x + _L1_ffn_ref(_layernorm(x, axis=-1), L1_ffn_W1, L1_ffn_W2, L1_ffn_W3)
    return x

_drawn_inputs = setup_inputs


def setup_inputs(seed=0):
    import zlib

    import numpy as np

    out = dict(_drawn_inputs(seed))
    spreads = {'L0_attn_D': (1.0, 0.6),
     'L0_attn_ssm_norm_w': (1.0, 0.2),
     'L0_attn_norm_mamba_w': (1.0, 0.2),
     'L0_attn_norm_moe_w': (1.0, 0.6),
     'L0_attn_sp1_b': (0.0, 0.1),
     'L0_attn_sp2_b': (0.0, 0.1),
     'L0_attn_harm_b': (0.0, 0.1),
     'L1_attn_gamma': (1.0, 0.2),
     'L1_attn_beta': (0.0, 0.1)}
    factors = {'L0_attn_dt_bias': 200.0,
     'L0_attn_A_log': 64.0,
     'L0_ffn_router_w': 8.0,
     'L0_ffn_w1': 2.845,
     'L0_ffn_b1': 175.136,
     'L0_ffn_b2': 64.0}
    for name, (base, spread) in spreads.items():
        noise = np.random.default_rng([zlib.crc32(name.encode()), seed]).standard_normal(out[name].shape)
        drawn = base * np.exp(spread * noise) if base else spread * noise
        out[name] = jnp.asarray(drawn.astype(out[name].dtype))
    for name, factor in factors.items():
        out[name] = (out[name] * factor).astype(out[name].dtype)
    return out
```

```python
from contextlib import ExitStack

import numpy as np

import concourse.bass as bass
from concourse import mybir

F32 = mybir.dt.float32
U32 = mybir.dt.uint32
ALU = mybir.AluOpType
ACT = mybir.ActivationFunctionType
AX = mybir.AxisListType

P = 128
SEQS, D = 16, 256
KD = D // P
GROUP = 4
GROUPS = SEQS // GROUP
GT = GROUP * P
DI, HEADS, HD, NS = 512, 8, 64, 64
CI = DI // P
TAPS = 4
PAD = TAPS - 1
EXPERTS, FF = 8, 1024
KF = FF // P
CAP = 64
LN_EPS, RMS_EPS = 1e-5, 1e-6


def merge_stats(v, link, stats, mean_var, halves):
    link(v.tensor_tensor(halves[:, 0], stats[:, :, 1], stats[:, :, 4], ALU.add))
    link(v.tensor_tensor(halves[:, 1], stats[:, :, 1], stats[:, :, 4], ALU.subtract))
    link(v.tensor_tensor(halves[:, 2], stats[:, :, 2], stats[:, :, 5], ALU.add))
    link(v.tensor_scalar(mean_var[:, :, 0], halves[:, 0], 0.5, None, ALU.mult))
    link(v.scalar_tensor_tensor(out=halves[:, 3], in0=halves[:, 1], scalar=0.25, in1=halves[:, 1],
                                op0=ALU.mult, op1=ALU.mult))
    link(v.scalar_tensor_tensor(out=mean_var[:, :, 1], in0=halves[:, 2], scalar=1.0 / D, in1=halves[:, 3],
                                op0=ALU.mult, op1=ALU.add))


class Shared:
    pass


class Links:

    def __init__(self, eng, sem, base=0):
        self.eng, self.sem, self.base, self.n = eng, sem, base, 0

    def __call__(self, ins):
        ins.then_inc(self.sem, 1)
        self.n += 1
        self.eng.wait_ge(self.sem, self.base + self.n)


def bc(ap, shape):
    return ap.broadcast_to(shape)


def log1p_terms(n):
    return [1.0 / (2 * k + 1) for k in range(n, 0, -1)]


def mamba_phase(nc, g):
    SS_COL = D
    VEC_STEPS = g.vec_steps_mamba
    with ExitStack() as ctx:
        def sb(name, *shape):
            return ctx.enter_context(nc.sbuf_tensor(name, list(shape), F32))

        def ps(name, *shape):
            return ctx.enter_context(nc.psum_tensor(name, list(shape), F32))

        sem = g.sem
        win = sb("win", P, KD, 2 * DI + 2 * NS + HEADS)
        wout = sb("wout", P, CI, D)
        norm_w = sb("norm_w", P, KD)
        moe_w = sb("moe_w", P, KD)
        ssm_w = sb("ssm_w", P, CI)
        conv_w = sb("conv_w", P, CI, TAPS)
        conv_b = sb("conv_b", P, CI)
        convbc_w = sb("convbc_w", NS, 2, TAPS)
        convbc_b = sb("convbc_b", NS, 2)
        dt_bias = sb("dt_bias", P, HEADS)
        a_neg = sb("a_neg", P, HEADS)
        d_skip = sb("d_skip", P, CI)
        stats = sb("stats", P, GROUP, 6)
        mean_var = sb("mean_var", P, GROUP, 2)
        halves = sb("halves", P, 4, GROUP)
        small = sb("small", P, 8, GROUP)
        u_tok = sb("u_tok", P, GROUP, D)
        h_tok = sb("h_tok", P, GROUP, D)
        h_feat = sb("h_feat", P, KD, GT)
        dtw = sb("dtw", P, 6, GROUP * HEADS)
        dt = sb("dt", P, GROUP * HEADS)
        da = sb("da", P, GROUP * HEADS)
        xpad = sb("xpad", P, CI, GROUP, PAD + P)
        bcpad = sb("bcpad", NS, 2, GROUP, PAD + P)
        conv = sb("conv", P, 2, GROUP, P)
        tanh = sb("tanh", P, 2, GT)
        xs_feat = sb("xs_feat", P, CI, GT)
        bc_feat = sb("bc_feat", NS, 2, GT)
        gate = sb("gate", P, CI, GT)
        gate_t = sb("gate_t", P, 2, GT)
        gm = sb("gm", P, 2, P)
        xdt = sb("xdt", P, 2, DI)
        steps_da = sb("steps_da", P, HEADS, P)
        decay = sb("decay", P, 2, HEADS, P)
        mix = sb("mix", P, 2, HEADS, P)
        y_feat = sb("y_feat", P, CI, P)
        yg = sb("yg", P, 2, CI, P)
        yg2 = sb("yg2", P, 2, CI, P)
        hm = sb("hm", P, 2, D)
        hm_sq = sb("hm_sq", P, D)
        xm_tok = sb("xm_tok", P, 2, D)
        sc = sb("sc", P, 2, 4)

        bank_t = [ps(f"bank_t{k}", P, GT) for k in range(KD)]
        bank_p = [ps(f"bank_p{k}", P, GT) for k in range(2)]
        bank_d = ps("bank_d", P, HEADS, P)
        bank_dt = ps("bank_dt", P, GROUP * HEADS)
        bank_y = ps("bank_y", P, CI, P)

        loaded, consts = sem("m_loaded"), sem("m_consts")
        vec, pool_done = sem("m_vec"), sem("m_pool")
        var_ready, rstd_ready = sem("m_var_ready"), sem("m_rstd_ready")
        u_ready, h_ready = sem("m_u_ready"), sem("m_h_ready")
        hT_ps, hT_ready = sem("m_hT_ps"), sem("m_hT_ready")
        dt_ps, dt_abs, dt_exp, dt_ready = sem("m_dt_ps"), sem("m_dt_abs"), sem("m_dt_exp"), sem("m_dt_ready")
        proj_ps, proj_used_a, proj_used_v = sem("m_proj_ps"), sem("m_proj_used_a"), sem("m_proj_used_v")
        pad_ready, conv_ready, ctanh_ready, feat_ready = (
            sem("m_pad_ready"), sem("m_conv_ready"), sem("m_ctanh_ready"), sem("m_feat_ready"))
        ztanh_ready, gate_ready = sem("m_ztanh_ready"), sem("m_gate_ready")
        g_ps, gm_ready = sem("m_g_ps"), sem("m_gm_ready")
        xsT_ps, xdt_ready = sem("m_xsT_ps"), sem("m_xdt_ready")
        steps_ready, d_ps, decay_ready, mix_ready = (
            sem("m_steps_ready"), sem("m_d_ps"), sem("m_decay_ready"), sem("m_mix_ready"))
        y_ps, yg_ready, yg2_ready, out_ps = sem("m_y_ps"), sem("m_yg_ready"), sem("m_yg2_ready"), sem("m_out_ps")
        ms_ready, r_ready, hm_ready, hms_ready = (
            sem("m_ms_ready"), sem("m_r_ready"), sem("m_hm_ready"), sem("m_hms_ready"))
        xm_ready, xmT_ps, xmT_used, x_added = (
            sem("m_xm_ready"), sem("m_xmT_ps"), sem("m_xmT_used"), sem("m_x_added"))

        NPROJ = 2 + CI + CI

        def slots(a, b, c, d):
            for s in range(GROUP + 3):
                for stage, late in ((a, 0), (b, 1), (c, 2), (d, 3)):
                    if 0 <= s - late < GROUP:
                        stage(s - late)

        block = ctx.enter_context(nc.Block())

        @block.sync
        def _(sp):
            def load(dst, src):
                sp.dma_start(dst, src).then_inc(loaded, 16)
            for n in range(GROUPS):
                q = slice(GROUP * n, GROUP * n + GROUP)
                sp.dma_start(g.X[:, q, :], g.dram["x"].rearrange("b t d -> t b d")[:, q, :]).then_inc(g.x_loaded, 16)
            load(norm_w[:], g.dram["norm_mamba_w"])
            load(win[:], g.dram["in_proj_w"])
            load(conv_w[:], g.dram["conv_w_inner"])
            load(conv_b[:], g.dram["conv_b_inner"])
            load(convbc_w[:], g.dram["conv_w_bc"])
            load(convbc_b[:], g.dram["conv_b_bc"])
            load(dt_bias[:], g.dram["dt_bias"].partition_broadcast(P))
            load(a_neg[:], g.dram["A_log"].partition_broadcast(P))
            for h in range(2):
                load(d_skip[HD * h:HD * h + HD, :], g.dram["D"][h].partition_broadcast(HD))
            load(wout[:], g.dram["out_proj_w"])
            load(ssm_w[:], g.dram["ssm_norm_w"])
            load(moe_w[:], g.dram["norm_moe_w"])
        LOADS = 16 * 13

        @block.gpsimd
        def _(pool):
            nc.gpsimd.memset(g.ident[:], 0.0).then_inc(pool_done, 1)
            nc.gpsimd.memset(g.upto[:], 1.0).then_inc(pool_done, 1)
            nc.gpsimd.memset(g.after[:], 1.0).then_inc(pool_done, 1)
            nc.gpsimd.memset(g.ones[:], 1.0).then_inc(consts, 1)
            nc.gpsimd.memset(g.neg_half[:], -0.5).then_inc(consts, 1)
            for e in range(EXPERTS):
                nc.gpsimd.memset(g.iota8[:, e:e + 1], float(e))
            nc.gpsimd.memset(xpad[:], 0.0).then_inc(consts, 1)
            nc.gpsimd.memset(bcpad[:], 0.0).then_inc(consts, 1)
            pool.wait_ge(pool_done, 3)
            nc.gpsimd.affine_select(out=g.ident[:], in_=g.ident[:], compare_op=ALU.not_equal, fill=1.0,
                                    base=0, pattern=[[-1, P]], channel_multiplier=1).then_inc(consts, 1)
            nc.gpsimd.affine_select(out=g.upto[:], in_=g.upto[:], compare_op=ALU.is_ge, fill=0.0,
                                    base=0, pattern=[[1, P]], channel_multiplier=-1).then_inc(consts, 1)
            nc.gpsimd.affine_select(out=g.after[:], in_=g.after[:], compare_op=ALU.is_gt, fill=0.0,
                                    base=0, pattern=[[-1, P]], channel_multiplier=1).then_inc(consts, 1)
            pool.wait_ge(consts, 7)
            with pool.Fori(0, GROUPS) as i:
                for n in range(2):
                    pool.wait_ge(var_ready, i * 2 + (n + 1))
                    nc.gpsimd.tensor_tensor(small[:, 2 * n + 1, :], small[:, 2 * n, :], g.neg_half[:, 0:GROUP],
                                            ALU.pow).then_inc(rstd_ready, 1)
                pool.wait_ge(dt_ready, i + 1)

                def a(j):
                    if j:
                        pool.wait_ge(d_ps, i * GROUP + j)
                    nc.gpsimd.tensor_tensor(
                        steps_da[:], bc(da[:, HEADS * j:HEADS * j + HEADS].unsqueeze(2), [P, HEADS, P]),
                        bc(g.upto[:].unsqueeze(1), [P, HEADS, P]), ALU.mult).then_inc(steps_ready, 1)

                def none(j):
                    pass

                def d(j):
                    pool.wait_ge(ms_ready, i * 2 * GROUP + (2 * j + 1))
                    nc.gpsimd.tensor_tensor(sc[:, j % 2, 1:2], sc[:, j % 2, 0:1], g.neg_half[:, 0:1],
                                            ALU.pow).then_inc(r_ready, 1)
                    pool.wait_ge(hm_ready, i * GROUP + (j + 1))
                    nc.gpsimd.tensor_tensor(g.X[:, i * GROUP + j, :], g.X[:, i * GROUP + j, :], hm[:, j % 2, :],
                                            ALU.add).then_inc(x_added, 1)
                    pool.wait_ge(ms_ready, i * 2 * GROUP + (2 * j + 2))
                    nc.gpsimd.tensor_tensor(sc[:, j % 2, 3:4], sc[:, j % 2, 2:3], g.neg_half[:, 0:1],
                                            ALU.pow).then_inc(r_ready, 1)
                slots(a, none, none, d)

        @block.tensor
        def _(pe):
            pe.wait_ge(consts, 7)
            pe.wait_ge(loaded, LOADS)
            pe.wait_ge(vec, 3)
            with pe.Fori(0, GROUPS) as i:
                for j in range(GROUP):
                    pe.wait_ge(h_ready, i * GROUP + (j + 1))
                    for k in range(KD):
                        last = nc.tensor.transpose(bank_t[k][:, P * j:P * j + P], h_tok[:, j, P * k:P * k + P],
                                                   g.ident[:])
                last.then_inc(hT_ps, 1)
                pe.wait_ge(hT_ready, i * KD + KD)
                for j in range(GROUP):
                    for k in range(KD):
                        last = nc.tensor.matmul(bank_dt[:, HEADS * j:HEADS * j + HEADS],
                                                h_feat[:, k, P * j:P * j + P], win[:, k, 2 * DI + 2 * NS:],
                                                start=(k == 0), stop=(k == KD - 1))
                last.then_inc(dt_ps, 1)
                for n in range(NPROJ):
                    if n >= 2:
                        if n - 2 < 2 + CI:
                            pe.wait_ge(proj_used_a, i * (2 + CI) + (n - 1))
                        else:
                            pe.wait_ge(proj_used_v, i * CI + (n - 2 - (2 + CI) + 1))
                    if n < 2:
                        cols = slice(2 * DI + NS * n, 2 * DI + NS * n + NS)
                    elif n < 2 + CI:
                        cols = slice(DI + P * (n - 2), DI + P * (n - 2) + P)
                    else:
                        cols = slice(P * (n - 2 - CI), P * (n - 2 - CI) + P)
                    out = bank_p[n % 2][0:NS, :] if n < 2 else bank_p[n % 2][:]
                    for k in range(KD):
                        last = nc.tensor.matmul(out, win[:, k, cols], h_feat[:, k, :], start=(k == 0),
                                                stop=(k == KD - 1))
                    last.then_inc(proj_ps, 1)

                def a(j):
                    if j == 0:
                        pe.wait_ge(feat_ready, i * (2 + CI) + 2)
                        pe.wait_ge(proj_used_v, i * CI + CI)
                        pe.wait_ge(dt_ready, i + 1)
                    else:
                        pe.wait_ge(gm_ready, i * GROUP + j)
                    tok = slice(P * j, P * j + P)
                    nc.tensor.matmul(bank_p[0][:, 0:P], bc_feat[:, 0, tok], bc_feat[:, 1, tok],
                                     start=True, stop=True).then_inc(g_ps, 1)
                    if j == 0:
                        pe.wait_ge(feat_ready, i * (2 + CI) + 2 + CI)
                    else:
                        pe.wait_ge(xdt_ready, i * GROUP + j)
                    for c in range(CI):
                        last = nc.tensor.transpose(bank_t[0][:, P * c:P * c + P], xs_feat[:, c, tok], g.ident[:])
                    last.then_inc(xsT_ps, 1)
                    pe.wait_ge(steps_ready, i * GROUP + (j + 1))
                    if j:
                        pe.wait_ge(decay_ready, i * GROUP + j)
                    for n in range(2):
                        hs = slice(HEADS // 2 * n, HEADS // 2 * (n + 1))
                        last = nc.tensor.matmul(bank_d[:, hs, :], g.after[:], steps_da[:, hs, :], start=True, stop=True)
                    last.then_inc(d_ps, 1)

                def b(j):
                    pe.wait_ge(mix_ready, i * GROUP + (j + 1))
                    pe.wait_ge(xdt_ready, i * GROUP + (j + 1))
                    if j:
                        pe.wait_ge(yg_ready, i * GROUP + j)
                    for h in range(HEADS):
                        last = nc.tensor.matmul(bank_y[HD * (h % 2):HD * (h % 2) + HD, h // 2, :],
                                                xdt[:, j % 2, HD * h:HD * h + HD], mix[:, j % 2, h, :],
                                                start=True, stop=True)
                    last.then_inc(y_ps, 1)

                def c(j):
                    pe.wait_ge(yg2_ready, i * GROUP + (j + 1))
                    if j:
                        pe.wait_ge(hm_ready, i * GROUP + j)
                    for c in range(CI):
                        nc.tensor.matmul(bank_t[1][:, SS_COL:SS_COL + 1], yg2[:, j % 2, c, :], g.ones[:, 0:1],
                                         start=(c == 0), stop=(c == CI - 1))
                    for c in range(CI):
                        last = nc.tensor.matmul(bank_t[1][:, 0:D], yg[:, j % 2, c, :], wout[:, c, :],
                                                start=(c == 0), stop=(c == CI - 1))
                    last.then_inc(out_ps, 1)

                def d(j):
                    pe.wait_ge(xm_ready, i * GROUP + (j + 1))
                    if j:
                        pe.wait_ge(xmT_used, i * GROUP + j)
                    for k in range(KD):
                        last = nc.tensor.transpose(bank_p[1][:, P * k:P * k + P],
                                                   xm_tok[:, j % 2, P * k:P * k + P], g.ident[:])
                    last.then_inc(xmT_ps, 1)
                slots(a, b, c, d)
                pe.wait_ge(xmT_used, i * GROUP + GROUP)

        @block.scalar
        def _(act):
            act.wait_ge(loaded, LOADS)
            act.wait_ge(vec, 1)
            nc.scalar.activation(a_neg[:], a_neg[:], ACT.Exp).then_inc(g.a_exp, 1)
            with act.Fori(0, GROUPS) as i:
                act.wait_ge(rstd_ready, i * 2 + 2)
                for j in range(GROUP):
                    act.wait_ge(u_ready, i * GROUP + (j + 1))
                    nc.scalar.activation(h_tok[:, j, :], u_tok[:, j, :], ACT.Copy,
                                         scale=small[:, 3, j:j + 1]).then_inc(h_ready, 1)
                act.wait_ge(hT_ps, i + 1)
                for k in range(KD):
                    nc.scalar.activation(h_feat[:, k, :], bank_t[k][:], ACT.Copy,
                                         scale=norm_w[:, k:k + 1]).then_inc(hT_ready, 1)
                act.wait_ge(dt_abs, i + 1)
                nc.scalar.activation(dtw[:, 2, :], dtw[:, 1, :], ACT.Exp, scale=-1.0).then_inc(dt_exp, 1)

                def conv_tanh(n):
                    act.wait_ge(conv_ready, i * (2 + CI) + (n + 1))
                    rows = NS if n < 2 else P
                    nc.scalar.activation(tanh[0:rows, n % 2, :], conv[0:rows, n % 2, :, :].rearrange("p a b -> p (a b)"),
                                         ACT.Tanh, scale=0.5).then_inc(ctanh_ready, 1)
                for n in range(2 + CI):
                    act.wait_ge(proj_ps, i * NPROJ + (n + 1))
                    dst = bcpad[:, n, :, PAD:] if n < 2 else xpad[:, n - 2, :, PAD:]
                    src = bank_p[n % 2][0:NS, :] if n < 2 else bank_p[n % 2][:]
                    nc.scalar.activation(dst, src.rearrange("p (a b) -> p a b", a=GROUP), ACT.Copy)\
                        .then_inc(proj_used_a, 1)
                    if n >= 1:
                        conv_tanh(n - 1)
                for c in range(CI):
                    n = 2 + CI + c
                    act.wait_ge(proj_ps, i * NPROJ + (n + 1))
                    nc.scalar.activation(gate_t[:, c % 2, :], bank_p[n % 2][:], ACT.Tanh, scale=0.5)\
                        .then_inc(ztanh_ready, 1)
                    if c == 0:
                        conv_tanh(1 + CI)

                def a(j):
                    act.wait_ge(d_ps, i * GROUP + (j + 1))
                    nc.scalar.activation(decay[:, j % 2, :, :], bank_d[:], ACT.Exp).then_inc(decay_ready, 1)

                def none(j):
                    pass

                def c(j):
                    act.wait_ge(yg_ready, i * GROUP + (j + 1))
                    nc.scalar.activation(yg2[:, j % 2, :, :], yg[:, j % 2, :, :], ACT.Square).then_inc(yg2_ready, 1)

                def d(j):
                    act.wait_ge(hm_ready, i * GROUP + (j + 1))
                    nc.scalar.activation(hm_sq[:], hm[:, j % 2, :], ACT.Square,
                                         accum_out=sc[:, j % 2, 2:3]).then_inc(hms_ready, 1)
                    act.wait_ge(xmT_ps, i * GROUP + (j + 1))
                    for k in range(KD):
                        last = nc.scalar.activation(g.xm_feat[:, k, bass.ds(i * GT + P * j, P)],
                                                    bank_p[1][:, P * k:P * k + P], ACT.Copy,
                                                    scale=moe_w[:, k:k + 1])
                    last.then_inc(xmT_used, 1)
                slots(a, none, c, d)

        @block.vector
        def _(dve):
            v = nc.vector
            dve.wait_ge(loaded, LOADS)
            v.tensor_scalar(a_neg[:], a_neg[:], 80.0, None, ALU.min).then_inc(vec, 1)
            dve.wait_ge(g.a_exp, 1)
            v.tensor_scalar(a_neg[:], a_neg[:], -1.0, None, ALU.mult).then_inc(vec, 1)
            v.tensor_tensor(wout[:], wout[:], bc(ssm_w[:].unsqueeze(2), [P, CI, D]), ALU.mult).then_inc(vec, 1)
            dve.wait_ge(vec, 3)
            dve.wait_ge(consts, 7)
            with dve.Fori(0, GROUPS) as i:
                link = Links(dve, vec, i * VEC_STEPS + 3)
                dve.wait_ge(g.x_loaded, i * 16 + 16)
                for j in range(GROUP):
                    ins = v.bn_stats(stats[:, j, :], g.X[:, i * GROUP + j, :])
                link(ins)
                merge_stats(v, link, stats[:], mean_var, halves)
                v.tensor_scalar(small[:, 0, :], mean_var[:, :, 1], LN_EPS, None, ALU.add).then_inc(var_ready, 1)
                dve.wait_ge(rstd_ready, i * 2 + 1)
                link(v.tensor_tensor(small[:, 4, :], mean_var[:, :, 1], small[:, 1, :], ALU.mult))
                link(v.tensor_tensor(small[:, 5, :], small[:, 4, :], small[:, 1, :], ALU.mult))
                v.tensor_scalar(small[:, 2, :], small[:, 5, :], RMS_EPS, None, ALU.add).then_inc(var_ready, 1)
                for j in range(GROUP):
                    v.tensor_scalar(u_tok[:, j, :], g.X[:, i * GROUP + j, :], mean_var[:, j, 0:1],
                                    small[:, 1, j:j + 1], ALU.subtract, ALU.mult).then_inc(u_ready, 1)
                dve.wait_ge(dt_ps, i + 1)
                link(v.tensor_tensor(dtw[:, 0, :].rearrange("p (j h) -> p j h", j=GROUP),
                                     bank_dt[:].rearrange("p (j h) -> p j h", j=GROUP),
                                     bc(dt_bias[:].unsqueeze(1), [P, GROUP, HEADS]), ALU.add))
                v.scalar_tensor_tensor(out=dtw[:, 1, :], in0=dtw[:, 0, :], scalar=-1.0, in1=dtw[:, 0, :],
                                       op0=ALU.mult, op1=ALU.max).then_inc(dt_abs, 1)
                dve.wait_ge(dt_exp, i + 1)
                link(v.tensor_scalar(dtw[:, 3, :], dtw[:, 2, :], 2.0, None, ALU.add))
                link(v.reciprocal(dtw[:, 4, :], dtw[:, 3, :]))
                link(v.tensor_tensor(dtw[:, 3, :], dtw[:, 2, :], dtw[:, 4, :], ALU.mult))
                link(v.tensor_tensor(dtw[:, 4, :], dtw[:, 3, :], dtw[:, 3, :], ALU.mult))
                terms = log1p_terms(8)
                link(v.tensor_scalar(dtw[:, 5, :], dtw[:, 4, :], terms[0], None, ALU.mult))
                for c in terms[1:]:
                    link(v.scalar_tensor_tensor(out=dtw[:, 5, :], in0=dtw[:, 5, :], scalar=c, in1=dtw[:, 4, :],
                                                op0=ALU.add, op1=ALU.mult))
                link(v.scalar_tensor_tensor(out=dtw[:, 5, :], in0=dtw[:, 5, :], scalar=1.0, in1=dtw[:, 3, :],
                                            op0=ALU.add, op1=ALU.mult))
                link(v.tensor_scalar(dtw[:, 3, :], dtw[:, 0, :], 0.0, 0.5, ALU.max, ALU.mult))
                link(v.tensor_tensor(dtw[:, 4, :], dtw[:, 3, :], dtw[:, 5, :], ALU.add))
                link(v.tensor_scalar(dt[:], dtw[:, 4, :], 2.0, None, ALU.mult))
                link(v.tensor_tensor(dtw[:, 3, :].rearrange("p (j h) -> p j h", j=GROUP),
                                     dt[:].rearrange("p (j h) -> p j h", j=GROUP),
                                     bc(a_neg[:].unsqueeze(1), [P, GROUP, HEADS]), ALU.mult))
                v.tensor_scalar(da[:], dtw[:, 3, :], -1e30, None, ALU.max).then_inc(dt_ready, 1)

                def taps(n):
                    dve.wait_ge(proj_used_a, i * (2 + CI) + (n + 1))
                    if n < 2:
                        src, w, b, out = bcpad[:, n], convbc_w[:, n], convbc_b[:, n:n + 1], conv[0:NS, n % 2]
                    else:
                        src, w, b, out = xpad[:, n - 2], conv_w[:, n - 2], conv_b[:, n - 2:n - 1], conv[:, n % 2]
                    link(v.tensor_scalar(out, src[:, :, 0:P], w[:, 0:1], b, ALU.mult, ALU.add))
                    for k in range(1, TAPS):
                        ins = v.scalar_tensor_tensor(out=out, in0=src[:, :, k:k + P], scalar=w[:, k:k + 1], in1=out,
                                                     op0=ALU.mult, op1=ALU.add)
                        if k < TAPS - 1:
                            link(ins)
                        else:
                            ins.then_inc(conv_ready, 1)

                def silu(n):
                    dve.wait_ge(ctanh_ready, i * (2 + CI) + (n + 1))
                    rows = NS if n < 2 else P
                    out = bc_feat[:, n, :] if n < 2 else xs_feat[:, n - 2, :]
                    link(v.scalar_tensor_tensor(out=tanh[0:rows, n % 2, :], in0=tanh[0:rows, n % 2, :], scalar=1.0,
                                                in1=conv[0:rows, n % 2, :, :].rearrange("p a b -> p (a b)"),
                                                op0=ALU.add, op1=ALU.mult))
                    v.tensor_scalar(out, tanh[0:rows, n % 2, :], 0.5, None, ALU.mult).then_inc(feat_ready, 1)
                for n in range(2 + CI):
                    taps(n)
                    if n >= 1:
                        silu(n - 1)
                for c in range(CI):
                    n = 2 + CI + c
                    dve.wait_ge(ztanh_ready, i * CI + (c + 1))
                    v.scalar_tensor_tensor(out=gate[:, c, :], in0=gate_t[:, c % 2, :], scalar=1.0,
                                           in1=bank_p[n % 2][:], op0=ALU.add, op1=ALU.mult).then_inc(proj_used_v, 1)
                    if c == 0:
                        silu(1 + CI)

                def a(j):
                    dve.wait_ge(g_ps, i * GROUP + (j + 1))
                    v.tensor_tensor(gm[:, j % 2, :], bank_p[0][:, 0:P], g.upto[:], ALU.mult)\
                        .then_inc(gm_ready, 1)
                    dve.wait_ge(xsT_ps, i * GROUP + (j + 1))
                    v.tensor_tensor(xdt[:, j % 2, :].rearrange("p (h d) -> p h d", h=HEADS),
                                    bank_t[0][:].rearrange("p (h d) -> p h d", h=HEADS),
                                    bc(dt[:, HEADS * j:HEADS * j + HEADS].unsqueeze(2), [P, HEADS, HD]), ALU.mult)\
                        .then_inc(xdt_ready, 1)

                def b(j):
                    dve.wait_ge(gm_ready, i * GROUP + (j + 1))
                    dve.wait_ge(decay_ready, i * GROUP + (j + 1))
                    v.tensor_tensor(mix[:, j % 2, :, :], decay[:, j % 2, :, :],
                                    bc(gm[:, j % 2, :].unsqueeze(1), [P, HEADS, P]), ALU.mult).then_inc(mix_ready, 1)

                def c(j):
                    tok = slice(P * j, P * j + P)
                    dve.wait_ge(y_ps, i * GROUP + (j + 1))
                    for c in range(CI):
                        ins = v.scalar_tensor_tensor(out=y_feat[:, c, :], in0=xs_feat[:, c, tok],
                                                     scalar=d_skip[:, c:c + 1], in1=bank_y[:, c, :],
                                                     op0=ALU.mult, op1=ALU.add)
                    link(ins)
                    v.scalar_tensor_tensor(out=yg[:, j % 2, :, :], in0=y_feat[:], scalar=0.5, in1=gate[:, :, tok],
                                           op0=ALU.mult, op1=ALU.mult).then_inc(yg_ready, 1)

                def d(j):
                    dve.wait_ge(out_ps, i * GROUP + (j + 1))
                    v.tensor_scalar(sc[:, j % 2, 0:1], bank_t[1][:, SS_COL:SS_COL + 1], 1.0 / DI, RMS_EPS,
                                    ALU.mult, ALU.add).then_inc(ms_ready, 1)
                    dve.wait_ge(r_ready, i * 2 * GROUP + (2 * j + 1))
                    v.scalar_tensor_tensor(out=hm[:, j % 2, :], in0=bank_t[1][:, 0:D], scalar=sc[:, j % 2, 1:2],
                                           in1=u_tok[:, j, :], op0=ALU.mult, op1=ALU.add).then_inc(hm_ready, 1)
                    dve.wait_ge(hms_ready, i * GROUP + (j + 1))
                    v.tensor_scalar(sc[:, j % 2, 2:3], sc[:, j % 2, 2:3], 1.0 / D, RMS_EPS, ALU.mult, ALU.add)\
                        .then_inc(ms_ready, 1)
                    dve.wait_ge(r_ready, i * 2 * GROUP + (2 * j + 2))
                    v.tensor_scalar(xm_tok[:, j % 2, :], hm[:, j % 2, :], sc[:, j % 2, 3:4], None, ALU.mult)\
                        .then_inc(xm_ready, 1)
                slots(a, b, c, d)
                assert link.n == VEC_STEPS, link.n


def route_pe(nc, pe, g, r):
    pe.wait_ge(r.loaded, r.loads)
    for n in range(GROUPS):
        if n >= 2:
            pe.wait_ge(r.logits_used, n - 1)
        for k in range(KD):
            last = nc.tensor.matmul(r.bank_l[n % 2][0:EXPERTS, :], r.gate_w[:, k, :],
                                    g.xm_feat[:, k, GT * n:GT * n + GT], start=(k == 0), stop=(k == KD - 1))
        last.then_inc(r.logits_ps, 1)
    pe.wait_ge(r.logits_used, GROUPS)
    for q in range(SEQS):
        last = nc.tensor.transpose(r.bank_lt[:, q, :], r.logits_e[:, P * q:P * q + P], g.ident[0:EXPERTS, 0:EXPERTS])
    last.then_inc(r.logits_t, 1)


def route_act(nc, act, g, r, full):
    for n in range(GROUPS):
        act.wait_ge(r.logits_ps, n + 1)
        nc.scalar.copy(r.logits_e[:, GT * n:GT * n + GT], r.bank_l[n % 2][0:EXPERTS, :]).then_inc(r.logits_used, 1)
    act.wait_ge(r.second_less_first, 1)
    nc.scalar.activation(r.work[:, 1, :], r.work[:, 0, :], ACT.Exp).then_inc(r.exps, 1)
    if full:
        nc.scalar.activation(r.all_exp[:], r.logits[:], ACT.Exp).then_inc(r.exps, 1)


def route_dve(nc, dve, g, r, link, full):
    v = nc.vector
    dve.wait_ge(r.logits_t, 1)
    link(v.tensor_copy(r.logits[:], r.bank_lt[:]))
    for q in range(SEQS):
        ins = v.max(r.top[:, q, :], r.logits[:, q, :])
    link(ins)
    for q in range(SEQS):
        ins = v.max_index(r.top_at[:, q, :], r.top[:, q, :], r.logits[:, q, :])
    link(ins)
    link(v.tensor_copy(r.at[:], r.top_at[:, :, 0:2]))
    for n in range(2):
        link(v.tensor_tensor(r.hot[:, n], bc(r.at[:, :, n:n + 1], [P, SEQS, EXPERTS]),
                             bc(g.iota8[:].unsqueeze(1), [P, SEQS, EXPERTS]), ALU.is_equal))
    if full:
        link(v.tensor_tensor(r.logits[:], r.logits[:], bc(r.top[:, :, 0:1], [P, SEQS, EXPERTS]), ALU.subtract))
    v.tensor_tensor(r.work[:, 0, :], r.top[:, :, 1], r.top[:, :, 0], ALU.subtract).then_inc(r.second_less_first, 1)
    dve.wait_ge(r.exps, 2 if full else 1)
    if full:
        link(v.tensor_reduce(r.work[:, 2, :], r.all_exp[:], AX.X, ALU.add))
    else:
        link(v.tensor_scalar(r.work[:, 2, :], r.work[:, 1, :], 1.0, None, ALU.add))
    link(v.reciprocal(r.prob[:, 0, :], r.work[:, 2, :]))
    link(v.tensor_tensor(r.prob[:, 1, :], r.prob[:, 0, :], r.work[:, 1, :], ALU.mult))


def route_buffers(ctx, nc, g, tag):
    def sb(name, *shape, dt=F32):
        return ctx.enter_context(nc.sbuf_tensor(tag + name, list(shape), dt))
    r = Shared()
    r.gate_w = sb("gate_w", P, KD, EXPERTS)
    r.logits_e = sb("logits_e", EXPERTS, SEQS * P)
    r.logits, r.all_exp = sb("logits", P, SEQS, EXPERTS), sb("all_exp", P, SEQS, EXPERTS)
    r.top, r.top_at, r.at = sb("top", P, SEQS, 8), sb("top_at", P, SEQS, 8, dt=U32), sb("at", P, SEQS, 2)
    r.hot = sb("hot", P, 2, SEQS, EXPERTS)
    r.work, r.prob = sb("work", P, 3, SEQS), sb("prob", P, 2, SEQS)
    r.logits_ps, r.logits_used, r.logits_t = g.sem(tag + "logits_ps"), g.sem(tag + "logits_used"), g.sem(tag + "logits_t")
    r.second_less_first, r.exps, r.link = g.sem(tag + "second_less_first"), g.sem(tag + "exps"), g.sem(tag + "link")
    return r


def moe_phase(nc, g):
    UP_BANKS, OUT_BANKS = 4, 2
    with ExitStack() as ctx:
        def sb(name, *shape):
            return ctx.enter_context(nc.sbuf_tensor(name, list(shape), F32))

        def ps(name, *shape):
            return ctx.enter_context(nc.psum_tensor(name, list(shape), F32))

        sem = g.sem
        r = route_buffers(ctx, nc, g, "e_")
        w1 = sb("w1", P, 2, KD, FF)
        w2 = sb("w2", P, 2, KF, D)
        tanh = sb("e_tanh", P, UP_BANKS, GT)
        hid = sb("e_hid", P, 2, KF, GT)
        combine = sb("combine", P, SEQS, EXPERTS)
        second = sb("e_second", P, SEQS, EXPERTS)
        bank_up = [ps(f"bank_up{n}", P, GT) for n in range(UP_BANKS)]
        bank_out = [ps(f"bank_out{n}", P, D) for n in range(OUT_BANKS)]
        r.bank_l = bank_up[0:2]
        r.bank_lt = ps("bank_lt", P, SEQS, EXPERTS)
        r.loaded, r.loads = sem("e_gate_loaded"), 16
        w_loaded = [sem("e_w_loaded0"), sem("e_w_loaded1")]
        w_used = sem("e_w_used")
        up_ps, tanh_ready, hid_ready = sem("e_up_ps"), sem("e_tanh_ready"), sem("e_hid_ready")
        out_ps, added, combine_ready = sem("e_out_ps"), sem("e_added"), sem("e_combine_ready")
        block = ctx.enter_context(nc.Block())

        @block.sync
        def _(sp):
            sp.dma_start(r.gate_w[:], g.dram["gate_w"]).then_inc(r.loaded, 16)
            for b in range(2):
                sp.dma_start(w1[:, b], g.dram["moe_w1"][b]).then_inc(w_loaded[b], 16)
                sp.dma_start(w2[:, b], g.dram["moe_w2"][b]).then_inc(w_loaded[b], 16)
            with sp.Fori(0, EXPERTS // 2 - 1) as i:
                for b in range(2):
                    sp.wait_ge(w_used, i * 2 + (b + 1))
                    sp.dma_start(w1[:, b], g.dram["moe_w1"][i * 2 + (2 + b)]).then_inc(w_loaded[b], 16)
                    sp.dma_start(w2[:, b], g.dram["moe_w2"][i * 2 + (2 + b)]).then_inc(w_loaded[b], 16)

        STEPS_E, STEPS_I = GROUPS, 2 * GROUPS

        @block.tensor
        def _(pe):
            route_pe(nc, pe, g, r)
            with pe.Fori(0, EXPERTS // 2) as i:
                for b in range(2):
                    with pe.Fori(0, GROUPS // 2) as m:
                        pe.wait_ge(w_loaded[b], i * 32 + 32)
                        for gb in range(2):
                            step = i * STEPS_I + m * 2 + (b * STEPS_E + gb)
                            tok = m * (2 * GT) + gb * GT
                            for f in range(KF):
                                pe.wait_ge(hid_ready, step * KF + (f + 1))
                                for k in range(KD):
                                    last = nc.tensor.matmul(bank_up[f % UP_BANKS][:], w1[:, b, k, P * f:P * f + P],
                                                            g.xm_feat[:, k, bass.ds(tok, GT)],
                                                            start=(k == 0), stop=(k == KD - 1))
                                last.then_inc(up_ps, 1)
                            for j in range(GROUP):
                                pe.wait_ge(added, step * GROUP + (j + 1))
                                for f in range(KF):
                                    if j == 0:
                                        pe.wait_ge(hid_ready, step * KF + (f + 1 + UP_BANKS))
                                    last = nc.tensor.matmul(bank_out[j % OUT_BANKS][:],
                                                            hid[:, gb, f, P * j:P * j + P], w2[:, b, f, :],
                                                            start=(f == 0), stop=(f == KF - 1))
                                last.then_inc(out_ps, 1)
                    pe.drain().then_inc(w_used, 1)

        @block.scalar
        def _(act):
            route_act(nc, act, g, r, False)
            with act.Fori(0, EXPERTS * GROUPS // 2) as s:
                for gb in range(2):
                    for f in range(KF):
                        act.wait_ge(up_ps, s * (2 * KF) + (gb * KF + f + 1))
                        nc.scalar.activation(tanh[:, f % UP_BANKS, :], bank_up[f % UP_BANKS][:], ACT.Tanh, scale=0.5)\
                            .then_inc(tanh_ready, 1)

        @block.vector
        def _(dve):
            v = nc.vector
            link = Links(dve, r.link)
            route_dve(nc, dve, g, r, link, False)
            link(v.scalar_tensor_tensor(out=second[:], in0=r.hot[:, 1], scalar=0.5,
                                        in1=bc(r.prob[:, 1, :].unsqueeze(2), [P, SEQS, EXPERTS]),
                                        op0=ALU.mult, op1=ALU.mult))
            link(v.scalar_tensor_tensor(out=combine[:], in0=r.hot[:, 0], scalar=0.5,
                                        in1=bc(r.prob[:, 0, :].unsqueeze(2), [P, SEQS, EXPERTS]),
                                        op0=ALU.mult, op1=ALU.mult))
            link(v.tensor_tensor(combine[:], combine[:], second[:], ALU.add))
            dve.sem_inc(hid_ready, UP_BANKS)
            dve.sem_inc(added, OUT_BANKS)
            with dve.Fori(0, EXPERTS) as e:
                with dve.Fori(0, GROUPS // 2) as m:
                    for gb in range(2):
                        step = e * GROUPS + m * 2 + gb
                        for f in range(KF):
                            dve.wait_ge(tanh_ready, step * KF + (f + 1))
                            v.scalar_tensor_tensor(out=hid[:, gb, f, :], in0=tanh[:, f % UP_BANKS, :], scalar=1.0,
                                                   in1=bank_up[f % UP_BANKS][:], op0=ALU.add, op1=ALU.mult)\
                                .then_inc(hid_ready, 1)
                        for j in range(GROUP):
                            dve.wait_ge(out_ps, step * GROUP + (j + 1))
                            q = m * (2 * GROUP) + (gb * GROUP + j)
                            v.scalar_tensor_tensor(out=g.X[:, q, :], in0=bank_out[j % OUT_BANKS][:],
                                                   scalar=combine[:, q, bass.ds(e, 1)], in1=g.X[:, q, :],
                                                   op0=ALU.mult, op1=ALU.add).then_inc(added, 1)


def wkv_phase(nc, g):
    SP1 = P + 1
    with ExitStack() as ctx:
        def sb(name, *shape):
            return ctx.enter_context(nc.sbuf_tensor(name, list(shape), F32))

        def ps(name, *shape):
            return ctx.enter_context(nc.psum_tensor(name, list(shape), F32))

        sem = g.sem
        stats, mean_var, halves = sb("k_stats", P, GROUP, 6), sb("k_mean_var", P, GROUP, 2), sb("k_halves", P, 4, GROUP)
        small = sb("k_small", P, 4, GROUP)
        n_tok = sb("k_n_tok", P, GROUP, D)
        v_feat = sb("k_v_feat", P, 2, KD, GROUP, P)
        time_decay, time_first = sb("k_time_decay", P, KD), sb("k_time_first", P, KD)
        fac = sb("k_fac", P, 4, KD)
        keep = sb("k_keep", P, KD, GROUP, SP1)
        ek, ekv = sb("k_ek", P, KD, GROUP, SP1), sb("k_ekv", P, KD, GROUP, SP1)
        eu, euv = sb("k_eu", P, KD, GT), sb("k_euv", P, KD, GT)
        den_sum, num_sum = sb("k_den_sum", P, KD, GROUP, SP1), sb("k_num_sum", P, KD, GROUP, SP1)
        den, num = sb("k_den", P, KD, GT), sb("k_num", P, KD, GT)
        bank_t = [ps(f"k_bank_t{k}", P, GT) for k in range(KD)]
        bank_y = [ps(f"k_bank_y{j}", P, 2, D) for j in range(2)]
        bank_n = [ps(f"k_bank_n{k}", P, GT) for k in range(KD)]

        loaded, consts, vec = sem("k_loaded"), sem("k_consts"), sem("k_vec")
        v_loaded = [sem("k_v_loaded0"), sem("k_v_loaded1")]
        var_ready, rstd_ready, n_ready = sem("k_var_ready"), sem("k_rstd_ready"), sem("k_n_ready")
        kT_ps, ek_ready, v_used = sem("k_kT_ps"), sem("k_ek_ready"), sem("k_v_used")
        ekv_ready, y_ready, y_ps, added = sem("k_ekv_ready"), sem("k_y_ready"), sem("k_y_ps"), sem("k_added")
        n2_ready, nT_ps, nT_used = sem("k_n2_ready"), sem("k_nT_ps"), sem("k_nT_used")
        VEC_STEPS, PRE = 26, 5
        block = ctx.enter_context(nc.Block())

        @block.sync
        def _(sp):
            sp.dma_start(time_decay[:], g.dram["time_decay"]).then_inc(loaded, 16)
            sp.dma_start(time_first[:], g.dram["time_first"]).then_inc(loaded, 16)
            with sp.Fori(0, GROUPS // 2) as i:
                for b in range(2):
                    sp.wait_ge(v_used, i * 2 + (b + 1))
                    for k in range(KD):
                        sp.dma_start(v_feat[:, b, k], g.dram["ctx_feat"][:, k, bass.ds(i * (2 * GROUP) + b * GROUP, GROUP), :])\
                            .then_inc(v_loaded[b], 16)

        @block.gpsimd
        def _(pool):
            p = nc.gpsimd
            p.memset(keep[:], 0.0).then_inc(consts, 1)
            p.memset(ek[:], 0.0).then_inc(consts, 1)
            p.memset(ekv[:], 0.0).then_inc(consts, 1)
            pool.sem_inc(v_used, 2)
            pool.wait_ge(consts, 3)
            with pool.Fori(0, GROUPS // 2) as m:
                for b in range(2):
                    i = m * 2 + b
                    pool.wait_ge(var_ready, i * 2 + 1)
                    p.tensor_tensor(small[:, 1, :], small[:, 0, :], g.neg_half[:, 0:GROUP], ALU.pow)\
                        .then_inc(rstd_ready, 1)
                    pool.wait_ge(v_loaded[b], m * 32 + 32)
                    for k in range(KD):
                        pool.wait_ge(ek_ready, i * 4 + (2 * k + 1))
                        p.tensor_tensor(ekv[:, k, :, 1:], ek[:, k, :, 1:], v_feat[:, b, k], ALU.mult)\
                            .then_inc(ekv_ready, 1)
                        pool.wait_ge(ek_ready, i * 4 + (2 * k + 2))
                        ins = p.tensor_tensor(euv[:, k, :], eu[:, k, :], v_feat[:, b, k].rearrange("p a b -> p (a b)"),
                                              ALU.mult)
                        ins.then_inc(ekv_ready, 1)
                    pool.wait_ge(ekv_ready, i * 4 + 4)
                    pool.sem_inc(v_used, 1)
                    pool.wait_ge(var_ready, i * 2 + 2)
                    p.tensor_tensor(small[:, 1, :], small[:, 0, :], g.neg_half[:, 0:GROUP], ALU.pow)\
                        .then_inc(rstd_ready, 1)

        @block.tensor
        def _(pe):
            with pe.Fori(0, GROUPS) as i:
                for j in range(GROUP):
                    pe.wait_ge(n_ready, i * GROUP + (j + 1))
                    for k in range(KD):
                        last = nc.tensor.transpose(bank_t[k][:, P * j:P * j + P], n_tok[:, j, P * k:P * k + P], g.ident[:])
                last.then_inc(kT_ps, 1)
                for k in range(KD):
                    pe.wait_ge(y_ready, i * KD + (k + 1))
                    for j in range(GROUP):
                        last = nc.tensor.transpose(bank_y[j // 2][:, j % 2, P * k:P * k + P],
                                                   num[:, k, P * j:P * j + P], g.ident[:])
                last.then_inc(y_ps, 1)
                for j in range(GROUP):
                    pe.wait_ge(n2_ready, i * GROUP + (j + 1))
                    for k in range(KD):
                        last = nc.tensor.transpose(bank_n[k][:, P * j:P * j + P], n_tok[:, j, P * k:P * k + P], g.ident[:])
                last.then_inc(nT_ps, 1)

        @block.scalar
        def _(act):
            act.wait_ge(loaded, 32)
            nc.scalar.activation(fac[:, 1, :], time_decay[:], ACT.Exp).then_inc(vec, 1)
            act.wait_ge(vec, 1)
            nc.scalar.activation(fac[:, 0, :], fac[:, 1, :], ACT.Exp, scale=-1.0).then_inc(vec, 1)
            act.wait_ge(vec, 4)
            nc.scalar.activation(fac[:, 3, :], fac[:, 3, :], ACT.Exp).then_inc(vec, 1)
            act.wait_ge(consts, 3)
            with act.Fori(0, GROUPS) as i:
                act.wait_ge(kT_ps, i + 1)
                for k in range(KD):
                    nc.scalar.activation(ek[:, k, :, 1:], bank_t[k][:].rearrange("p (a b) -> p a b", a=GROUP), ACT.Exp)\
                        .then_inc(ek_ready, 1)
                    nc.scalar.activation(eu[:, k, :], bank_t[k][:], ACT.Exp, bias=fac[:, 2, k:k + 1]).then_inc(ek_ready, 1)
                act.wait_ge(nT_ps, i + 1)
                for k in range(KD):
                    nc.scalar.copy(g.xm_feat[:, k, bass.ds(i * GT, GT)], bank_n[k][:]).then_inc(nT_used, 1)

        @block.vector
        def _(dve):
            v = nc.vector
            dve.wait_ge(loaded, 32)
            dve.wait_ge(vec, 2)
            v.tensor_scalar(fac[:, 2, :], time_first[:], 0.0, None, ALU.min).then_inc(vec, 1)
            v.tensor_scalar(fac[:, 3, :], time_first[:], 0.0, -1.0, ALU.max, ALU.mult).then_inc(vec, 1)
            dve.wait_ge(vec, 5)
            dve.wait_ge(consts, 3)
            for k in range(KD):
                ins = v.tensor_scalar(keep[:, k, :, 1:], keep[:, k, :, 1:], fac[:, 0, k:k + 1], None, ALU.add)
            ins.then_inc(consts, 1)
            dve.wait_ge(consts, 4)

            def layer_norm(link, i, part, ready):
                for j in range(GROUP):
                    ins = v.bn_stats(stats[:, j, :], g.X[:, i * GROUP + j, :])
                link(ins)
                merge_stats(v, link, stats[:], mean_var, halves)
                v.tensor_scalar(small[:, 0, :], mean_var[:, :, 1], LN_EPS, None, ALU.add).then_inc(var_ready, 1)
                dve.wait_ge(rstd_ready, i * 2 + (part + 1))
                for j in range(GROUP):
                    v.tensor_scalar(n_tok[:, j, :], g.X[:, i * GROUP + j, :], mean_var[:, j, 0:1],
                                    small[:, 1, j:j + 1], ALU.subtract, ALU.mult).then_inc(ready, 1)
            with dve.Fori(0, GROUPS) as i:
                link = Links(dve, vec, i * VEC_STEPS + PRE)
                layer_norm(link, i, 0, n_ready)
                for k in range(KD):
                    dve.wait_ge(ek_ready, i * 4 + (2 * k + 1))
                    link(v.tensor_tensor_scan(den_sum[:, k].rearrange("p a b -> p (a b)"),
                                              keep[:, k].rearrange("p a b -> p (a b)"),
                                              ek[:, k].rearrange("p a b -> p (a b)"), 0.0, ALU.mult, ALU.add))
                    dve.wait_ge(ek_ready, i * 4 + (2 * k + 2))
                    link(v.scalar_tensor_tensor(out=den[:, k].rearrange("p (a b) -> p a b", a=GROUP),
                                                in0=den_sum[:, k, :, 0:P], scalar=fac[:, 3, k:k + 1],
                                                in1=eu[:, k].rearrange("p (a b) -> p a b", a=GROUP),
                                                op0=ALU.mult, op1=ALU.add))
                    link(v.reciprocal(den[:, k], den[:, k]))
                    dve.wait_ge(ekv_ready, i * 4 + (2 * k + 1))
                    link(v.tensor_tensor_scan(num_sum[:, k].rearrange("p a b -> p (a b)"),
                                              keep[:, k].rearrange("p a b -> p (a b)"),
                                              ekv[:, k].rearrange("p a b -> p (a b)"), 0.0, ALU.mult, ALU.add))
                    dve.wait_ge(ekv_ready, i * 4 + (2 * k + 2))
                    link(v.scalar_tensor_tensor(out=num[:, k].rearrange("p (a b) -> p a b", a=GROUP),
                                                in0=num_sum[:, k, :, 0:P], scalar=fac[:, 3, k:k + 1],
                                                in1=euv[:, k].rearrange("p (a b) -> p a b", a=GROUP),
                                                op0=ALU.mult, op1=ALU.add))
                    v.tensor_tensor(num[:, k], num[:, k], den[:, k], ALU.mult).then_inc(y_ready, 1)
                dve.wait_ge(y_ps, i + 1)
                for h in range(2):
                    seqs = bass.ds(i * GROUP + 2 * h, 2)
                    link(v.tensor_tensor(g.X[:, seqs, :], g.X[:, seqs, :], bank_y[h][:], ALU.add))
                v.memset(small[:, 3, :], 0.0)
                layer_norm(link, i, 1, n2_ready)
                dve.wait_ge(nT_used, i * KD + KD)
                assert link.n == VEC_STEPS, link.n


def switch_phase(nc, g):
    UP_BANKS, OUT_BANKS = 4, 2
    BLOCKS = 2 * SEQS
    with ExitStack() as ctx:
        def sb(name, *shape):
            return ctx.enter_context(nc.sbuf_tensor(name, list(shape), F32))

        def ps(name, *shape):
            return ctx.enter_context(nc.psum_tensor(name, list(shape), F32))

        sem = g.sem
        r = route_buffers(ctx, nc, g, "s_")
        w1, w2 = sb("s_w1", P, KD, FF), sb("s_w2", P, KF, D)
        b1, b2 = sb("s_b1", P, KF), sb("s_b2", 1, D)
        hid = sb("s_hid", P, 2, KF, GT)
        before = sb("s_before", P, P)
        counts = sb("s_counts", P, EXPERTS, BLOCKS + 1)
        carry = sb("s_carry", P, EXPERTS, BLOCKS + 1)
        offset = sb("s_offset", P, EXPERTS, BLOCKS + 1)
        slot = sb("s_slot", P, BLOCKS, EXPERTS)
        kept = sb("s_kept", P, 2, SEQS)
        weight = sb("s_weight", P, SEQS)
        bank_up = [ps(f"s_bank_up{n}", P, GT) for n in range(UP_BANKS)]
        bank_out = [ps(f"s_bank_out{n}", P, D) for n in range(OUT_BANKS)]
        r.bank_l = bank_up[0:2]
        r.bank_lt = ps("s_bank_lt", P, SEQS, EXPERTS)
        bank_c = ps("s_bank_c", P, 2, BLOCKS * EXPERTS)
        r.loaded, r.loads = sem("s_loaded"), 16 * 5
        consts, hot_ready, counts_ps = sem("s_consts"), sem("s_hot_ready"), sem("s_counts_ps")
        up_ps, hid_ready, out_ps, added = sem("s_up_ps"), sem("s_hid_ready"), sem("s_out_ps"), sem("s_added")
        block = ctx.enter_context(nc.Block())

        @block.sync
        def _(sp):
            for dst, src in ((r.gate_w, g.dram["router_w"]), (w1, g.dram["switch_w1"]), (b1, g.dram["switch_b1"]), (w2, g.dram["switch_w2"]), (b2, g.dram["switch_b2"])):
                sp.dma_start(dst[:], src).then_inc(r.loaded, 16)

        @block.gpsimd
        def _(pool):
            nc.gpsimd.memset(counts[:], 0.0).then_inc(consts, 1)
            nc.gpsimd.memset(carry[:], 1.0).then_inc(consts, 1)
            pool.wait_ge(consts, 2)
            nc.gpsimd.memset(carry[:, :, 0:1], 0.0).then_inc(consts, 1)
            nc.gpsimd.tensor_tensor(before[:], g.upto[:], g.ident[:], ALU.subtract).then_inc(consts, 1)

        @block.tensor
        def _(pe):
            route_pe(nc, pe, g, r)
            pe.wait_ge(consts, 4)
            pe.wait_ge(hot_ready, 1)
            hot = r.hot[:].rearrange("p n q e -> p (n q e)")
            nc.tensor.matmul(bank_c[:, 0, :], before[:], hot, start=True, stop=True)
            nc.tensor.matmul(bank_c[:, 1, :], g.ones[:], hot, start=True, stop=True).then_inc(counts_ps, 1)
            with pe.Fori(0, GROUPS // 2) as m:
                for gb in range(2):
                    i = m * 2 + gb
                    for f in range(KF):
                        pe.wait_ge(hid_ready, i * KF + (f + 1))
                        for k in range(KD):
                            last = nc.tensor.matmul(bank_up[f % UP_BANKS][:], w1[:, k, P * f:P * f + P],
                                                    g.xm_feat[:, k, bass.ds(i * GT, GT)],
                                                    start=(k == 0), stop=(k == KD - 1))
                        last.then_inc(up_ps, 1)
                    for j in range(GROUP):
                        pe.wait_ge(added, i * GROUP + (j + 1))
                        nc.tensor.matmul(bank_out[j % OUT_BANKS][:], g.ones[0:1, :], b2[:], start=True, stop=False)
                        for f in range(KF):
                            if j == 0:
                                pe.wait_ge(hid_ready, i * KF + (f + 1 + UP_BANKS))
                            last = nc.tensor.matmul(bank_out[j % OUT_BANKS][:], hid[:, gb, f, P * j:P * j + P],
                                                    w2[:, f, :], start=False, stop=(f == KF - 1))
                        last.then_inc(out_ps, 1)

        @block.scalar
        def _(act):
            route_act(nc, act, g, r, True)
            act.sem_inc(hid_ready, UP_BANKS)
            with act.Fori(0, GROUPS // 2) as m:
                for gb in range(2):
                    for f in range(KF):
                        act.wait_ge(up_ps, m * (2 * KF) + (gb * KF + f + 1))
                        nc.scalar.activation(hid[:, gb, f, :], bank_up[f % UP_BANKS][:], ACT.Gelu, bias=b1[:, f:f + 1])\
                            .then_inc(hid_ready, 1)

        @block.vector
        def _(dve):
            v = nc.vector
            link = Links(dve, r.link)
            route_dve(nc, dve, g, r, link, True)
            dve.sem_inc(hot_ready, 1)
            dve.wait_ge(counts_ps, 1)
            dve.wait_ge(consts, 4)
            link(v.tensor_copy(counts[:, :, 1:], bank_c[:, 1, :].rearrange("p (n e) -> p e n", e=EXPERTS)))
            link(v.tensor_tensor_scan(offset[:].rearrange("p e n -> p (e n)"), carry[:].rearrange("p e n -> p (e n)"),
                                      counts[:].rearrange("p e n -> p (e n)"), 0.0, ALU.mult, ALU.add))
            link(v.tensor_tensor(slot[:], bank_c[:, 0, :].rearrange("p (n e) -> p n e", e=EXPERTS),
                                 offset[:, :, 0:BLOCKS].rearrange("p e n -> p n e"), ALU.add))
            link(v.tensor_scalar(slot[:], slot[:], CAP - 0.5, None, ALU.is_lt))
            link(v.tensor_tensor(slot[:], slot[:], r.hot[:].rearrange("p n q e -> p (n q) e"), ALU.mult))
            link(v.tensor_reduce(kept[:].rearrange("p n q -> p (n q)"), slot[:], AX.X, ALU.add))
            link(v.tensor_tensor(kept[:], kept[:], r.prob[:], ALU.mult))
            link(v.tensor_tensor(weight[:], kept[:, 0], kept[:, 1], ALU.add))
            dve.sem_inc(added, OUT_BANKS)
            with dve.Fori(0, GROUPS) as i:
                for j in range(GROUP):
                    dve.wait_ge(out_ps, i * GROUP + (j + 1))
                    q = i * GROUP + j
                    v.scalar_tensor_tensor(out=g.X[:, q, :], in0=bank_out[j % OUT_BANKS][:], scalar=weight[:, bass.ds(q, 1)],
                                           in1=g.X[:, q, :], op0=ALU.mult, op1=ALU.add).then_inc(added, 1)


def norm_buffers(ctx, nc, g, tag):
    def sb(name, *shape):
        return ctx.enter_context(nc.sbuf_tensor(tag + name, list(shape), F32))
    n = Shared()
    n.stats, n.mean_var, n.halves = sb("stats", P, GROUP, 6), sb("mean_var", P, GROUP, 2), sb("halves", P, 4, GROUP)
    n.small, n.tok = sb("small", P, 2, GROUP), sb("n_tok", P, GROUP, D)
    n.var_ready, n.rstd_ready, n.ready = g.sem(tag + "var_ready"), g.sem(tag + "rstd_ready"), g.sem(tag + "n_ready")
    return n


def norm_dve(nc, dve, g, n, link, i):
    v = nc.vector
    for j in range(GROUP):
        ins = v.bn_stats(n.stats[:, j, :], g.X[:, i * GROUP + j, :])
    link(ins)
    merge_stats(v, link, n.stats[:], n.mean_var, n.halves)
    v.tensor_scalar(n.small[:, 0, :], n.mean_var[:, :, 1], LN_EPS, None, ALU.add).then_inc(n.var_ready, 1)
    dve.wait_ge(n.rstd_ready, i + 1)
    for j in range(GROUP):
        v.tensor_scalar(n.tok[:, j, :], g.X[:, i * GROUP + j, :], n.mean_var[:, j, 0:1], n.small[:, 1, j:j + 1],
                        ALU.subtract, ALU.mult).then_inc(n.ready, 1)


def norm_pool(nc, pool, g, n, i):
    pool.wait_ge(n.var_ready, i + 1)
    nc.gpsimd.tensor_tensor(n.small[:, 1, :], n.small[:, 0, :], g.neg_half[:, 0:GROUP], ALU.pow)\
        .then_inc(n.rstd_ready, 1)


def turn_pe(nc, pe, g, n, banks, turned, i):
    for j in range(GROUP):
        pe.wait_ge(n.ready, i * GROUP + (j + 1))
        for k in range(KD):
            last = nc.tensor.transpose(banks[k][:, P * j:P * j + P], n.tok[:, j, P * k:P * k + P], g.ident[:])
    last.then_inc(turned, 1)


BLK = 16
NBLK = P // BLK
FLOOR = -75.0
GH = 8
HK = P // GH


def gla_phase(nc, g):
    UNITS = GROUP * KD
    VEC_STEPS = 7 + KD * 2 + GROUP * 7
    with ExitStack() as ctx:
        def sb(name, *shape):
            return ctx.enter_context(nc.sbuf_tensor("g_" + name, list(shape), F32))

        def ps(name, *shape):
            return ctx.enter_context(nc.psum_tensor("g_" + name, list(shape), F32))

        sem = lambda name: g.sem("g_" + name)
        n = norm_buffers(ctx, nc, g, "g_")
        w = {m: sb("w" + m, P, KD, D) for m in "qkvgo"}
        gamma, beta = sb("gamma", P, KD), sb("beta", P, KD)
        n_feat = sb("n_feat", P, KD, GT)
        k_feat, q_feat, v_tok = sb("k_feat", P, KD, GT), sb("q_feat", P, KD, GT), sb("v_tok", P, GROUP, D)
        absx, soft = sb("absx", P, GT), sb("soft", P, KD, GT)
        logg, run = sb("logg", P, KD, GT), sb("run", P, KD, GROUP, P)
        front = sb("front", P, KD, GROUP, NBLK)
        eq = sb("eq", P, KD, GT)
        reset = sb("reset", P, GROUP, P)
        head = sb("head", P, GH)
        dk = sb("dk", P, 2, NBLK, P)
        kt = sb("kt", P, 2, NBLK, P)
        qbd = sb("qbd", P, 2, NBLK, GH, BLK)
        att = sb("att", P, 2, GH, NBLK, BLK)
        y_stats, y_mv, y_half = sb("y_stats", P, 1, 6), sb("y_mv", P, 1, 2), sb("y_half", P, 4, 1)
        y_small = sb("y_small", P, 2)
        y_tok = sb("y_tok", P, 2, D)
        y_feat = sb("y_feat", P, 2, KD, P)
        bank_t = [ps(f"bank_t{k}", P, GT) for k in range(2)]
        bank_p = [ps(f"bank_p{k}", P, GT) for k in range(2)]
        bank_s = [ps(f"bank_s{k}", P, NBLK // 2, GH, BLK) for k in range(2)]
        bank_y = [ps(f"bank_y{k}", P, D) for k in range(2)]

        loaded, consts, vec = sem("loaded"), sem("consts"), sem("vec")
        turned, feat_ready = sem("turned"), sem("feat_ready")
        proj_ps, p_used = sem("proj_ps"), sem("p_used")
        soft_ready, sum_ready, dq_ready, eq_ready, k_ready, q_ready, v_ready = (
            sem("soft_ready"), sem("sum_ready"), sem("dq_ready"), sem("eq_ready"), sem("k_ready"), sem("q_ready"),
            sem("v_ready"))
        dk_ready, ek_ready, kt_ready, qbd_ready = sem("dk_ready"), sem("ek_ready"), sem("kt_ready"), sem("qbd_ready")
        s_ps, att_ready, y_ps = sem("s_ps"), sem("att_ready"), sem("y_ps")
        y_var, y_rstd, y_ready, yT_ps, yT_ready, o_ps, added = (
            sem("y_var"), sem("y_rstd"), sem("y_ready"), sem("yT_ps"), sem("yT_ready"), sem("o_ps"), sem("added"))
        PROJ = [("g", 0), ("g", 1), ("k", 0), ("k", 1), ("q", 0), ("q", 1)] + [("v", j) for j in range(GROUP)]
        NPROJ = len(PROJ)
        block = ctx.enter_context(nc.Block())

        def slots(a, b, c, o):
            for s in range(UNITS + 4):
                if s < UNITS:
                    a(s)
                if 1 <= s <= UNITS:
                    b(s - 1)
                if s >= 3 and s % 2 == 1 and (s - 3) // 2 < GROUP:
                    c((s - 3) // 2)
                if s >= 4 and s % 2 == 0 and (s - 4) // 2 < GROUP:
                    o((s - 4) // 2)

        @block.sync
        def _(sp):
            for m in "gkqvo":
                sp.dma_start(w[m][:], g.dram["gla_w" + m]).then_inc(loaded, 16)
            sp.dma_start(gamma[:], g.dram["gla_gamma"]).then_inc(loaded, 16)
            sp.dma_start(beta[:], g.dram["gla_beta"]).then_inc(loaded, 16)

        @block.gpsimd
        def _(pool):
            p = nc.gpsimd
            p.memset(reset[:], 1.0).then_inc(consts, 1)
            p.memset(front[:], 0.0).then_inc(consts, 1)
            p.memset(head[:], 1.0).then_inc(consts, 1)
            pool.wait_ge(consts, 3)
            p.memset(reset[:, :, 0:1], 0.0).then_inc(consts, 1)
            p.affine_select(out=head[:], in_=head[:], compare_op=ALU.is_ge, fill=0.0, base=0,
                            pattern=[[-HK, GH]], channel_multiplier=1).then_inc(consts, 1)
            pool.wait_ge(consts, 5)
            p.affine_select(out=head[:], in_=head[:], compare_op=ALU.is_ge, fill=0.0, base=HK - 1,
                            pattern=[[HK, GH]], channel_multiplier=-1).then_inc(consts, 1)
            pool.wait_ge(consts, 6)
            with pool.Fori(0, GROUPS) as i:
                norm_pool(nc, pool, g, n, i)

                def a(u):
                    j, k = u // KD, u % KD
                    tok = slice(P * j, P * j + P)
                    pool.wait_ge(q_ready, i * KD + (k + 1))
                    if u >= 2:
                        pool.wait_ge(s_ps, i * (2 * UNITS) + (2 * (u - 1)))
                    p.tensor_tensor(qbd[:, u % 2],
                                    bc(q_feat[:, k, tok].rearrange("p (n t) -> p n t", n=NBLK).unsqueeze(2), [P, NBLK, GH, BLK]),
                                    bc(head[:].unsqueeze(1).unsqueeze(3), [P, NBLK, GH, BLK]), ALU.mult)\
                        .then_inc(qbd_ready, 1)
                    pool.wait_ge(ek_ready, i * UNITS + (u + 1))
                    pool.wait_ge(k_ready, i * KD + (k + 1))
                    p.tensor_tensor(kt[:, u % 2], dk[:, u % 2], bc(k_feat[:, k, tok].unsqueeze(1), [P, NBLK, P]),
                                    ALU.mult).then_inc(kt_ready, 1)

                def none(u):
                    pass

                def c(j):
                    pool.wait_ge(y_var, i * GROUP + (j + 1))
                    p.tensor_tensor(y_small[:, 1:2], y_small[:, 0:1], g.neg_half[:, 0:1], ALU.pow).then_inc(y_rstd, 1)
                slots(a, none, c, none)

        @block.tensor
        def _(pe):
            pe.wait_ge(loaded, 16 * 7)
            with pe.Fori(0, GROUPS) as i:
                turn_pe(nc, pe, g, n, bank_t, turned, i)
                pe.wait_ge(feat_ready, i * KD + KD)
                for m, (what, c) in enumerate(PROJ):
                    pe.wait_ge(p_used, i * NPROJ + (m + 1))
                    for k in range(KD):
                        if what == "v":
                            last = nc.tensor.matmul(bank_p[m % 2][:, 0:D], n_feat[:, k, P * c:P * c + P], w["v"][:, k, :],
                                                    start=(k == 0), stop=(k == KD - 1))
                        else:
                            last = nc.tensor.matmul(bank_p[m % 2][:], w[what][:, k, P * c:P * c + P], n_feat[:, k, :],
                                                    start=(k == 0), stop=(k == KD - 1))
                    last.then_inc(proj_ps, 1)

                def a(u):
                    pe.wait_ge(qbd_ready, i * UNITS + (u + 1))
                    pe.wait_ge(kt_ready, i * UNITS + (u + 1))
                    for h in range(2):
                        if u:
                            pe.wait_ge(att_ready, i * (2 * UNITS) + (2 * (u - 1) + h + 1))
                        for b in range(NBLK // 2):
                            blk = NBLK // 2 * h + b
                            last = nc.tensor.matmul(bank_s[h][:, b], kt[:, u % 2, blk, :], qbd[:, u % 2, blk],
                                                    start=True, stop=True)
                        last.then_inc(s_ps, 1)

                def b(u):
                    j, k = u // KD, u % KD
                    pe.wait_ge(att_ready, i * (2 * UNITS) + (2 * u + 2))
                    if u == 0:
                        pe.wait_ge(v_ready, i * GROUP + GROUP)
                    if k == 0 and j >= 2:
                        pe.wait_ge(y_ready, i * GROUP + (j - 1))
                    for h in range(GH):
                        col = P * k + HK * h
                        last = nc.tensor.matmul(bank_y[j % 2][:, col:col + HK], att[:, u % 2, h].rearrange("p n t -> p (n t)"),
                                                v_tok[:, j, col:col + HK], start=True, stop=True)
                    last.then_inc(y_ps, 1)

                def c(j):
                    pe.wait_ge(y_ready, i * GROUP + (j + 1))
                    for k in range(KD):
                        last = nc.tensor.transpose(bank_t[0][:, P * k:P * k + P], y_tok[:, j % 2, P * k:P * k + P],
                                                   g.ident[:])
                    last.then_inc(yT_ps, 1)

                def o(j):
                    pe.wait_ge(yT_ready, i * GROUP + (j + 1))
                    if j:
                        pe.wait_ge(added, i * GROUP + j)
                    for k in range(KD):
                        last = nc.tensor.matmul(bank_t[1][:, 0:D], y_feat[:, j % 2, k, :], w["o"][:, k, :],
                                                start=(k == 0), stop=(k == KD - 1))
                    last.then_inc(o_ps, 1)
                slots(a, b, c, o)
                pe.wait_ge(added, i * GROUP + GROUP)

        @block.scalar
        def _(act):
            s = nc.scalar
            act.wait_ge(loaded, 16 * 7)
            with act.Fori(0, GROUPS) as i:
                act.wait_ge(turned, i + 1)
                for k in range(KD):
                    s.copy(n_feat[:, k, :], bank_t[k][:]).then_inc(feat_ready, 1)
                for m, (what, c) in enumerate(PROJ):
                    if what == "q":
                        act.wait_ge(dq_ready, i * KD + (c + 1))
                        s.activation(eq[:, c, :], eq[:, c, :], ACT.Exp).then_inc(eq_ready, 1)
                        continue
                    act.wait_ge(proj_ps, i * NPROJ + (m + 1))
                    if what == "g":
                        s.activation(absx[:], bank_p[m % 2][:], ACT.Abs).then_inc(soft_ready, 1)
                        act.wait_ge(soft_ready, i * (3 * KD) + (3 * c + 1))
                        s.activation(soft[:, c, :], absx[:], ACT.Exp, scale=-1.0).then_inc(soft_ready, 1)
                        act.wait_ge(soft_ready, i * (3 * KD) + (3 * c + 2))
                        s.activation(soft[:, c, :], soft[:, c, :], ACT.Ln, bias=1.0).then_inc(soft_ready, 1)
                    if what == "k":
                        s.copy(k_feat[:, c, :], bank_p[m % 2][:]).then_inc(k_ready, 1)
                    if what == "v":
                        s.copy(v_tok[:, c, :], bank_p[m % 2][:, 0:D]).then_inc(v_ready, 1)

                def a(u):
                    act.wait_ge(dk_ready, i * UNITS + (u + 1))
                    s.activation(dk[:, u % 2], dk[:, u % 2], ACT.Exp, scale=-1.0).then_inc(ek_ready, 1)

                def none(u):
                    pass

                def c(j):
                    act.wait_ge(yT_ps, i * GROUP + (j + 1))
                    for k in range(KD):
                        last = s.activation(y_feat[:, j % 2, k, :], bank_t[0][:, P * k:P * k + P], ACT.Identity,
                                            scale=gamma[:, k:k + 1], bias=beta[:, k:k + 1])
                    last.then_inc(yT_ready, 1)
                slots(a, none, c, none)

        @block.vector
        def _(dve):
            v = nc.vector
            dve.wait_ge(consts, 6)
            dve.sem_inc(p_used, 2)
            with dve.Fori(0, GROUPS) as i:
                link = Links(dve, vec, i * VEC_STEPS)
                norm_dve(nc, dve, g, n, link, i)
                for m, (what, c) in enumerate(PROJ):
                    if what == "g":
                        dve.wait_ge(soft_ready, i * (3 * KD) + (3 * c + 3))
                        v.scalar_tensor_tensor(out=logg[:, c, :], in0=bank_p[m % 2][:], scalar=0.0, in1=soft[:, c, :],
                                               op0=ALU.min, op1=ALU.subtract).then_inc(p_used, 1)
                        dve.wait_ge(p_used, i * NPROJ + (m + 3))
                        link(v.tensor_tensor_scan(run[:, c].rearrange("p a b -> p (a b)"),
                                                  reset[:].rearrange("p a b -> p (a b)"), logg[:, c, :], 0.0,
                                                  ALU.mult, ALU.add))
                        link(v.tensor_copy(front[:, c, :, 1:], run[:, c, :, BLK - 1:P - 1:BLK]))
                        v.tensor_tensor(eq[:, c, :].rearrange("p (n t) -> p n t", t=BLK),
                                        run[:, c].rearrange("p a (n t) -> p (a n) t", t=BLK),
                                        bc(front[:, c].rearrange("p a n -> p (a n)").unsqueeze(2), [P, GROUP * NBLK, BLK]),
                                        ALU.subtract).then_inc(dq_ready, 1)
                    if what == "k":
                        dve.wait_ge(k_ready, i * KD + (c + 1))
                        dve.sem_inc(p_used, 1)
                    if what == "q":
                        dve.wait_ge(proj_ps, i * NPROJ + (m + 1))
                        dve.wait_ge(eq_ready, i * KD + (c + 1))
                        v.scalar_tensor_tensor(out=q_feat[:, c, :], in0=bank_p[m % 2][:], scalar=float(HK) ** -0.5,
                                               in1=eq[:, c, :], op0=ALU.mult, op1=ALU.mult).then_inc(q_ready, 1)
                        dve.wait_ge(q_ready, i * KD + (c + 1))
                        dve.sem_inc(p_used, 1)
                    if what == "v":
                        dve.wait_ge(v_ready, i * GROUP + (c + 1))
                        dve.sem_inc(p_used, 1)

                def a(u):
                    j, k = u // KD, u % KD
                    if u >= 2:
                        dve.wait_ge(kt_ready, i * UNITS + (u - 1))
                    for b in range(NBLK):
                        last = v.tensor_scalar(dk[:, u % 2, b, :], run[:, k, j, :], front[:, k, j, b:b + 1], FLOOR,
                                               ALU.subtract, ALU.max)
                    last.then_inc(dk_ready, 1)

                def b(u):
                    for h in range(2):
                        dve.wait_ge(s_ps, i * (2 * UNITS) + (2 * u + h + 1))
                        if u >= 2:
                            dve.wait_ge(y_ps, i * UNITS + (u - 1))
                        half = slice(NBLK // 2 * h, NBLK // 2 * (h + 1))
                        v.tensor_tensor(att[:, u % 2, :, half].rearrange("p h n t -> p n h t"), bank_s[h][:],
                                        bc(g.upto[:, P // 2 * h:P // 2 * (h + 1)]
                                           .rearrange("p (n t) -> p n t", t=BLK).unsqueeze(2), [P, NBLK // 2, GH, BLK]),
                                        ALU.mult).then_inc(att_ready, 1)

                def c(j):
                    dve.wait_ge(y_ps, i * UNITS + KD * (j + 1))
                    v.memset(y_half[:, 0], 0.0)
                    link(v.bn_stats(y_stats[:, 0, :], bank_y[j % 2][:]))
                    merge_stats(v, link, y_stats[:], y_mv, y_half)
                    v.tensor_scalar(y_small[:, 0:1], y_mv[:, :, 1], LN_EPS, None, ALU.add).then_inc(y_var, 1)
                    dve.wait_ge(y_rstd, i * GROUP + (j + 1))
                    v.tensor_scalar(y_tok[:, j % 2, :], bank_y[j % 2][:], y_mv[:, 0, 0:1], y_small[:, 1:2],
                                    ALU.subtract, ALU.mult).then_inc(y_ready, 1)

                def o(j):
                    dve.wait_ge(o_ps, i * GROUP + (j + 1))
                    q = i * GROUP + j
                    v.tensor_tensor(g.X[:, q, :], g.X[:, q, :], bank_t[1][:, 0:D], ALU.add).then_inc(added, 1)
                slots(a, b, c, o)
                assert link.n == VEC_STEPS, link.n


def channel_phase(nc, g):
    SCALE = float(D) ** -0.5
    VEC_STEPS = 7 + GROUP
    with ExitStack() as ctx:
        def sb(name, *shape):
            return ctx.enter_context(nc.sbuf_tensor("c_" + name, list(shape), F32))

        def ps(name, *shape):
            return ctx.enter_context(nc.psum_tensor("c_" + name, list(shape), F32))

        sem = lambda name: g.sem("c_" + name)
        n = norm_buffers(ctx, nc, g, "c_")
        c_tok, c_feat = sb("c_tok", P, 2, GROUP, D), sb("c_feat", P, 2, KD, GROUP, P)
        peak, bias, total, inv = sb("peak", P, 2, KD), sb("bias", P, 2, KD), sb("total", P, 2, KD), sb("inv", P, 2, KD)
        prob = sb("prob", P, 2, KD, D)
        bank_a = [ps(f"bank_a{k}", P, KD, D) for k in range(2)]
        bank_o = [ps(f"bank_o{k}", P, D) for k in range(2)]
        c_loaded, c_used = [sem("c_loaded0"), sem("c_loaded1")], sem("c_used")
        vec = sem("vec")
        a_ps, bias_ready, exp_ready, prob_ready, o_ps, added = (
            sem("a_ps"), sem("bias_ready"), sem("exp_ready"), sem("prob_ready"), sem("o_ps"), sem("added"))
        block = ctx.enter_context(nc.Block())

        def slots(a, b, c):
            for s in range(GROUP + 2):
                for stage, late in ((a, 0), (b, 1), (c, 2)):
                    if 0 <= s - late < GROUP:
                        stage(s - late)

        @block.sync
        def _(sp):
            with sp.Fori(0, GROUPS // 2) as m:
                for b in range(2):
                    sp.wait_ge(c_used, m * 2 + (b + 1))
                    seqs = bass.ds(m * (2 * GROUP) + b * GROUP, GROUP)
                    sp.dma_start(c_tok[:, b], g.dram["ctx"].rearrange("q s d -> s q d")[:, seqs, :]).then_inc(c_loaded[b], 16)
                    for k in range(KD):
                        sp.dma_start(c_feat[:, b, k], g.dram["ctx_feat"][:, k, seqs, :]).then_inc(c_loaded[b], 16)

        @block.gpsimd
        def _(pool):
            with pool.Fori(0, GROUPS) as i:
                norm_pool(nc, pool, g, n, i)

        @block.tensor
        def _(pe):
            with pe.Fori(0, GROUPS // 2) as m:
                for gb in range(2):
                    i = m * 2 + gb
                    pe.wait_ge(c_loaded[gb], m * 48 + 48)

                    def a(j):
                        pe.wait_ge(n.ready, i * GROUP + (j + 1))
                        pe.wait_ge(exp_ready, i * GROUP + (j + 1))
                        for k in range(KD):
                            last = nc.tensor.matmul(bank_a[j % 2][:, k, :], c_tok[:, gb, j, P * k:P * k + P], n.tok[:, j, :],
                                                    start=True, stop=True)
                        last.then_inc(a_ps, 1)

                    def none(j):
                        pass

                    def c(j):
                        pe.wait_ge(prob_ready, i * GROUP + (j + 1))
                        pe.wait_ge(added, i * GROUP + (j + 1))
                        for k in range(KD):
                            last = nc.tensor.matmul(bank_o[j % 2][:], c_feat[:, gb, k, j, :], prob[:, j % 2, k, :],
                                                    start=(k == 0), stop=(k == KD - 1))
                        last.then_inc(o_ps, 1)
                    slots(a, none, c)

        @block.scalar
        def _(act):
            act.sem_inc(exp_ready, 2)
            with act.Fori(0, GROUPS) as i:
                for j in range(GROUP):
                    act.wait_ge(bias_ready, i * GROUP + (j + 1))
                    for k in range(KD):
                        last = nc.scalar.activation(prob[:, j % 2, k, :], bank_a[j % 2][:, k, :], ACT.Exp, scale=SCALE,
                                                    bias=bias[:, j % 2, k:k + 1], accum_out=total[:, j % 2, k:k + 1])
                    last.then_inc(exp_ready, 1)

        @block.vector
        def _(dve):
            v = nc.vector
            dve.sem_inc(added, 2)
            dve.sem_inc(c_used, 2)
            with dve.Fori(0, GROUPS) as i:
                link = Links(dve, vec, i * VEC_STEPS)
                norm_dve(nc, dve, g, n, link, i)

                def a(j):
                    dve.wait_ge(a_ps, i * GROUP + (j + 1))
                    if j >= 2:
                        dve.wait_ge(o_ps, i * GROUP + (j - 1))
                    link(v.tensor_reduce(peak[:, j % 2, :], bank_a[j % 2][:], AX.X, ALU.max))
                    v.tensor_scalar(bias[:, j % 2, :], peak[:, j % 2, :], -SCALE, None, ALU.mult).then_inc(bias_ready, 1)

                def b(j):
                    dve.wait_ge(exp_ready, i * GROUP + (j + 3))
                    v.reciprocal(inv[:, j % 2, :], total[:, j % 2, :]).then_inc(g.c_inv, 1)
                    dve.wait_ge(g.c_inv, i * GROUP + (j + 1))
                    v.tensor_tensor(prob[:, j % 2], prob[:, j % 2], bc(inv[:, j % 2, :].unsqueeze(2), [P, KD, D]), ALU.mult)\
                        .then_inc(prob_ready, 1)

                def c(j):
                    dve.wait_ge(o_ps, i * GROUP + (j + 1))
                    q = i * GROUP + j
                    v.tensor_tensor(g.X[:, q, :], g.X[:, q, :], bank_o[j % 2][:], ALU.add).then_inc(added, 1)
                slots(a, b, c)
                dve.sem_inc(c_used, 1)
                assert link.n == VEC_STEPS, link.n


def ffn_phase(nc, g):
    VEC_STEPS = 7 + KF
    with ExitStack() as ctx:
        def sb(name, *shape):
            return ctx.enter_context(nc.sbuf_tensor("f_" + name, list(shape), F32))

        def ps(name, *shape):
            return ctx.enter_context(nc.psum_tensor("f_" + name, list(shape), F32))

        sem = lambda name: g.sem("f_" + name)
        n = norm_buffers(ctx, nc, g, "f_")
        w1, w3 = sb("w1", P, KD, FF), sb("w3", P, KD, FF)
        w2, w2b, w2h = sb("w2", P, KF, D), sb("w2b", P, KF, D), sb("w2h", P, KF, D)
        had = sb("had", P, P)
        n_feat = sb("n_feat", P, KD, GT)
        tanh, silu = sb("tanh", P, 2, GT), sb("silu", P, 2, GT)
        hid = sb("hid", P, KF, GT)
        bank_t = [ps(f"bank_t{k}", P, GT) for k in range(2)]
        bank_g = [ps(f"bank_g{k}", P, GT) for k in range(2)]
        bank_u = [ps(f"bank_u{k}", P, GT) for k in range(2)]
        bank_o = [ps(f"bank_o{k}", P, D) for k in range(2)]
        loaded, w_loaded, vec = sem("loaded"), sem("w_loaded"), sem("vec")
        fold, had_ps, had_used = sem("fold"), sem("had_ps"), sem("had_used")
        turned, feat_ready, gu_ps, tanh_ready, hid_ready = (
            sem("turned"), sem("feat_ready"), sem("gu_ps"), sem("tanh_ready"), sem("hid_ready"))
        o_ps, added, stored = sem("o_ps"), sem("added"), sem("stored")
        block = ctx.enter_context(nc.Block())

        @block.sync
        def _(sp):
            sp.dma_start(w2[:], g.dram["ffn_w2"]).then_inc(loaded, 16)
            sp.dma_start(had[:], g.dram["hadamard"]).then_inc(loaded, 16)
            sp.dma_start(w1[:], g.dram["ffn_w1"]).then_inc(w_loaded, 16)
            sp.dma_start(w3[:], g.dram["ffn_w3"]).then_inc(w_loaded, 16)
            with sp.Fori(0, GROUPS) as i:
                sp.wait_ge(added, i * GROUP + (GROUP + 2))
                seqs = bass.ds(i * GROUP, GROUP)
                sp.dma_start(g.dram["out"].rearrange("q t d -> t q d")[:, seqs, :], g.X[:, seqs, :]).then_inc(stored, 16)
            sp.wait_ge(stored, 16 * GROUPS)

        @block.gpsimd
        def _(pool):
            pool.wait_ge(loaded, 32)
            src, dst = w2, w2b
            for m in range(3):
                h = 1 << m
                a = src[:].rearrange("p (n two h) d -> p n two h d", two=2, h=h)
                o = dst[:].rearrange("p (n two h) d -> p n two h d", two=2, h=h)
                for x in range(KF // (2 * h)):
                    nc.gpsimd.tensor_tensor(o[:, x, 0], a[:, x, 0], a[:, x, 1], ALU.add).then_inc(fold, 1)
                    nc.gpsimd.tensor_tensor(o[:, x, 1], a[:, x, 0], a[:, x, 1], ALU.subtract).then_inc(fold, 1)
                pool.wait_ge(fold, sum(2 * (KF >> (q + 1)) for q in range(m + 1)))
                src, dst = dst, src
            pool.sem_inc(g.folded, 1)
            with pool.Fori(0, GROUPS) as i:
                norm_pool(nc, pool, g, n, i)

        @block.tensor
        def _(pe):
            pe.wait_ge(g.folded, 1)
            for f in range(KF):
                if f >= 2:
                    pe.wait_ge(had_used, f - 1)
                nc.tensor.matmul(bank_o[f % 2][:], had[:], w2b[:, f, :], start=True, stop=True).then_inc(had_ps, 1)
            pe.wait_ge(w_loaded, 32)
            with pe.Fori(0, GROUPS) as i:
                turn_pe(nc, pe, g, n, bank_t, turned, i)
                pe.wait_ge(feat_ready, i * KD + KD)
                for f in range(KF):
                    pe.wait_ge(hid_ready, i * KF + (f + 1))
                    for w, bank in ((w1, bank_g), (w3, bank_u)):
                        for k in range(KD):
                            last = nc.tensor.matmul(bank[f % 2][:], w[:, k, P * f:P * f + P], n_feat[:, k, :],
                                                    start=(k == 0), stop=(k == KD - 1))
                    last.then_inc(gu_ps, 1)
                for j in range(GROUP):
                    pe.wait_ge(added, i * GROUP + (j + 1))
                    for f in range(KF):
                        if j == 0:
                            pe.wait_ge(hid_ready, i * KF + (f + 3))
                        last = nc.tensor.matmul(bank_o[j % 2][:], hid[:, f, P * j:P * j + P], w2h[:, f, :],
                                                start=(f == 0), stop=(f == KF - 1))
                    last.then_inc(o_ps, 1)

        @block.scalar
        def _(act):
            for f in range(KF):
                act.wait_ge(had_ps, f + 1)
                nc.scalar.mul(w2h[:, f, :], bank_o[f % 2][:], 0.5 / float(FF) ** 0.5).then_inc(had_used, 1)
            with act.Fori(0, GROUPS) as i:
                act.wait_ge(turned, i + 1)
                for k in range(KD):
                    nc.scalar.copy(n_feat[:, k, :], bank_t[k][:]).then_inc(feat_ready, 1)
                for f in range(KF):
                    act.wait_ge(gu_ps, i * KF + (f + 1))
                    nc.scalar.activation(tanh[:, f % 2, :], bank_g[f % 2][:], ACT.Tanh, scale=0.5).then_inc(tanh_ready, 1)

        @block.vector
        def _(dve):
            v = nc.vector
            dve.wait_ge(had_used, KF)
            dve.sem_inc(hid_ready, 2)
            dve.sem_inc(added, 2)
            with dve.Fori(0, GROUPS) as i:
                link = Links(dve, vec, i * VEC_STEPS)
                norm_dve(nc, dve, g, n, link, i)
                for f in range(KF):
                    dve.wait_ge(tanh_ready, i * KF + (f + 1))
                    link(v.scalar_tensor_tensor(out=silu[:, f % 2, :], in0=tanh[:, f % 2, :], scalar=1.0,
                                                in1=bank_g[f % 2][:], op0=ALU.add, op1=ALU.mult))
                    v.tensor_tensor(hid[:, f, :], silu[:, f % 2, :], bank_u[f % 2][:], ALU.mult).then_inc(hid_ready, 1)
                for j in range(GROUP):
                    dve.wait_ge(o_ps, i * GROUP + (j + 1))
                    q = i * GROUP + j
                    v.tensor_tensor(g.X[:, q, :], g.X[:, q, :], bank_o[j % 2][:], ALU.add).then_inc(added, 1)
                assert link.n == VEC_STEPS, link.n


def build_program(nc, dram):
    with ExitStack() as ctx:
        g = Shared()
        g.dram = dram
        g.sem = lambda name: ctx.enter_context(nc.semaphore(name))

        def sb(name, *shape):
            return ctx.enter_context(nc.sbuf_tensor(name, list(shape), F32))
        g.X = sb("X", P, SEQS, D)
        g.xm_feat = sb("xm_feat", P, KD, SEQS * P)
        g.ident, g.upto, g.after, g.ones = sb("ident", P, P), sb("upto", P, P), sb("after", P, P), sb("ones", P, P)
        g.neg_half = sb("neg_half", P, SEQS)
        g.x_loaded, g.a_exp = g.sem("x_loaded"), g.sem("a_exp")
        g.vec_steps_mamba = 55
        g.iota8 = sb("iota8", P, EXPERTS)
        mamba_phase(nc, g)
        moe_phase(nc, g)
        wkv_phase(nc, g)
        switch_phase(nc, g)
        g.c_inv, g.folded = g.sem("c_inv"), g.sem("f_folded")
        gla_phase(nc, g)
        channel_phase(nc, g)
        ffn_phase(nc, g)


def _tiles(a):
    return a.reshape((a.shape[0] // P, P) + a.shape[1:]).swapaxes(0, 1)


def hadamard(n):
    h = np.ones((1, 1), np.float32)
    while len(h) < n:
        h = np.block([[h, h], [h, -h]])
    return h


def laid_out(inputs):
    f = {k: np.asarray(v) for k, v in inputs.items()}
    w = lambda name: f[name]
    return {
        "x": w("x"),
        "in_proj_w": _tiles(w("L0_attn_in_proj_w").T),
        "out_proj_w": _tiles(w("L0_attn_out_proj_w").T),
        "norm_mamba_w": _tiles(w("L0_attn_norm_mamba_w")),
        "norm_moe_w": _tiles(w("L0_attn_norm_moe_w")),
        "ssm_norm_w": _tiles(w("L0_attn_ssm_norm_w")),
        "conv_w_inner": _tiles(w("L0_attn_conv_w")[:DI]),
        "conv_b_inner": _tiles(w("L0_attn_conv_b")[:DI]),
        "conv_w_bc": w("L0_attn_conv_w")[DI:].reshape(2, NS, TAPS).swapaxes(0, 1),
        "conv_b_bc": w("L0_attn_conv_b")[DI:].reshape(2, NS).T,
        "dt_bias": w("L0_attn_dt_bias"),
        "gate_w": _tiles(w("L0_attn_gate_w").T),
        "moe_w1": w("L0_attn_w1").transpose(0, 2, 1).reshape(EXPERTS, KD, P, FF).swapaxes(1, 2),
        "moe_w2": w("L0_attn_w2").transpose(0, 2, 1).reshape(EXPERTS, KF, P, D).swapaxes(1, 2),
        "ctx_feat": w("ctx_2048").reshape(SEQS, P, KD, P).transpose(3, 2, 0, 1),
        "time_decay": _tiles(w("L0_xattn_time_decay")),
        "time_first": _tiles(w("L0_xattn_time_first")),
        "router_w": _tiles(w("L0_ffn_router_w").T),
        "switch_w1": _tiles(w("L0_ffn_w1").T),
        "switch_b1": _tiles(w("L0_ffn_b1")),
        "switch_w2": _tiles(w("L0_ffn_w2").T),
        "switch_b2": w("L0_ffn_b2").reshape(1, D),
        "gla_wq": _tiles(w("L1_attn_Wq").T),
        "gla_wk": _tiles(w("L1_attn_Wk").T),
        "gla_wv": _tiles(w("L1_attn_Wv").T),
        "gla_wg": _tiles(w("L1_attn_Wg").T),
        "gla_wo": _tiles(w("L1_attn_Wo").T),
        "gla_gamma": _tiles(w("L1_attn_gamma")),
        "gla_beta": _tiles(w("L1_attn_beta")),
        "ctx": w("ctx_2048"),
        "ffn_w1": _tiles(w("L1_ffn_W1").T),
        "ffn_w3": _tiles(w("L1_ffn_W3").T),
        "ffn_w2": _tiles(w("L1_ffn_W2").T),
        "hadamard": hadamard(P),
        "A_log": w("L0_attn_A_log"),
        "D": w("L0_attn_D").reshape(CI, 2).T,
    }


def kernel(**inputs):
    import concourse.bacc as bacc
    from concourse.bass_utils import run_bass_kernel_spmd

    nc = bacc.Bacc("TRN2", target_bir_lowering=False, num_devices=1)
    arrays, handles = {}, {}
    for name, a in laid_out(inputs).items():
        a = np.ascontiguousarray(a)
        arrays[f"in_{name}"] = a
        handles[name] = nc.dram_tensor(f"in_{name}", a.shape, mybir.dt.from_np(a.dtype), kind="ExternalInput").ap()
    handles["out"] = nc.dram_tensor("out_x", (SEQS, P, D), F32, kind="ExternalOutput").ap()
    build_program(nc, handles)
    r = run_bass_kernel_spmd(nc, [arrays], core_ids=[0])
    return r.results[0]["out_x"]
```

```python
from contextlib import ExitStack

import numpy as np

import concourse.bass as bass
from concourse import mybir

F32 = mybir.dt.float32
U32 = mybir.dt.uint32
I32 = mybir.dt.int32
ALU = mybir.AluOpType
ACT = mybir.ActivationFunctionType
AX = mybir.AxisListType

P = 128
SEQS, D = 16, 256
KD = D // P
GROUP = 4
GROUPS = SEQS // GROUP
GT = GROUP * P
DI, HEADS, HD, NS = 512, 8, 64, 64
CI = DI // P
TAPS = 4
PAD = TAPS - 1
EXPERTS, FF = 8, 1024
KF = FF // P
TILES = 2 * SEQS + EXPERTS - 1
CAP = 64
BLOCKS = 2 * SEQS
LN_EPS, RMS_EPS = 1e-5, 1e-6


def merge_stats(v, link, stats, mean_var, halves):
    link(v.tensor_tensor(halves[:, 0], stats[:, :, 1], stats[:, :, 4], ALU.add))
    link(v.tensor_tensor(halves[:, 1], stats[:, :, 1], stats[:, :, 4], ALU.subtract))
    link(v.tensor_tensor(halves[:, 2], stats[:, :, 2], stats[:, :, 5], ALU.add))
    link(v.tensor_scalar(mean_var[:, :, 0], halves[:, 0], 0.5, None, ALU.mult))
    link(v.scalar_tensor_tensor(out=halves[:, 3], in0=halves[:, 1], scalar=0.25, in1=halves[:, 1],
                                op0=ALU.mult, op1=ALU.mult))
    link(v.scalar_tensor_tensor(out=mean_var[:, :, 1], in0=halves[:, 2], scalar=1.0 / D, in1=halves[:, 3],
                                op0=ALU.mult, op1=ALU.add))


class Shared:
    pass


class Links:

    def __init__(self, eng, sem, base=0):
        self.eng, self.sem, self.base, self.n = eng, sem, base, 0

    def __call__(self, ins):
        ins.then_inc(self.sem, 1)
        self.n += 1
        self.eng.wait_ge(self.sem, self.base + self.n)


def bc(ap, shape):
    return ap.broadcast_to(shape)


def log1p_terms(n):
    return [1.0 / (2 * k + 1) for k in range(n, 0, -1)]


def mamba_phase(nc, g):
    SS_COL = D
    VEC_STEPS = g.vec_steps_mamba
    with ExitStack() as ctx:
        def sb(name, *shape):
            return ctx.enter_context(nc.sbuf_tensor(name, list(shape), F32))

        def ps(name, *shape):
            return ctx.enter_context(nc.psum_tensor(name, list(shape), F32))

        sem = g.sem
        win = sb("win", P, KD, 2 * DI + 2 * NS + HEADS)
        wout = sb("wout", P, CI, D)
        norm_w = sb("norm_w", P, KD)
        moe_w = g.moe_norm_w
        ssm_w = sb("ssm_w", P, CI)
        conv_w = sb("conv_w", P, CI, TAPS)
        conv_b = sb("conv_b", P, CI)
        convbc_w = sb("convbc_w", NS, 2, TAPS)
        convbc_b = sb("convbc_b", NS, 2)
        dt_bias = sb("dt_bias", P, HEADS)
        a_neg = sb("a_neg", P, HEADS)
        d_skip = sb("d_skip", P, CI)
        stats = sb("stats", P, GROUP, 6)
        mean_var = sb("mean_var", P, GROUP, 2)
        halves = sb("halves", P, 4, GROUP)
        small = sb("small", P, 8, GROUP)
        u_tok = sb("u_tok", P, GROUP, D)
        h_tok = sb("h_tok", P, GROUP, D)
        h_feat = sb("h_feat", P, KD, GT)
        dtw = sb("dtw", P, 6, GROUP * HEADS)
        dt = sb("dt", P, GROUP * HEADS)
        da = sb("da", P, GROUP * HEADS)
        xpad = sb("xpad", P, CI, GROUP, PAD + P)
        bcpad = sb("bcpad", NS, 2, GROUP, PAD + P)
        conv = sb("conv", P, 2, GROUP, P)
        tanh = sb("tanh", P, 2, GT)
        xs_feat = sb("xs_feat", P, CI, GT)
        bc_feat = sb("bc_feat", NS, 2, GT)
        gate = sb("gate", P, CI, GT)
        gate_t = sb("gate_t", P, 2, GT)
        gm = sb("gm", P, 2, P)
        xdt = sb("xdt", P, 2, DI)
        steps_da = sb("steps_da", P, HEADS, P)
        decay = sb("decay", P, 2, HEADS, P)
        y_feat = sb("y_feat", P, CI, P)
        yg = sb("yg", P, 2, CI, P)
        yg2 = sb("yg2", P, 2, CI, P)
        hm = sb("hm", P, 2, D)
        hm_sq = sb("hm_sq", P, D)
        xm_tok = sb("xm_tok", P, 2, D)
        sc = sb("sc", P, 2, 4)

        bank_t = [ps(f"bank_t{k}", P, GT) for k in range(KD)]
        bank_p = [ps(f"bank_p{k}", P, GT) for k in range(2)]
        bank_d = ps("bank_d", P, HEADS, P)
        bank_dt = ps("bank_dt", P, GROUP * HEADS)
        bank_y = ps("bank_y", P, CI, P)

        loaded, consts = sem("m_loaded"), sem("m_consts")
        vec, pool_done = sem("m_vec"), sem("m_pool")
        var_ready, rstd_ready = sem("m_var_ready"), sem("m_rstd_ready")
        u_ready, h_ready = sem("m_u_ready"), sem("m_h_ready")
        hT_ps, hT_ready = sem("m_hT_ps"), sem("m_hT_ready")
        dt_ps, dt_abs, dt_exp, dt_ready = sem("m_dt_ps"), sem("m_dt_abs"), sem("m_dt_exp"), sem("m_dt_ready")
        proj_ps, proj_used_a, proj_used_v = sem("m_proj_ps"), sem("m_proj_used_a"), sem("m_proj_used_v")
        pad_ready, conv_ready, ctanh_ready, feat_ready = (
            sem("m_pad_ready"), sem("m_conv_ready"), sem("m_ctanh_ready"), sem("m_feat_ready"))
        ztanh_ready, gate_ready = sem("m_ztanh_ready"), sem("m_gate_ready")
        g_ps, gm_ready = sem("m_g_ps"), sem("m_gm_ready")
        xsT_ps, xdt_ready = sem("m_xsT_ps"), sem("m_xdt_ready")
        steps_ready, d_ps, decay_ready, mix_ready = (
            sem("m_steps_ready"), sem("m_d_ps"), sem("m_decay_ready"), sem("m_mix_ready"))
        y_ps, yg_ready, yg2_ready, out_ps = sem("m_y_ps"), sem("m_yg_ready"), sem("m_yg2_ready"), sem("m_out_ps")
        ms_ready, r_ready, hm_ready, hms_ready = (
            sem("m_ms_ready"), sem("m_r_ready"), sem("m_hm_ready"), sem("m_hms_ready"))
        xm_ready, xmT_ps, xmT_used, x_added = (
            sem("m_xm_ready"), sem("m_xmT_ps"), sem("m_xmT_used"), sem("m_x_added"))

        NPROJ = 2 + CI + CI

        def slots(a, b, c, d):
            for s in range(GROUP + 3):
                for stage, late in ((a, 0), (b, 1), (c, 2), (d, 3)):
                    if 0 <= s - late < GROUP:
                        stage(s - late)

        block = ctx.enter_context(nc.Block())

        @block.sync
        def _(sp):
            def load(dst, src):
                sp.dma_start(dst, src).then_inc(loaded, 16)
            for n in range(GROUPS):
                q = slice(GROUP * n, GROUP * n + GROUP)
                sp.dma_start(g.X[:, q, :], g.dram["x"].rearrange("b t d -> t b d")[:, q, :]).then_inc(g.x_loaded, 16)
            load(norm_w[:], g.dram["norm_mamba_w"])
            load(win[:], g.dram["in_proj_w"])
            load(conv_w[:], g.dram["conv_w_inner"])
            load(conv_b[:], g.dram["conv_b_inner"])
            load(convbc_w[:], g.dram["conv_w_bc"])
            load(convbc_b[:], g.dram["conv_b_bc"])
            load(dt_bias[:], g.dram["dt_bias"].partition_broadcast(P))
            load(a_neg[:], g.dram["A_log"].partition_broadcast(P))
            for h in range(2):
                load(d_skip[HD * h:HD * h + HD, :], g.dram["D"][h].partition_broadcast(HD))
            load(wout[:], g.dram["out_proj_w"])
            load(ssm_w[:], g.dram["ssm_norm_w"])
            load(moe_w[:], g.dram["norm_moe_w"])
            sp.wait_ge(g.zeroed, 1)
            sp.dma_start(g.slot_in.rearrange("(t p) d -> p t d", p=P), bc(g.zeros[:].unsqueeze(1), [P, TILES + 1, D]))\
                .then_inc(g.slots_zero, 16)
            for e in range(EXPERTS - 2):
                sp.dma_start(g.moe_w2[:, e], g.dram["moe_w2"][e]).then_inc(g.w2_loaded, 16)
        LOADS = 16 * 13

        @block.gpsimd
        def _(pool):
            nc.gpsimd.memset(g.ident[:], 0.0).then_inc(pool_done, 1)
            nc.gpsimd.memset(g.upto[:], 1.0).then_inc(pool_done, 1)
            nc.gpsimd.memset(g.after[:], 1.0).then_inc(pool_done, 1)
            nc.gpsimd.memset(g.zeros[:], 0.0).then_inc(g.zeroed, 1)
            nc.gpsimd.memset(g.ones[:], 1.0).then_inc(consts, 1)
            nc.gpsimd.memset(g.neg_half[:], -0.5).then_inc(consts, 1)
            for e in range(EXPERTS):
                nc.gpsimd.memset(g.iota8[:, e:e + 1], float(e))
            nc.gpsimd.memset(xpad[:], 0.0).then_inc(consts, 1)
            nc.gpsimd.memset(bcpad[:], 0.0).then_inc(consts, 1)
            pool.wait_ge(pool_done, 3)
            nc.gpsimd.affine_select(out=g.ident[:], in_=g.ident[:], compare_op=ALU.not_equal, fill=1.0,
                                    base=0, pattern=[[-1, P]], channel_multiplier=1).then_inc(consts, 1)
            nc.gpsimd.affine_select(out=g.upto[:], in_=g.upto[:], compare_op=ALU.is_ge, fill=0.0,
                                    base=0, pattern=[[1, P]], channel_multiplier=-1).then_inc(consts, 1)
            nc.gpsimd.affine_select(out=g.after[:], in_=g.after[:], compare_op=ALU.is_gt, fill=0.0,
                                    base=0, pattern=[[-1, P]], channel_multiplier=1).then_inc(consts, 1)
            pool.wait_ge(consts, 7)
            with pool.Fori(0, GROUPS) as i:
                for n in range(2):
                    pool.wait_ge(var_ready, i * 2 + (n + 1))
                    nc.gpsimd.tensor_tensor(small[:, 2 * n + 1, :], small[:, 2 * n, :], g.neg_half[:, 0:GROUP],
                                            ALU.pow).then_inc(rstd_ready, 1)
                pool.wait_ge(dt_ready, i + 1)

                def a(j):
                    if j:
                        pool.wait_ge(d_ps, i * GROUP + j)
                    nc.gpsimd.tensor_tensor(
                        steps_da[:], bc(da[:, HEADS * j:HEADS * j + HEADS].unsqueeze(2), [P, HEADS, P]),
                        bc(g.upto[:].unsqueeze(1), [P, HEADS, P]), ALU.mult).then_inc(steps_ready, 1)

                def none(j):
                    pass

                def d(j):
                    pool.wait_ge(ms_ready, i * 2 * GROUP + (2 * j + 1))
                    nc.gpsimd.tensor_tensor(sc[:, j % 2, 1:2], sc[:, j % 2, 0:1], g.neg_half[:, 0:1],
                                            ALU.pow).then_inc(r_ready, 1)
                    pool.wait_ge(hm_ready, i * GROUP + (j + 1))
                    nc.gpsimd.tensor_tensor(g.X[:, i * GROUP + j, :], g.X[:, i * GROUP + j, :], hm[:, j % 2, :],
                                            ALU.add).then_inc(x_added, 1)
                    pool.wait_ge(ms_ready, i * 2 * GROUP + (2 * j + 2))
                    nc.gpsimd.tensor_tensor(sc[:, j % 2, 3:4], sc[:, j % 2, 2:3], g.neg_half[:, 0:1],
                                            ALU.pow).then_inc(r_ready, 1)
                    pool.wait_ge(xm_ready, i * GROUP + (j + 1))
                    nc.gpsimd.tensor_copy(g.xm_tok[:, i * GROUP + j, :], xm_tok[:, j % 2, :]).then_inc(x_added, 1)
                slots(a, none, none, d)

        @block.tensor
        def _(pe):
            pe.wait_ge(consts, 7)
            pe.wait_ge(loaded, LOADS)
            pe.wait_ge(vec, 3)
            with pe.Fori(0, GROUPS) as i:
                for j in range(GROUP):
                    pe.wait_ge(h_ready, i * GROUP + (j + 1))
                    for k in range(KD):
                        last = nc.tensor.transpose(bank_t[k][:, P * j:P * j + P], h_tok[:, j, P * k:P * k + P],
                                                   g.ident[:])
                last.then_inc(hT_ps, 1)
                pe.wait_ge(hT_ready, i * KD + KD)
                for j in range(GROUP):
                    for k in range(KD):
                        last = nc.tensor.matmul(bank_dt[:, HEADS * j:HEADS * j + HEADS],
                                                h_feat[:, k, P * j:P * j + P], win[:, k, 2 * DI + 2 * NS:],
                                                start=(k == 0), stop=(k == KD - 1))
                last.then_inc(dt_ps, 1)
                for n in range(NPROJ):
                    if n >= 2:
                        if n - 2 < 2 + CI:
                            pe.wait_ge(proj_used_a, i * (2 + CI) + (n - 1))
                        else:
                            pe.wait_ge(proj_used_v, i * CI + (n - 2 - (2 + CI) + 1))
                    if n < 2:
                        cols = slice(2 * DI + NS * n, 2 * DI + NS * n + NS)
                    elif n < 2 + CI:
                        cols = slice(DI + P * (n - 2), DI + P * (n - 2) + P)
                    else:
                        cols = slice(P * (n - 2 - CI), P * (n - 2 - CI) + P)
                    out = bank_p[n % 2][0:NS, :] if n < 2 else bank_p[n % 2][:]
                    for k in range(KD):
                        last = nc.tensor.matmul(out, win[:, k, cols], h_feat[:, k, :], start=(k == 0),
                                                stop=(k == KD - 1))
                    last.then_inc(proj_ps, 1)

                def a(j):
                    if j == 0:
                        pe.wait_ge(feat_ready, i * (2 + CI) + 2)
                        pe.wait_ge(proj_used_v, i * CI + CI)
                        pe.wait_ge(dt_ready, i + 1)
                    else:
                        pe.wait_ge(gm_ready, i * GROUP + j)
                    tok = slice(P * j, P * j + P)
                    nc.tensor.matmul(bank_p[0][:, 0:P], bc_feat[:, 0, tok], bc_feat[:, 1, tok],
                                     start=True, stop=True).then_inc(g_ps, 1)
                    if j == 0:
                        pe.wait_ge(feat_ready, i * (2 + CI) + 2 + CI)
                    else:
                        pe.wait_ge(xdt_ready, i * GROUP + j)
                    for c in range(CI):
                        last = nc.tensor.transpose(bank_t[0][:, P * c:P * c + P], xs_feat[:, c, tok], g.ident[:])
                    last.then_inc(xsT_ps, 1)
                    pe.wait_ge(steps_ready, i * GROUP + (j + 1))
                    if j:
                        pe.wait_ge(decay_ready, i * GROUP + j)
                    for n in range(2):
                        hs = slice(HEADS // 2 * n, HEADS // 2 * (n + 1))
                        last = nc.tensor.matmul(bank_d[:, hs, :], g.after[:], steps_da[:, hs, :], start=True, stop=True)
                    last.then_inc(d_ps, 1)

                def b(j):
                    pe.wait_ge(mix_ready, i * GROUP + (j + 1))
                    pe.wait_ge(xdt_ready, i * GROUP + (j + 1))
                    if j:
                        pe.wait_ge(yg_ready, i * GROUP + j)
                    for h in range(HEADS):
                        last = nc.tensor.matmul(bank_y[HD * (h % 2):HD * (h % 2) + HD, h // 2, :],
                                                xdt[:, j % 2, HD * h:HD * h + HD], decay[:, j % 2, h, :],
                                                start=True, stop=True)
                    last.then_inc(y_ps, 1)

                def c(j):
                    pe.wait_ge(yg2_ready, i * GROUP + (j + 1))
                    if j:
                        pe.wait_ge(hm_ready, i * GROUP + j)
                    for c in range(CI):
                        nc.tensor.matmul(bank_t[1][:, SS_COL:SS_COL + 1], yg2[:, j % 2, c, :], g.ones[:, 0:1],
                                         start=(c == 0), stop=(c == CI - 1))
                    for c in range(CI):
                        last = nc.tensor.matmul(bank_t[1][:, 0:D], yg[:, j % 2, c, :], wout[:, c, :],
                                                start=(c == 0), stop=(c == CI - 1))
                    last.then_inc(out_ps, 1)

                def d(j):
                    pe.wait_ge(xm_ready, i * GROUP + (j + 1))
                    if j:
                        pe.wait_ge(xmT_used, i * GROUP + j)
                    for k in range(KD):
                        last = nc.tensor.transpose(bank_p[1][:, P * k:P * k + P],
                                                   xm_tok[:, j % 2, P * k:P * k + P], g.ident[:])
                    last.then_inc(xmT_ps, 1)
                slots(a, b, c, d)
                pe.wait_ge(xmT_used, i * GROUP + GROUP)

        @block.scalar
        def _(act):
            act.wait_ge(loaded, LOADS)
            act.wait_ge(vec, 1)
            nc.scalar.activation(a_neg[:], a_neg[:], ACT.Exp).then_inc(g.a_exp, 1)
            with act.Fori(0, GROUPS) as i:
                act.wait_ge(rstd_ready, i * 2 + 2)
                for j in range(GROUP):
                    act.wait_ge(u_ready, i * GROUP + (j + 1))
                    nc.scalar.activation(h_tok[:, j, :], u_tok[:, j, :], ACT.Copy,
                                         scale=small[:, 3, j:j + 1]).then_inc(h_ready, 1)
                act.wait_ge(hT_ps, i + 1)
                for k in range(KD):
                    nc.scalar.activation(h_feat[:, k, :], bank_t[k][:], ACT.Copy,
                                         scale=norm_w[:, k:k + 1]).then_inc(hT_ready, 1)
                act.wait_ge(dt_abs, i + 1)
                nc.scalar.activation(dtw[:, 2, :], dtw[:, 1, :], ACT.Exp, scale=-1.0).then_inc(dt_exp, 1)

                def conv_tanh(n):
                    act.wait_ge(conv_ready, i * (2 + CI) + (n + 1))
                    rows = NS if n < 2 else P
                    nc.scalar.activation(tanh[0:rows, n % 2, :], conv[0:rows, n % 2, :, :].rearrange("p a b -> p (a b)"),
                                         ACT.Tanh, scale=0.5).then_inc(ctanh_ready, 1)
                for n in range(2 + CI):
                    act.wait_ge(proj_ps, i * NPROJ + (n + 1))
                    dst = bcpad[:, n, :, PAD:] if n < 2 else xpad[:, n - 2, :, PAD:]
                    src = bank_p[n % 2][0:NS, :] if n < 2 else bank_p[n % 2][:]
                    nc.scalar.activation(dst, src.rearrange("p (a b) -> p a b", a=GROUP), ACT.Copy)\
                        .then_inc(proj_used_a, 1)
                    if n >= 1:
                        conv_tanh(n - 1)
                for c in range(CI):
                    n = 2 + CI + c
                    act.wait_ge(proj_ps, i * NPROJ + (n + 1))
                    nc.scalar.activation(gate_t[:, c % 2, :], bank_p[n % 2][:], ACT.Tanh, scale=0.5)\
                        .then_inc(ztanh_ready, 1)
                    if c == 0:
                        conv_tanh(1 + CI)

                def a(j):
                    act.wait_ge(d_ps, i * GROUP + (j + 1))
                    nc.scalar.activation(decay[:, j % 2, :, :], bank_d[:], ACT.Exp).then_inc(decay_ready, 1)

                def none(j):
                    pass

                def c(j):
                    act.wait_ge(yg_ready, i * GROUP + (j + 1))
                    nc.scalar.activation(yg2[:, j % 2, :, :], yg[:, j % 2, :, :], ACT.Square).then_inc(yg2_ready, 1)

                def d(j):
                    act.wait_ge(hm_ready, i * GROUP + (j + 1))
                    nc.scalar.activation(hm_sq[:], hm[:, j % 2, :], ACT.Square,
                                         accum_out=sc[:, j % 2, 2:3]).then_inc(hms_ready, 1)
                    act.wait_ge(xmT_ps, i * GROUP + (j + 1))
                    for k in range(KD):
                        last = nc.scalar.activation(g.xm_feat[:, k, bass.ds(i * GT + P * j, P)],
                                                    bank_p[1][:, P * k:P * k + P], ACT.Copy,
                                                    scale=moe_w[:, k:k + 1])
                    last.then_inc(xmT_used, 1)
                slots(a, none, c, d)

        @block.vector
        def _(dve):
            v = nc.vector
            dve.wait_ge(loaded, LOADS)
            v.tensor_scalar(a_neg[:], a_neg[:], 80.0, None, ALU.min).then_inc(vec, 1)
            dve.wait_ge(g.a_exp, 1)
            v.tensor_scalar(a_neg[:], a_neg[:], -1.0, None, ALU.mult).then_inc(vec, 1)
            v.tensor_tensor(wout[:], wout[:], bc(ssm_w[:].unsqueeze(2), [P, CI, D]), ALU.mult).then_inc(vec, 1)
            dve.wait_ge(vec, 3)
            dve.wait_ge(consts, 7)
            with dve.Fori(0, GROUPS) as i:
                link = Links(dve, vec, i * VEC_STEPS + 3)
                dve.wait_ge(g.x_loaded, i * 16 + 16)
                for j in range(GROUP):
                    ins = v.bn_stats(stats[:, j, :], g.X[:, i * GROUP + j, :])
                link(ins)
                merge_stats(v, link, stats[:], mean_var, halves)
                v.tensor_scalar(small[:, 0, :], mean_var[:, :, 1], LN_EPS, None, ALU.add).then_inc(var_ready, 1)
                dve.wait_ge(rstd_ready, i * 2 + 1)
                link(v.tensor_tensor(small[:, 4, :], mean_var[:, :, 1], small[:, 1, :], ALU.mult))
                link(v.tensor_tensor(small[:, 5, :], small[:, 4, :], small[:, 1, :], ALU.mult))
                v.tensor_scalar(small[:, 2, :], small[:, 5, :], RMS_EPS, None, ALU.add).then_inc(var_ready, 1)
                for j in range(GROUP):
                    v.tensor_scalar(u_tok[:, j, :], g.X[:, i * GROUP + j, :], mean_var[:, j, 0:1],
                                    small[:, 1, j:j + 1], ALU.subtract, ALU.mult).then_inc(u_ready, 1)
                dve.wait_ge(dt_ps, i + 1)
                link(v.tensor_tensor(dtw[:, 0, :].rearrange("p (j h) -> p j h", j=GROUP),
                                     bank_dt[:].rearrange("p (j h) -> p j h", j=GROUP),
                                     bc(dt_bias[:].unsqueeze(1), [P, GROUP, HEADS]), ALU.add))
                v.scalar_tensor_tensor(out=dtw[:, 1, :], in0=dtw[:, 0, :], scalar=-1.0, in1=dtw[:, 0, :],
                                       op0=ALU.mult, op1=ALU.max).then_inc(dt_abs, 1)
                dve.wait_ge(dt_exp, i + 1)
                link(v.tensor_scalar(dtw[:, 3, :], dtw[:, 2, :], 2.0, None, ALU.add))
                link(v.reciprocal(dtw[:, 4, :], dtw[:, 3, :]))
                link(v.tensor_tensor(dtw[:, 3, :], dtw[:, 2, :], dtw[:, 4, :], ALU.mult))
                link(v.tensor_tensor(dtw[:, 4, :], dtw[:, 3, :], dtw[:, 3, :], ALU.mult))
                terms = log1p_terms(8)
                link(v.tensor_scalar(dtw[:, 5, :], dtw[:, 4, :], terms[0], None, ALU.mult))
                for c in terms[1:]:
                    link(v.scalar_tensor_tensor(out=dtw[:, 5, :], in0=dtw[:, 5, :], scalar=c, in1=dtw[:, 4, :],
                                                op0=ALU.add, op1=ALU.mult))
                link(v.scalar_tensor_tensor(out=dtw[:, 5, :], in0=dtw[:, 5, :], scalar=1.0, in1=dtw[:, 3, :],
                                            op0=ALU.add, op1=ALU.mult))
                link(v.tensor_scalar(dtw[:, 3, :], dtw[:, 0, :], 0.0, 0.5, ALU.max, ALU.mult))
                link(v.tensor_tensor(dtw[:, 4, :], dtw[:, 3, :], dtw[:, 5, :], ALU.add))
                link(v.tensor_scalar(dt[:], dtw[:, 4, :], 2.0, None, ALU.mult))
                link(v.tensor_tensor(dtw[:, 3, :].rearrange("p (j h) -> p j h", j=GROUP),
                                     dt[:].rearrange("p (j h) -> p j h", j=GROUP),
                                     bc(a_neg[:].unsqueeze(1), [P, GROUP, HEADS]), ALU.mult))
                v.tensor_scalar(da[:], dtw[:, 3, :], -1e30, None, ALU.max).then_inc(dt_ready, 1)

                def taps(n):
                    dve.wait_ge(proj_used_a, i * (2 + CI) + (n + 1))
                    if n < 2:
                        src, w, b, out = bcpad[:, n], convbc_w[:, n], convbc_b[:, n:n + 1], conv[0:NS, n % 2]
                    else:
                        src, w, b, out = xpad[:, n - 2], conv_w[:, n - 2], conv_b[:, n - 2:n - 1], conv[:, n % 2]
                    link(v.tensor_scalar(out, src[:, :, 0:P], w[:, 0:1], b, ALU.mult, ALU.add))
                    for k in range(1, TAPS):
                        ins = v.scalar_tensor_tensor(out=out, in0=src[:, :, k:k + P], scalar=w[:, k:k + 1], in1=out,
                                                     op0=ALU.mult, op1=ALU.add)
                        if k < TAPS - 1:
                            link(ins)
                        else:
                            ins.then_inc(conv_ready, 1)

                def silu(n):
                    dve.wait_ge(ctanh_ready, i * (2 + CI) + (n + 1))
                    rows = NS if n < 2 else P
                    out = bc_feat[:, n, :] if n < 2 else xs_feat[:, n - 2, :]
                    link(v.scalar_tensor_tensor(out=tanh[0:rows, n % 2, :], in0=tanh[0:rows, n % 2, :], scalar=1.0,
                                                in1=conv[0:rows, n % 2, :, :].rearrange("p a b -> p (a b)"),
                                                op0=ALU.add, op1=ALU.mult))
                    v.tensor_scalar(out, tanh[0:rows, n % 2, :], 0.5, None, ALU.mult).then_inc(feat_ready, 1)
                for n in range(2 + CI):
                    taps(n)
                    if n >= 1:
                        silu(n - 1)
                for c in range(CI):
                    n = 2 + CI + c
                    dve.wait_ge(ztanh_ready, i * CI + (c + 1))
                    v.scalar_tensor_tensor(out=gate[:, c, :], in0=gate_t[:, c % 2, :], scalar=1.0,
                                           in1=bank_p[n % 2][:], op0=ALU.add, op1=ALU.mult).then_inc(proj_used_v, 1)
                    if c == 0:
                        silu(1 + CI)

                def a(j):
                    dve.wait_ge(g_ps, i * GROUP + (j + 1))
                    v.tensor_tensor(gm[:, j % 2, :], bank_p[0][:, 0:P], g.upto[:], ALU.mult)\
                        .then_inc(gm_ready, 1)
                    dve.wait_ge(xsT_ps, i * GROUP + (j + 1))
                    v.tensor_tensor(xdt[:, j % 2, :].rearrange("p (h d) -> p h d", h=HEADS),
                                    bank_t[0][:].rearrange("p (h d) -> p h d", h=HEADS),
                                    bc(dt[:, HEADS * j:HEADS * j + HEADS].unsqueeze(2), [P, HEADS, HD]), ALU.mult)\
                        .then_inc(xdt_ready, 1)

                def b(j):
                    dve.wait_ge(gm_ready, i * GROUP + (j + 1))
                    dve.wait_ge(decay_ready, i * GROUP + (j + 1))
                    v.tensor_tensor(decay[:, j % 2, :, :], decay[:, j % 2, :, :],
                                    bc(gm[:, j % 2, :].unsqueeze(1), [P, HEADS, P]), ALU.mult).then_inc(mix_ready, 1)

                def c(j):
                    tok = slice(P * j, P * j + P)
                    dve.wait_ge(y_ps, i * GROUP + (j + 1))
                    for c in range(CI):
                        ins = v.scalar_tensor_tensor(out=y_feat[:, c, :], in0=xs_feat[:, c, tok],
                                                     scalar=d_skip[:, c:c + 1], in1=bank_y[:, c, :],
                                                     op0=ALU.mult, op1=ALU.add)
                    link(ins)
                    v.scalar_tensor_tensor(out=yg[:, j % 2, :, :], in0=y_feat[:], scalar=0.5, in1=gate[:, :, tok],
                                           op0=ALU.mult, op1=ALU.mult).then_inc(yg_ready, 1)

                def d(j):
                    dve.wait_ge(out_ps, i * GROUP + (j + 1))
                    v.tensor_scalar(sc[:, j % 2, 0:1], bank_t[1][:, SS_COL:SS_COL + 1], 1.0 / DI, RMS_EPS,
                                    ALU.mult, ALU.add).then_inc(ms_ready, 1)
                    dve.wait_ge(r_ready, i * 2 * GROUP + (2 * j + 1))
                    v.scalar_tensor_tensor(out=hm[:, j % 2, :], in0=bank_t[1][:, 0:D], scalar=sc[:, j % 2, 1:2],
                                           in1=u_tok[:, j, :], op0=ALU.mult, op1=ALU.add).then_inc(hm_ready, 1)
                    dve.wait_ge(hms_ready, i * GROUP + (j + 1))
                    v.tensor_scalar(sc[:, j % 2, 2:3], sc[:, j % 2, 2:3], 1.0 / D, RMS_EPS, ALU.mult, ALU.add)\
                        .then_inc(ms_ready, 1)
                    dve.wait_ge(r_ready, i * 2 * GROUP + (2 * j + 2))
                    v.tensor_scalar(xm_tok[:, j % 2, :], hm[:, j % 2, :], sc[:, j % 2, 3:4], None, ALU.mult)\
                        .then_inc(xm_ready, 1)
                slots(a, b, c, d)
                assert link.n == VEC_STEPS, link.n


def route_pe(nc, pe, g, r):
    pe.wait_ge(r.loaded, r.loads)
    for n in range(GROUPS):
        if n >= 2:
            pe.wait_ge(r.logits_used, n - 1)
        for k in range(KD):
            last = nc.tensor.matmul(r.bank_l[n % 2][0:EXPERTS, :], r.gate_w[:, k, :],
                                    g.xm_feat[:, k, GT * n:GT * n + GT], start=(k == 0), stop=(k == KD - 1))
        last.then_inc(r.logits_ps, 1)
    pe.wait_ge(r.logits_used, GROUPS)
    for q in range(SEQS):
        last = nc.tensor.transpose(r.bank_lt[:, q, :], r.logits_e[:, P * q:P * q + P], g.ident[0:EXPERTS, 0:EXPERTS])
    last.then_inc(r.logits_t, 1)


def route_act(nc, act, g, r, full):
    for n in range(GROUPS):
        act.wait_ge(r.logits_ps, n + 1)
        nc.scalar.copy(r.logits_e[:, GT * n:GT * n + GT], r.bank_l[n % 2][0:EXPERTS, :]).then_inc(r.logits_used, 1)
    act.wait_ge(r.second_less_first, 1)
    nc.scalar.activation(r.work[:, 1, :], r.work[:, 0, :], ACT.Exp).then_inc(r.exps, 1)
    if full:
        nc.scalar.activation(r.all_exp[:], r.logits[:], ACT.Exp).then_inc(r.exps, 1)


def route_dve(nc, dve, g, r, link, full):
    v = nc.vector
    dve.wait_ge(r.logits_t, 1)
    link(v.tensor_copy(r.logits[:], r.bank_lt[:]))
    for q in range(SEQS):
        ins = v.max(r.top[:, q, :], r.logits[:, q, :])
    link(ins)
    for q in range(SEQS):
        ins = v.max_index(r.top_at[:, q, :], r.top[:, q, :], r.logits[:, q, :])
    link(ins)
    link(v.tensor_copy(r.at[:], r.top_at[:, :, 0:2]))
    for n in range(2):
        link(v.tensor_tensor(r.hot[:, n], bc(r.at[:, :, n:n + 1], [P, SEQS, EXPERTS]),
                             bc(g.iota8[:].unsqueeze(1), [P, SEQS, EXPERTS]), ALU.is_equal))
    if full:
        link(v.tensor_tensor(r.logits[:], r.logits[:], bc(r.top[:, :, 0:1], [P, SEQS, EXPERTS]), ALU.subtract))
    v.tensor_tensor(r.work[:, 0, :], r.top[:, :, 1], r.top[:, :, 0], ALU.subtract).then_inc(r.second_less_first, 1)
    dve.wait_ge(r.exps, 2 if full else 1)
    if full:
        link(v.tensor_reduce(r.work[:, 2, :], r.all_exp[:], AX.X, ALU.add))
    else:
        link(v.tensor_scalar(r.work[:, 2, :], r.work[:, 1, :], 1.0, None, ALU.add))
    link(v.reciprocal(r.prob[:, 0, :], r.work[:, 2, :]))
    link(v.tensor_tensor(r.prob[:, 1, :], r.prob[:, 0, :], r.work[:, 1, :], ALU.mult))


def count_buffers(ctx, nc, g, r, tag):
    def sb(name, *shape):
        return ctx.enter_context(nc.sbuf_tensor(tag + name, list(shape), F32))
    r.before = sb("before", P, P)
    r.counts, r.carry, r.offset = (sb(name, P, EXPERTS, BLOCKS + 1) for name in ("counts", "carry", "offset"))
    r.slot = sb("slot", P, BLOCKS, EXPERTS)
    r.bank_c = ctx.enter_context(nc.psum_tensor(tag + "bank_c", [P, 2, BLOCKS * EXPERTS], F32))
    r.count_consts, r.hot_ready, r.counts_ps = g.sem(tag + "count_consts"), g.sem(tag + "hot_ready"), g.sem(tag + "counts_ps")


def count_pool(nc, pool, g, r):
    nc.gpsimd.memset(r.counts[:], 0.0).then_inc(r.count_consts, 1)
    nc.gpsimd.memset(r.carry[:], 1.0).then_inc(r.count_consts, 1)
    pool.wait_ge(r.count_consts, 2)
    nc.gpsimd.memset(r.carry[:, :, 0:1], 0.0).then_inc(r.count_consts, 1)
    nc.gpsimd.tensor_tensor(r.before[:], g.upto[:], g.ident[:], ALU.subtract).then_inc(r.count_consts, 1)


def count_pe(nc, pe, g, r):
    pe.wait_ge(r.count_consts, 4)
    pe.wait_ge(r.hot_ready, 1)
    hot = r.hot[:].rearrange("p n q e -> p (n q e)")
    nc.tensor.matmul(r.bank_c[:, 0, :], r.before[:], hot, start=True, stop=True)
    nc.tensor.matmul(r.bank_c[:, 1, :], g.ones[:], hot, start=True, stop=True).then_inc(r.counts_ps, 1)


def count_dve(nc, dve, g, r, link):
    v = nc.vector
    dve.sem_inc(r.hot_ready, 1)
    dve.wait_ge(r.counts_ps, 1)
    dve.wait_ge(r.count_consts, 4)
    link(v.tensor_copy(r.counts[:, :, 1:], r.bank_c[:, 1, :].rearrange("p (n e) -> p e n", e=EXPERTS)))
    link(v.tensor_tensor_scan(r.offset[:].rearrange("p e n -> p (e n)"), r.carry[:].rearrange("p e n -> p (e n)"),
                              r.counts[:].rearrange("p e n -> p (e n)"), 0.0, ALU.mult, ALU.add))
    link(v.tensor_tensor(r.slot[:], r.bank_c[:, 0, :].rearrange("p (n e) -> p n e", e=EXPERTS),
                         r.offset[:, :, 0:BLOCKS].rearrange("p e n -> p n e"), ALU.add))


def route_buffers(ctx, nc, g, tag):
    def sb(name, *shape, dt=F32):
        return ctx.enter_context(nc.sbuf_tensor(tag + name, list(shape), dt))
    r = Shared()
    r.gate_w = sb("gate_w", P, KD, EXPERTS)
    r.logits, r.all_exp = sb("logits", P, SEQS, EXPERTS), sb("all_exp", P, SEQS, EXPERTS)
    r.top, r.top_at, r.at = sb("top", P, SEQS, 8), sb("top_at", P, SEQS, 8, dt=U32), sb("at", P, SEQS, 2)
    r.hot = sb("hot", P, 2, SEQS, EXPERTS)
    r.work, r.prob = sb("work", P, 3, SEQS), sb("prob", P, 2, SEQS)
    r.logits_ps, r.logits_used, r.logits_t = g.sem(tag + "logits_ps"), g.sem(tag + "logits_used"), g.sem(tag + "logits_t")
    r.second_less_first, r.exps, r.link = g.sem(tag + "second_less_first"), g.sem(tag + "exps"), g.sem(tag + "link")
    return r


def moe_phase(nc, g):
    ROUND = float(1 << 23)
    with ExitStack() as ctx:
        def sb(name, *shape, dt=F32):
            return ctx.enter_context(nc.sbuf_tensor("e_" + name, list(shape), dt))

        def ps(name, *shape):
            return ctx.enter_context(nc.psum_tensor("e_" + name, list(shape), F32))

        sem = lambda name: g.sem("e_" + name)
        r = route_buffers(ctx, nc, g, "e_")
        w1 = sb("w1", P, EXPERTS, KD, FF)
        w2 = g.moe_w2
        x_tok, x_feat = sb("x_tok", P, 2, D), sb("x_feat", P, 2, KD, P)
        tanh = sb("tanh", P, 2, FF // 2)
        work = sb("rows", P, 2, FF)
        h_tok, h_feat = work[:, 0, :], work[:, 1, :].rearrange("p (f t) -> p f t", f=KF)
        back = work[:].rearrange("p a (b d) -> p (a b) d", d=D)
        BACK = 2 * FF // D
        r.logits_e = work[0:EXPERTS].rearrange("p a b -> p (a b)")
        y_tok = sb("y_tok", P, 2, D)
        fill = sb("fill", P, 6, EXPERTS)
        tile_iota, tile_cmp = sb("tile_iota", P, TILES), sb("tile_cmp", P, TILES, EXPERTS)
        tile_expert = sb("tile_expert", P, TILES, dt=I32)
        dest = sb("dest", P, BLOCKS)
        dest_at = sb("dest_at", P, BLOCKS, dt=U32)
        bank_x = ps("bank_x", P, KD, P)
        bank_u = [ps(f"bank_u{n}", P, FF // 2) for n in range(2)]
        bank_h = [ps(f"bank_h{n}", P, KF // 2, P) for n in range(2)]
        bank_o = ps("bank_o", P, D)
        count_buffers(ctx, nc, g, r, "e_")
        r.bank_l = bank_u
        r.bank_lt = ps("bank_lt", P, SEQS, EXPERTS)
        r.loaded, r.loads = sem("gate_loaded"), 16
        w1_loaded, iota_ready, table_ready, scattered = sem("w1_loaded"), sem("iota_ready"), sem("table_ready"), sem("scattered")
        x_loaded = [sem("x_loaded0"), sem("x_loaded1")]
        xT_ps, x_ready, u_ps, tanh_ready, h_ready = sem("xT_ps"), sem("x_ready"), sem("u_ps"), sem("tanh_ready"), sem("h_ready")
        hT_ps, hT_ready_a, hT_ready_v, o_ps = sem("hT_ps"), sem("hT_ready_a"), sem("hT_ready_v"), sem("o_ps")
        y_ready, stored = sem("y_ready"), [sem("stored0"), sem("stored1")]
        gathered, added = [sem(f"gathered{n}") for n in range(BACK)], sem("added")
        PAIRS = (TILES - 1) // 2
        assert TILES == 2 * PAIRS + 1
        block = ctx.enter_context(nc.Block())

        def steps(eng, step):
            step(0, 0, True, False)
            with eng.Fori(0, PAIRS) as m:
                for b in range(2):
                    step(m * 2 + (b + 1), (b + 1) % 2, False, False)
            step(TILES, TILES % 2, False, True)

        @block.sync
        def _(sp):
            sp.dma_start(r.gate_w[:], g.dram["gate_w"]).then_inc(r.loaded, 16)
            for e in range(EXPERTS):
                sp.dma_start(w1[:, e], g.dram["moe_w1"][e]).then_inc(w1_loaded, 16)
            sp.wait_ge(r.logits_ps, GROUPS)
            for e in range(EXPERTS - 2, EXPERTS):
                sp.dma_start(w2[:, e], g.dram["moe_w2"][e]).then_inc(g.w2_loaded, 16)
            sp.wait_ge(scattered, 16 * BLOCKS)
            for b in range(2):
                sp.dma_start(x_tok[:, b, :], g.slot_in[P * b:P * b + P, :]).then_inc(x_loaded[b], 16)

            def load(t, b):
                sp.wait_ge(xT_ps, t - 1)
                sp.dma_start(x_tok[:, b, :], g.slot_in[bass.ds(t * P, P), :]).then_inc(x_loaded[b], 16)

            def store(t, b):
                sp.wait_ge(y_ready, t + 2)
                sp.dma_start(g.slot_out[bass.ds(t * P, P), :], y_tok[:, b, :]).then_inc(stored[b], 16)
            load(2, 0)
            with sp.Fori(0, PAIRS - 1) as m:
                for b in range(2):
                    load(m * 2 + (b + 3), (b + 1) % 2)
                    store(m * 2 + b, b)
            load(TILES, TILES % 2)
            for t in range(2 * PAIRS - 2, TILES):
                store(t, t % 2)

        @block.gpsimd
        def _(pool):
            p = nc.gpsimd
            count_pool(nc, pool, g, r)
            for t in range(TILES):
                p.memset(tile_iota[:, t:t + 1], float(t)).then_inc(iota_ready, 1)
            pool.wait_ge(table_ready, 1)
            pool.wait_ge(g.slots_zero, 16)
            for n in range(BLOCKS):
                p.indirect_dma_start(g.slot_in[0:TILES * P, :], bass.IndirectOffsetOnAxis(ap=dest_at[:, n:n + 1], axis=0),
                                     g.xm_tok[:, n % SEQS, :], None).then_inc(scattered, 16)
            pool.wait_ge(stored[0], 16 * ((TILES + 1) // 2) + 16)
            pool.wait_ge(stored[1], 16 * (TILES // 2) + 16)
            pool.wait_ge(o_ps, TILES)
            for n in range(BLOCKS):
                if n >= BACK:
                    pool.wait_ge(added, n - BACK + 1)
                p.indirect_dma_start(back[:, n % BACK, :], None, g.slot_out,
                                     bass.IndirectOffsetOnAxis(ap=dest_at[:, n:n + 1], axis=0))\
                    .then_inc(gathered[n % BACK], 16)

        @block.tensor
        def _(pe):
            route_pe(nc, pe, g, r)
            count_pe(nc, pe, g, r)
            pe.wait_ge(table_ready, 1)
            pe.wait_ge(w1_loaded, 16 * EXPERTS)
            pe.wait_ge(g.w2_loaded, 16 * EXPERTS)

            def turn_x(t, b, loads):
                pe.wait_ge(x_loaded[b], loads)
                for k in range(KD):
                    last = nc.tensor.transpose(bank_x[:, k, :], x_tok[:, b, P * k:P * k + P], g.ident[:])
                last.then_inc(xT_ps, 1)
            turn_x(0, 0, 16)

            def step(s, b, first, last_step):
                if not first:
                    pe.wait_ge(h_ready, s * 2)
                    for f in range(KF):
                        last = nc.tensor.transpose(bank_h[f // (KF // 2)][:, f % (KF // 2), :], h_tok[:, P * f:P * f + P],
                                                   g.ident[:])
                        if f % (KF // 2) == KF // 2 - 1:
                            last.then_inc(hT_ps, 1)
                if not last_step:
                    pe.wait_ge(x_ready, s + 1)
                    e = pe.value_load(tile_expert[0:1, bass.ds(s, 1)], min_val=0, max_val=EXPERTS - 1)
                    for n in range(2):
                        for k in range(KD):
                            last = nc.tensor.matmul(bank_u[n][:], x_feat[:, b, k, :],
                                                    w1[:, bass.ds(e, 1), k, FF // 2 * n:FF // 2 * (n + 1)]
                                                    .rearrange("p a f -> p (a f)"),
                                                    start=(k == 0), stop=(k == KD - 1))
                        last.then_inc(u_ps, 1)
                    turn_x(s + 1, 1 - b, (s + 1) // 2 * 16 + 16 if first else (s + (1 + b) - 1) * 8 + 16)
                if not first:
                    e = pe.value_load(tile_expert[0:1, bass.ds(s - 1, 1)], min_val=0, max_val=EXPERTS - 1)
                    pe.wait_ge(hT_ready_a, s)
                    for f in range(KF):
                        if f == KF // 2:
                            pe.wait_ge(hT_ready_v, s)
                        if f == 0:
                            pe.wait_ge(y_ready, s)
                        last = nc.tensor.matmul(bank_o[:], h_feat[:, f, :],
                                                w2[:, bass.ds(e, 1), f, :].rearrange("p a d -> p (a d)"),
                                                start=(f == 0), stop=(f == KF - 1))
                    last.then_inc(o_ps, 1)
            steps(pe, step)

        @block.scalar
        def _(act):
            route_act(nc, act, g, r, False)

            def x_evac(t, b):
                act.wait_ge(xT_ps, t + 1)
                for k in range(KD):
                    last = nc.scalar.activation(x_feat[:, b, k, :], bank_x[:, k, :], ACT.Copy, scale=g.moe_norm_w[:, k:k + 1])
                last.then_inc(x_ready, 1)
            x_evac(0, 0)

            def step(s, b, first, last_step):
                if not first:
                    act.wait_ge(hT_ps, s * 2 - 1)
                    nc.scalar.copy(h_feat[:, 0:KF // 2, :], bank_h[0][:]).then_inc(hT_ready_a, 1)
                if not last_step:
                    for n in range(2):
                        act.wait_ge(u_ps, s * 2 + (n + 1))
                        nc.scalar.activation(tanh[:, n, :], bank_u[n][:], ACT.Tanh, scale=0.5).then_inc(tanh_ready, 1)
                    x_evac(s + 1, 1 - b)
            steps(act, step)

        @block.vector
        def _(dve):
            v = nc.vector
            link = Links(dve, r.link)
            route_dve(nc, dve, g, r, link, False)
            count_dve(nc, dve, g, r, link)
            number, tiles, end, base, ones = (fill[:, n, :] for n in range(5))
            link(v.tensor_scalar(number, r.offset[:, :, BLOCKS], 1.0 / P, (P - 1) / (2.0 * P), ALU.mult, ALU.add))
            link(v.tensor_scalar(tiles, number, ROUND, None, ALU.add))
            link(v.tensor_scalar(tiles, tiles, ROUND, None, ALU.subtract))
            link(v.memset(ones, 1.0))
            link(v.tensor_tensor_scan(end, ones, tiles, 0.0, ALU.mult, ALU.add))
            link(v.tensor_tensor(base, end, tiles, ALU.subtract))
            link(v.tensor_scalar(base, base, float(P), None, ALU.mult))
            link(v.tensor_tensor(r.slot[:], r.slot[:], bc(base.unsqueeze(1), [P, BLOCKS, EXPERTS]), ALU.add))
            link(v.tensor_tensor(r.slot[:], r.slot[:], r.hot[:].rearrange("p n q e -> p (n q) e"), ALU.mult))
            link(v.tensor_reduce(dest[:], r.slot[:], AX.X, ALU.add))
            link(v.tensor_copy(dest_at[:], dest[:]))
            dve.wait_ge(iota_ready, TILES)
            link(v.tensor_tensor(tile_cmp[:], bc(tile_iota[:].unsqueeze(2), [P, TILES, EXPERTS]),
                                 bc(end.unsqueeze(1), [P, TILES, EXPERTS]), ALU.is_ge))
            link(v.tensor_reduce(tile_iota[:], tile_cmp[:], AX.X, ALU.add))
            link(v.tensor_scalar(tile_iota[:], tile_iota[:], float(EXPERTS - 1), None, ALU.min))
            link(v.tensor_copy(tile_expert[:], tile_iota[:]))
            link(v.tensor_scalar(r.prob[:], r.prob[:], 0.5, None, ALU.mult))
            dve.sem_inc(table_ready, 1)
            dve.sem_inc(y_ready, 1)
            for b in range(2):
                dve.sem_inc(stored[b], 16)

            def step(s, b, first, last_step):
                if not first:
                    dve.wait_ge(hT_ps, s * 2)
                    v.tensor_copy(h_feat[:, KF // 2:, :], bank_h[1][:]).then_inc(hT_ready_v, 1)
                if not last_step:
                    for n in range(2):
                        dve.wait_ge(tanh_ready, s * 2 + (n + 1))
                        v.scalar_tensor_tensor(out=h_tok[:, FF // 2 * n:FF // 2 * (n + 1)], in0=tanh[:, n, :], scalar=1.0,
                                               in1=bank_u[n][:], op0=ALU.add, op1=ALU.mult).then_inc(h_ready, 1)
                if not first:
                    dve.wait_ge(o_ps, s)
                    dve.wait_ge(stored[1 - b], ((s - 1) // 2 * 16 + 16) if last_step else (s - 1 - (1 - b)) * 8 + 16)
                    v.tensor_copy(y_tok[:, 1 - b, :], bank_o[:]).then_inc(y_ready, 1)
            steps(dve, step)
            for n in range(BLOCKS):
                dve.wait_ge(gathered[n % BACK], 16 * (n // BACK + 1))
                if n >= SEQS:
                    dve.wait_ge(added, n - SEQS + 1)
                v.scalar_tensor_tensor(out=g.X[:, n % SEQS, :], in0=back[:, n % BACK, :],
                                       scalar=r.prob[:, n // SEQS, n % SEQS:n % SEQS + 1], in1=g.X[:, n % SEQS, :],
                                       op0=ALU.mult, op1=ALU.add).then_inc(added, 1)


def wkv_phase(nc, g):
    SP1 = P + 1
    with ExitStack() as ctx:
        def sb(name, *shape):
            return ctx.enter_context(nc.sbuf_tensor(name, list(shape), F32))

        def ps(name, *shape):
            return ctx.enter_context(nc.psum_tensor(name, list(shape), F32))

        sem = g.sem
        stats, mean_var, halves = sb("k_stats", P, GROUP, 6), sb("k_mean_var", P, GROUP, 2), sb("k_halves", P, 4, GROUP)
        small = sb("k_small", P, 4, GROUP)
        n_tok = sb("k_n_tok", P, GROUP, D)
        v_feat = sb("k_v_feat", P, 2, KD, GROUP, P)
        time_decay, time_first = sb("k_time_decay", P, KD), sb("k_time_first", P, KD)
        fac = sb("k_fac", P, 4, KD)
        keep = sb("k_keep", P, KD, GROUP, SP1)
        ek, ekv = sb("k_ek", P, KD, GROUP, SP1), sb("k_ekv", P, KD, GROUP, SP1)
        eu, euv = sb("k_eu", P, KD, GT), sb("k_euv", P, KD, GT)
        den_sum, num_sum = sb("k_den_sum", P, KD, GROUP, SP1), sb("k_num_sum", P, KD, GROUP, SP1)
        den, num = sb("k_den", P, KD, GT), sb("k_num", P, KD, GT)
        bank_t = [ps(f"k_bank_t{k}", P, GT) for k in range(KD)]
        bank_y = [ps(f"k_bank_y{j}", P, 2, D) for j in range(2)]
        bank_n = [ps(f"k_bank_n{k}", P, GT) for k in range(KD)]

        loaded, consts, vec = sem("k_loaded"), sem("k_consts"), sem("k_vec")
        v_loaded = [sem("k_v_loaded0"), sem("k_v_loaded1")]
        var_ready, rstd_ready, n_ready = sem("k_var_ready"), sem("k_rstd_ready"), sem("k_n_ready")
        kT_ps, ek_ready, v_used = sem("k_kT_ps"), sem("k_ek_ready"), sem("k_v_used")
        ekv_ready, y_ready, y_ps, added = sem("k_ekv_ready"), sem("k_y_ready"), sem("k_y_ps"), sem("k_added")
        n2_ready, nT_ps, nT_used = sem("k_n2_ready"), sem("k_nT_ps"), sem("k_nT_used")
        VEC_STEPS, PRE = 26, 5
        block = ctx.enter_context(nc.Block())

        @block.sync
        def _(sp):
            sp.dma_start(time_decay[:], g.dram["time_decay"]).then_inc(loaded, 16)
            sp.dma_start(time_first[:], g.dram["time_first"]).then_inc(loaded, 16)
            with sp.Fori(0, GROUPS // 2) as i:
                for b in range(2):
                    sp.wait_ge(v_used, i * 2 + (b + 1))
                    for k in range(KD):
                        sp.dma_start(v_feat[:, b, k], g.dram["ctx_feat"][:, k, bass.ds(i * (2 * GROUP) + b * GROUP, GROUP), :])\
                            .then_inc(v_loaded[b], 16)

        @block.gpsimd
        def _(pool):
            p = nc.gpsimd
            p.memset(keep[:], 0.0).then_inc(consts, 1)
            p.memset(ek[:], 0.0).then_inc(consts, 1)
            p.memset(ekv[:], 0.0).then_inc(consts, 1)
            pool.sem_inc(v_used, 2)
            pool.wait_ge(consts, 3)
            with pool.Fori(0, GROUPS // 2) as m:
                for b in range(2):
                    i = m * 2 + b
                    pool.wait_ge(var_ready, i * 2 + 1)
                    p.tensor_tensor(small[:, 1, :], small[:, 0, :], g.neg_half[:, 0:GROUP], ALU.pow)\
                        .then_inc(rstd_ready, 1)
                    pool.wait_ge(v_loaded[b], m * 32 + 32)
                    for k in range(KD):
                        pool.wait_ge(ek_ready, i * 4 + (2 * k + 1))
                        p.tensor_tensor(ekv[:, k, :, 1:], ek[:, k, :, 1:], v_feat[:, b, k], ALU.mult)\
                            .then_inc(ekv_ready, 1)
                        pool.wait_ge(ek_ready, i * 4 + (2 * k + 2))
                        ins = p.tensor_tensor(euv[:, k, :], eu[:, k, :], v_feat[:, b, k].rearrange("p a b -> p (a b)"),
                                              ALU.mult)
                        ins.then_inc(ekv_ready, 1)
                    pool.wait_ge(ekv_ready, i * 4 + 4)
                    pool.sem_inc(v_used, 1)
                    pool.wait_ge(var_ready, i * 2 + 2)
                    p.tensor_tensor(small[:, 1, :], small[:, 0, :], g.neg_half[:, 0:GROUP], ALU.pow)\
                        .then_inc(rstd_ready, 1)

        @block.tensor
        def _(pe):
            with pe.Fori(0, GROUPS) as i:
                for j in range(GROUP):
                    pe.wait_ge(n_ready, i * GROUP + (j + 1))
                    for k in range(KD):
                        last = nc.tensor.transpose(bank_t[k][:, P * j:P * j + P], n_tok[:, j, P * k:P * k + P], g.ident[:])
                last.then_inc(kT_ps, 1)
                for k in range(KD):
                    pe.wait_ge(y_ready, i * KD + (k + 1))
                    for j in range(GROUP):
                        last = nc.tensor.transpose(bank_y[j // 2][:, j % 2, P * k:P * k + P],
                                                   num[:, k, P * j:P * j + P], g.ident[:])
                last.then_inc(y_ps, 1)
                for j in range(GROUP):
                    pe.wait_ge(n2_ready, i * GROUP + (j + 1))
                    for k in range(KD):
                        last = nc.tensor.transpose(bank_n[k][:, P * j:P * j + P], n_tok[:, j, P * k:P * k + P], g.ident[:])
                last.then_inc(nT_ps, 1)

        @block.scalar
        def _(act):
            act.wait_ge(loaded, 32)
            nc.scalar.activation(fac[:, 1, :], time_decay[:], ACT.Exp).then_inc(vec, 1)
            act.wait_ge(vec, 1)
            nc.scalar.activation(fac[:, 0, :], fac[:, 1, :], ACT.Exp, scale=-1.0).then_inc(vec, 1)
            act.wait_ge(vec, 4)
            nc.scalar.activation(fac[:, 3, :], fac[:, 3, :], ACT.Exp).then_inc(vec, 1)
            act.wait_ge(consts, 3)
            with act.Fori(0, GROUPS) as i:
                act.wait_ge(kT_ps, i + 1)
                for k in range(KD):
                    nc.scalar.activation(ek[:, k, :, 1:], bank_t[k][:].rearrange("p (a b) -> p a b", a=GROUP), ACT.Exp)\
                        .then_inc(ek_ready, 1)
                    nc.scalar.activation(eu[:, k, :], bank_t[k][:], ACT.Exp, bias=fac[:, 2, k:k + 1]).then_inc(ek_ready, 1)
                act.wait_ge(nT_ps, i + 1)
                for k in range(KD):
                    nc.scalar.copy(g.xm_feat[:, k, bass.ds(i * GT, GT)], bank_n[k][:]).then_inc(nT_used, 1)

        @block.vector
        def _(dve):
            v = nc.vector
            dve.wait_ge(loaded, 32)
            dve.wait_ge(vec, 2)
            v.tensor_scalar(fac[:, 2, :], time_first[:], 0.0, None, ALU.min).then_inc(vec, 1)
            v.tensor_scalar(fac[:, 3, :], time_first[:], 0.0, -1.0, ALU.max, ALU.mult).then_inc(vec, 1)
            dve.wait_ge(vec, 5)
            dve.wait_ge(consts, 3)
            for k in range(KD):
                ins = v.tensor_scalar(keep[:, k, :, 1:], keep[:, k, :, 1:], fac[:, 0, k:k + 1], None, ALU.add)
            ins.then_inc(consts, 1)
            dve.wait_ge(consts, 4)

            def layer_norm(link, i, part, ready):
                for j in range(GROUP):
                    ins = v.bn_stats(stats[:, j, :], g.X[:, i * GROUP + j, :])
                link(ins)
                merge_stats(v, link, stats[:], mean_var, halves)
                v.tensor_scalar(small[:, 0, :], mean_var[:, :, 1], LN_EPS, None, ALU.add).then_inc(var_ready, 1)
                dve.wait_ge(rstd_ready, i * 2 + (part + 1))
                for j in range(GROUP):
                    v.tensor_scalar(n_tok[:, j, :], g.X[:, i * GROUP + j, :], mean_var[:, j, 0:1],
                                    small[:, 1, j:j + 1], ALU.subtract, ALU.mult).then_inc(ready, 1)
            with dve.Fori(0, GROUPS) as i:
                link = Links(dve, vec, i * VEC_STEPS + PRE)
                layer_norm(link, i, 0, n_ready)
                for k in range(KD):
                    dve.wait_ge(ek_ready, i * 4 + (2 * k + 1))
                    link(v.tensor_tensor_scan(den_sum[:, k].rearrange("p a b -> p (a b)"),
                                              keep[:, k].rearrange("p a b -> p (a b)"),
                                              ek[:, k].rearrange("p a b -> p (a b)"), 0.0, ALU.mult, ALU.add))
                    dve.wait_ge(ek_ready, i * 4 + (2 * k + 2))
                    link(v.scalar_tensor_tensor(out=den[:, k].rearrange("p (a b) -> p a b", a=GROUP),
                                                in0=den_sum[:, k, :, 0:P], scalar=fac[:, 3, k:k + 1],
                                                in1=eu[:, k].rearrange("p (a b) -> p a b", a=GROUP),
                                                op0=ALU.mult, op1=ALU.add))
                    link(v.reciprocal(den[:, k], den[:, k]))
                    dve.wait_ge(ekv_ready, i * 4 + (2 * k + 1))
                    link(v.tensor_tensor_scan(num_sum[:, k].rearrange("p a b -> p (a b)"),
                                              keep[:, k].rearrange("p a b -> p (a b)"),
                                              ekv[:, k].rearrange("p a b -> p (a b)"), 0.0, ALU.mult, ALU.add))
                    dve.wait_ge(ekv_ready, i * 4 + (2 * k + 2))
                    link(v.scalar_tensor_tensor(out=num[:, k].rearrange("p (a b) -> p a b", a=GROUP),
                                                in0=num_sum[:, k, :, 0:P], scalar=fac[:, 3, k:k + 1],
                                                in1=euv[:, k].rearrange("p (a b) -> p a b", a=GROUP),
                                                op0=ALU.mult, op1=ALU.add))
                    v.tensor_tensor(num[:, k], num[:, k], den[:, k], ALU.mult).then_inc(y_ready, 1)
                dve.wait_ge(y_ps, i + 1)
                for h in range(2):
                    seqs = bass.ds(i * GROUP + 2 * h, 2)
                    link(v.tensor_tensor(g.X[:, seqs, :], g.X[:, seqs, :], bank_y[h][:], ALU.add))
                v.memset(small[:, 3, :], 0.0)
                layer_norm(link, i, 1, n2_ready)
                dve.wait_ge(nT_used, i * KD + KD)
                assert link.n == VEC_STEPS, link.n


def switch_phase(nc, g):
    UP_BANKS, OUT_BANKS = 4, 2
    with ExitStack() as ctx:
        def sb(name, *shape):
            return ctx.enter_context(nc.sbuf_tensor(name, list(shape), F32))

        def ps(name, *shape):
            return ctx.enter_context(nc.psum_tensor(name, list(shape), F32))

        sem = g.sem
        r = route_buffers(ctx, nc, g, "s_")
        w1, w2 = sb("s_w1", P, KD, FF), sb("s_w2", P, KF, D)
        b1, b2 = sb("s_b1", P, KF), sb("s_b2", 1, D)
        hid = sb("s_hid", P, 2, KF, GT)
        kept = sb("s_kept", P, 2, SEQS)
        weight = sb("s_weight", P, SEQS)
        bank_up = [ps(f"s_bank_up{n}", P, GT) for n in range(UP_BANKS)]
        bank_out = [ps(f"s_bank_out{n}", P, D) for n in range(OUT_BANKS)]
        r.bank_l = bank_up[0:2]
        r.bank_lt = ps("s_bank_lt", P, SEQS, EXPERTS)
        count_buffers(ctx, nc, g, r, "s_")
        r.logits_e = sb("s_logits_e", EXPERTS, SEQS * P)
        r.loaded, r.loads = sem("s_loaded"), 16 * 5
        up_ps, hid_ready, out_ps, added = sem("s_up_ps"), sem("s_hid_ready"), sem("s_out_ps"), sem("s_added")
        block = ctx.enter_context(nc.Block())

        @block.sync
        def _(sp):
            for dst, src in ((r.gate_w, g.dram["router_w"]), (w1, g.dram["switch_w1"]), (b1, g.dram["switch_b1"]), (w2, g.dram["switch_w2"]), (b2, g.dram["switch_b2"])):
                sp.dma_start(dst[:], src).then_inc(r.loaded, 16)

        @block.gpsimd
        def _(pool):
            count_pool(nc, pool, g, r)

        @block.tensor
        def _(pe):
            route_pe(nc, pe, g, r)
            count_pe(nc, pe, g, r)
            with pe.Fori(0, GROUPS // 2) as m:
                for gb in range(2):
                    i = m * 2 + gb
                    for f in range(KF):
                        pe.wait_ge(hid_ready, i * KF + (f + 1))
                        for k in range(KD):
                            last = nc.tensor.matmul(bank_up[f % UP_BANKS][:], w1[:, k, P * f:P * f + P],
                                                    g.xm_feat[:, k, bass.ds(i * GT, GT)],
                                                    start=(k == 0), stop=(k == KD - 1))
                        last.then_inc(up_ps, 1)
                    for j in range(GROUP):
                        pe.wait_ge(added, i * GROUP + (j + 1))
                        nc.tensor.matmul(bank_out[j % OUT_BANKS][:], g.ones[0:1, :], b2[:], start=True, stop=False)
                        for f in range(KF):
                            if j == 0:
                                pe.wait_ge(hid_ready, i * KF + (f + 1 + UP_BANKS))
                            last = nc.tensor.matmul(bank_out[j % OUT_BANKS][:], hid[:, gb, f, P * j:P * j + P],
                                                    w2[:, f, :], start=False, stop=(f == KF - 1))
                        last.then_inc(out_ps, 1)

        @block.scalar
        def _(act):
            route_act(nc, act, g, r, True)
            act.sem_inc(hid_ready, UP_BANKS)
            with act.Fori(0, GROUPS // 2) as m:
                for gb in range(2):
                    for f in range(KF):
                        act.wait_ge(up_ps, m * (2 * KF) + (gb * KF + f + 1))
                        nc.scalar.activation(hid[:, gb, f, :], bank_up[f % UP_BANKS][:], ACT.Gelu, bias=b1[:, f:f + 1])\
                            .then_inc(hid_ready, 1)

        @block.vector
        def _(dve):
            v = nc.vector
            link = Links(dve, r.link)
            route_dve(nc, dve, g, r, link, True)
            count_dve(nc, dve, g, r, link)
            slot = r.slot
            link(v.tensor_scalar(slot[:], slot[:], CAP - 0.5, None, ALU.is_lt))
            link(v.tensor_tensor(slot[:], slot[:], r.hot[:].rearrange("p n q e -> p (n q) e"), ALU.mult))
            link(v.tensor_reduce(kept[:].rearrange("p n q -> p (n q)"), slot[:], AX.X, ALU.add))
            link(v.tensor_tensor(kept[:], kept[:], r.prob[:], ALU.mult))
            link(v.tensor_tensor(weight[:], kept[:, 0], kept[:, 1], ALU.add))
            dve.sem_inc(added, OUT_BANKS)
            with dve.Fori(0, GROUPS) as i:
                for j in range(GROUP):
                    dve.wait_ge(out_ps, i * GROUP + (j + 1))
                    q = i * GROUP + j
                    v.scalar_tensor_tensor(out=g.X[:, q, :], in0=bank_out[j % OUT_BANKS][:], scalar=weight[:, bass.ds(q, 1)],
                                           in1=g.X[:, q, :], op0=ALU.mult, op1=ALU.add).then_inc(added, 1)


def norm_buffers(ctx, nc, g, tag):
    def sb(name, *shape):
        return ctx.enter_context(nc.sbuf_tensor(tag + name, list(shape), F32))
    n = Shared()
    n.stats, n.mean_var, n.halves = sb("stats", P, GROUP, 6), sb("mean_var", P, GROUP, 2), sb("halves", P, 4, GROUP)
    n.small, n.tok = sb("small", P, 2, GROUP), sb("n_tok", P, GROUP, D)
    n.var_ready, n.rstd_ready, n.ready = g.sem(tag + "var_ready"), g.sem(tag + "rstd_ready"), g.sem(tag + "n_ready")
    return n


def groups(eng, first, group):
    first()
    with eng.Fori(0, GROUPS - 1) as i:
        group(i, True)
    group(GROUPS - 1, False)


def norm_stats_dve(nc, dve, g, n, link, i):
    v = nc.vector
    for j in range(GROUP):
        ins = v.bn_stats(n.stats[:, j, :], g.X[:, i * GROUP + j, :])
    link(ins)
    merge_stats(v, link, n.stats[:], n.mean_var, n.halves)
    v.tensor_scalar(n.small[:, 0, :], n.mean_var[:, :, 1], LN_EPS, None, ALU.add).then_inc(n.var_ready, 1)


def norm_apply_dve(nc, dve, g, n, i):
    dve.wait_ge(n.rstd_ready, i + 1)
    for j in range(GROUP):
        nc.vector.tensor_scalar(n.tok[:, j, :], g.X[:, i * GROUP + j, :], n.mean_var[:, j, 0:1], n.small[:, 1, j:j + 1],
                                ALU.subtract, ALU.mult).then_inc(n.ready, 1)


def norm_pool(nc, pool, g, n, i):
    pool.wait_ge(n.var_ready, i + 1)
    nc.gpsimd.tensor_tensor(n.small[:, 1, :], n.small[:, 0, :], g.neg_half[:, 0:GROUP], ALU.pow)\
        .then_inc(n.rstd_ready, 1)


def turn_pe(nc, pe, g, n, banks, turned, i):
    for j in range(GROUP):
        pe.wait_ge(n.ready, i * GROUP + (j + 1))
        for k in range(KD):
            last = nc.tensor.transpose(banks[k][:, P * j:P * j + P], n.tok[:, j, P * k:P * k + P], g.ident[:])
    last.then_inc(turned, 1)


BLK = 16
NBLK = P // BLK
LIMIT = 1e17
GH = 8
HK = P // GH


def gla_phase(nc, g):
    UNITS = GROUP * KD
    VEC_FIRST = 7 + 3
    VEC_LAST = 7
    with ExitStack() as ctx:
        def sb(name, *shape):
            return ctx.enter_context(nc.sbuf_tensor("g_" + name, list(shape), F32))

        def ps(name, *shape):
            return ctx.enter_context(nc.psum_tensor("g_" + name, list(shape), F32))

        sem = lambda name: g.sem("g_" + name)
        n = norm_buffers(ctx, nc, g, "g_")
        w = {m: sb("w" + m, P, KD, D) for m in "qkvgo"}
        gamma, beta = sb("gamma", P, KD), sb("beta", P, KD)
        n_feat = sb("n_feat", P, KD, GT)
        k_feat, q_feat, v_tok = sb("k_feat", P, KD, GT), sb("q_feat", P, KD, GT), sb("v_tok", P, GROUP, D)
        absx, soft = sb("absx", P, KD, GT), sb("soft", P, KD, GT)
        logg, run = sb("logg", P, KD, GT), sb("run", P, KD, GT)
        mid = sb("mid", P, KD, GROUP, NBLK)
        dist = sb("dist", P, KD, GT)
        ek, eq = sb("ek", P, KD, GT), sb("eq", P, KD, GT)
        hop = sb("hop", P, KD, GROUP, NBLK, NBLK)
        later = sb("later", P, NBLK, NBLK)
        reset = sb("reset", P, GROUP, P)
        head = sb("head", P, GH)
        kt = sb("kt", P, 2, NBLK, P)
        qbd = sb("qbd", P, 2, NBLK, GH, BLK)
        att = sb("att", P, 2, GH, NBLK, BLK)
        y_stats, y_mv, y_half = sb("y_stats", P, GROUP, 6), sb("y_mv", P, GROUP, 2), sb("y_half", P, 4, GROUP)
        y_small = sb("y_small", P, 2, GROUP)
        y_tok = sb("y_tok", P, GROUP, D)
        y_feat = sb("y_feat", P, KD, GT)
        bank_t = [ps(f"bank_t{k}", P, GT) for k in range(2)]
        bank_p = [ps(f"bank_p{k}", P, GT) for k in range(2)]
        bank_s = [ps(f"bank_s{k}", P, GT) for k in range(2)]
        bank_y = [ps(f"bank_y{k}", P, 2, D) for k in range(2)]

        loaded, consts, vec = sem("loaded"), sem("consts"), sem("vec")
        turned, feat_ready = sem("turned"), sem("feat_ready")
        g_ps, k_ps, q_ps, v_ps = sem("g_ps"), sem("k_ps"), sem("q_ps"), sem("v_ps")
        soft_ready, gates_read, exponents, decays, k_ready, q_ready, v_ready = (
            sem("soft_ready"), sem("gates_read"), sem("exponents"), sem("decays"), sem("k_ready"), sem("q_ready"),
            sem("v_ready"))
        kt_ready, qbd_ready = sem("kt_ready"), sem("qbd_ready")
        s_ps, att_ready, y_ps = sem("s_ps"), sem("att_ready"), sem("y_ps")
        y_var, y_rstd, y_ready, yT_ps, yT_ready, o_ps = (
            sem("y_var"), sem("y_rstd"), sem("y_ready"), sem("yT_ps"), sem("yT_ready"), sem("o_ps"))
        block = ctx.enter_context(nc.Block())

        def scores(u, h):
            return (bank_p if u % 2 else bank_s)[h][:].rearrange("p (b h t) -> p b h t", b=NBLK // 2, h=GH)

        @block.sync
        def _(sp):
            for m in "gkqvo":
                sp.dma_start(w[m][:], g.dram["gla_w" + m]).then_inc(loaded, 16)
            sp.dma_start(gamma[:], g.dram["gla_gamma"]).then_inc(loaded, 16)
            sp.dma_start(beta[:], g.dram["gla_beta"]).then_inc(loaded, 16)
            for m in ("w2", "had", "w1", "w3"):
                sp.dma_start(g.ffn[m], g.dram["ffn_" + m]).then_inc(g.ffn_w2_loaded if m == "w2" else g.ffn_loaded, 16)

        @block.gpsimd
        def _(pool):
            p = nc.gpsimd
            p.memset(reset[:], 1.0).then_inc(consts, 1)
            p.memset(head[:], float(HK) ** -0.5).then_inc(consts, 1)
            p.memset(later[:], 0.0).then_inc(consts, 1)
            pool.wait_ge(consts, 3)
            p.affine_select(out=later[:], in_=later[:], compare_op=ALU.is_ge, fill=-1000.0, base=0,
                            pattern=[[1, NBLK], [-1, NBLK]], channel_multiplier=0).then_inc(consts, 1)
            p.memset(reset[:, :, 0:1], 0.0).then_inc(consts, 1)
            p.affine_select(out=head[:], in_=head[:], compare_op=ALU.is_ge, fill=0.0, base=0,
                            pattern=[[-HK, GH]], channel_multiplier=1).then_inc(consts, 1)
            pool.wait_ge(consts, 6)
            p.affine_select(out=head[:], in_=head[:], compare_op=ALU.is_ge, fill=0.0, base=HK - 1,
                            pattern=[[HK, GH]], channel_multiplier=-1).then_inc(consts, 1)
            pool.wait_ge(consts, 7)

            def first():
                norm_pool(nc, pool, g, n, 0)
                pool.wait_ge(g.ffn_w2_loaded, 16)
                src, dst = g.ffn["w2"], g.ffn["w2b"]
                for m in range(3):
                    h = 1 << m
                    a = src.rearrange("p (n two h) d -> p n two h d", two=2, h=h)
                    o = dst.rearrange("p (n two h) d -> p n two h d", two=2, h=h)
                    for x in range(KF // (2 * h)):
                        p.tensor_tensor(o[:, x, 0], a[:, x, 0], a[:, x, 1], ALU.add).then_inc(g.folded, 1)
                        p.tensor_tensor(o[:, x, 1], a[:, x, 0], a[:, x, 1], ALU.subtract).then_inc(g.folded, 1)
                    pool.wait_ge(g.folded, sum(2 * (KF >> (q + 1)) for q in range(m + 1)))
                    src, dst = dst, src

            def group(i, more):
                for u in range(UNITS):
                    j, k = u // KD, u % KD
                    tok = slice(P * j, P * j + P)
                    if u < KD:
                        pool.wait_ge(q_ready, i * KD + (k + 1))
                    else:
                        pool.wait_ge(s_ps, i * (2 * UNITS) + (2 * (u - 1)))
                    p.tensor_tensor(qbd[:, u % 2],
                                    bc(q_feat[:, k, tok].rearrange("p (n t) -> p n t", n=NBLK).unsqueeze(2), [P, NBLK, GH, BLK]),
                                    bc(head[:].unsqueeze(1).unsqueeze(3), [P, NBLK, GH, BLK]), ALU.mult)\
                        .then_inc(qbd_ready, 1)
                if more:
                    norm_pool(nc, pool, g, n, i + 1)
                pool.wait_ge(y_var, i + 1)
                p.tensor_tensor(y_small[:, 1, :], y_small[:, 0, :], g.neg_half[:, 0:GROUP], ALU.pow).then_inc(y_rstd, 1)
            groups(pool, first, group)

        @block.tensor
        def _(pe):
            pe.wait_ge(loaded, 16 * 7)

            def project(what, banks, done):
                for c in range(KD):
                    for k in range(KD):
                        last = nc.tensor.matmul(banks[c][:], w[what][:, k, P * c:P * c + P], n_feat[:, k, :],
                                                start=(k == 0), stop=(k == KD - 1))
                    last.then_inc(done, 1)

            def project_v(i):
                pe.wait_ge(gates_read, i * KD + KD)
                for j in range(GROUP):
                    for k in range(KD):
                        last = nc.tensor.matmul(bank_s[j // 2][:, D * (j % 2):D * (j % 2) + D],
                                                n_feat[:, k, P * j:P * j + P], w["v"][:, k, :],
                                                start=(k == 0), stop=(k == KD - 1))
                    if j % 2:
                        last.then_inc(v_ps, 1)

            def first():
                turn_pe(nc, pe, g, n, bank_t, turned, 0)
                pe.wait_ge(feat_ready, KD)
                project("g", bank_s, g_ps)
                project("k", bank_t, k_ps)
                project("q", bank_p, q_ps)
                project_v(0)

            def a(i, u):
                pe.wait_ge(qbd_ready, i * UNITS + (u + 1))
                pe.wait_ge(kt_ready, i * UNITS + (u + 1))
                if u == 0:
                    pe.wait_ge(v_ready, i * 2 + 2)
                for h in range(2):
                    if u >= 2:
                        pe.wait_ge(att_ready, i * (2 * UNITS) + (2 * (u - 2) + h + 1))
                    for b in range(NBLK // 2):
                        blk = NBLK // 2 * h + b
                        last = nc.tensor.matmul(scores(u, h)[:, b], kt[:, u % 2, blk, :], qbd[:, u % 2, blk],
                                                start=True, stop=True)
                    last.then_inc(s_ps, 1)

            def b(i, u):
                j, k = u // KD, u % KD
                pe.wait_ge(att_ready, i * (2 * UNITS) + (2 * u + 2))
                for h in range(GH):
                    col = P * k + HK * h
                    last = nc.tensor.matmul(bank_y[j // 2][:, j % 2, col:col + HK],
                                            att[:, u % 2, h].rearrange("p n t -> p (n t)"),
                                            v_tok[:, j, col:col + HK], start=True, stop=True)
                last.then_inc(y_ps, 1)

            def group(i, more):
                for u in range(UNITS):
                    a(i, u)
                    if u >= 2:
                        b(i, u - 2)
                if more:
                    turn_pe(nc, pe, g, n, bank_t, turned, i + 1)
                b(i, UNITS - 2)
                b(i, UNITS - 1)
                if more:
                    pe.wait_ge(feat_ready, i * KD + 2 * KD)
                    project("g", bank_s, g_ps)
                    project("k", bank_t, k_ps)
                for j in range(GROUP):
                    pe.wait_ge(y_ready, i * GROUP + (j + 1))
                    for k in range(KD):
                        last = nc.tensor.transpose(bank_p[k][:, P * j:P * j + P], y_tok[:, j, P * k:P * k + P], g.ident[:])
                last.then_inc(yT_ps, 1)
                if more:
                    project_v(i + 1)
                pe.wait_ge(yT_ready, i * KD + KD)
                if more:
                    project("q", bank_p, q_ps)
                for j in range(GROUP):
                    for k in range(KD):
                        last = nc.tensor.matmul(bank_y[j // 2][:, j % 2, :], y_feat[:, k, P * j:P * j + P], w["o"][:, k, :],
                                                start=(k == 0), stop=(k == KD - 1))
                    if j % 2:
                        last.then_inc(o_ps, 1)
            groups(pe, first, group)

        @block.scalar
        def _(act):
            s = nc.scalar
            act.wait_ge(loaded, 16 * 7)

            def feats(i):
                act.wait_ge(turned, i + 1)
                for k in range(KD):
                    s.copy(n_feat[:, k, :], bank_t[k][:]).then_inc(feat_ready, 1)

            def gates(i):
                for k in range(KD):
                    act.wait_ge(g_ps, i * KD + (k + 1))
                    s.activation(absx[:, k, :], bank_s[k][:], ACT.Abs).then_inc(soft_ready, 1)
                for k in range(KD):
                    act.wait_ge(soft_ready, i * (3 * KD) + (k + 1))
                    s.activation(soft[:, k, :], absx[:, k, :], ACT.Exp, scale=-1.0).then_inc(soft_ready, 1)
                for k in range(KD):
                    act.wait_ge(soft_ready, i * (3 * KD) + (KD + k + 1))
                    s.activation(soft[:, k, :], soft[:, k, :], ACT.Ln, bias=1.0).then_inc(soft_ready, 1)

            def spread(i):
                for x, (out, sign) in enumerate(((ek, -1.0), (eq, 1.0))):
                    for k in range(KD):
                        act.wait_ge(exponents, i * (2 * KD) + (k + 1))
                        s.activation(out[:, k, :], dist[:, k, :], ACT.Exp, scale=sign).then_inc(decays, 1)
                for k in range(KD):
                    act.wait_ge(exponents, i * (2 * KD) + (KD + k + 1))
                    s.activation(hop[:, k], hop[:, k], ACT.Exp).then_inc(decays, 1)
                for h in range(2):
                    act.wait_ge(v_ps, i * 2 + (h + 1))
                    s.copy(v_tok[:, 2 * h:2 * h + 2, :].rearrange("p a d -> p (a d)"), bank_s[h][:]).then_inc(v_ready, 1)

            def first():
                feats(0)
                gates(0)
                spread(0)

            def group(i, more):
                if more:
                    feats(i + 1)
                    gates(i + 1)
                act.wait_ge(yT_ps, i + 1)
                for k in range(KD):
                    s.activation(y_feat[:, k, :], bank_p[k][:], ACT.Identity, scale=gamma[:, k:k + 1],
                                 bias=beta[:, k:k + 1]).then_inc(yT_ready, 1)
                if more:
                    spread(i + 1)
            groups(act, first, group)

        @block.vector
        def _(dve):
            v = nc.vector
            dve.wait_ge(consts, 7)

            def gates(i, link):
                for k in range(KD):
                    dve.wait_ge(soft_ready, i * (3 * KD) + (2 * KD + k + 1))
                    v.scalar_tensor_tensor(out=logg[:, k, :], in0=bank_s[k][:], scalar=0.0, in1=soft[:, k, :],
                                           op0=ALU.min, op1=ALU.subtract).then_inc(gates_read, 1)
                for k in range(KD):
                    dve.wait_ge(gates_read, i * KD + (k + 1))
                    ins = v.tensor_tensor_scan(run[:, k, :], reset[:].rearrange("p a b -> p (a b)"), logg[:, k, :], 0.0,
                                               ALU.mult, ALU.add)
                link(ins)
                for k in range(KD):
                    ins = v.tensor_copy(mid[:, k].rearrange("p a n -> p (a n)"), run[:, k, BLK // 2 - 1:GT:BLK])
                link(ins)
                for k in range(KD):
                    v.tensor_tensor(dist[:, k, :].rearrange("p (n t) -> p n t", t=BLK),
                                    run[:, k, :].rearrange("p (n t) -> p n t", t=BLK),
                                    bc(mid[:, k].rearrange("p a n -> p (a n)").unsqueeze(2), [P, GROUP * NBLK, BLK]),
                                    ALU.subtract).then_inc(exponents, 1)
                square = [P, GROUP, NBLK, NBLK]
                for k in range(KD):
                    ins = v.tensor_tensor(hop[:, k], bc(mid[:, k].unsqueeze(3), square), bc(mid[:, k].unsqueeze(2), square),
                                          ALU.subtract)
                link(ins)
                for k in range(KD):
                    v.scalar_tensor_tensor(out=hop[:, k], in0=hop[:, k], scalar=0.0, in1=bc(later[:].unsqueeze(1), square),
                                           op0=ALU.min, op1=ALU.add).then_inc(exponents, 1)

            def spread(i, link):
                for x, (e, banks, ps_ready, out, ready) in enumerate(((ek, bank_t, k_ps, k_feat, k_ready),
                                                                      (eq, bank_p, q_ps, q_feat, q_ready))):
                    for k in range(KD):
                        dve.wait_ge(ps_ready, i * KD + (k + 1))
                        dve.wait_ge(decays, i * (3 * KD) + (KD * x + k + 1))
                        ins = v.scalar_tensor_tensor(out=out[:, k, :], in0=e[:, k, :], scalar=LIMIT, in1=banks[k][:],
                                                     op0=ALU.min, op1=ALU.mult)
                        ins.then_inc(ready, 1)
                    dve.wait_ge(ready, i * KD + KD)

            def a(i, u):
                j, k = u // KD, u % KD
                if u >= 2:
                    dve.wait_ge(s_ps, i * (2 * UNITS) + 2 * (u - 1))
                if u == 0:
                    dve.wait_ge(decays, i * (3 * KD) + 3 * KD)
                four = [P, NBLK, NBLK, BLK]
                v.tensor_tensor(kt[:, u % 2].rearrange("p i (j t) -> p i j t", t=BLK),
                                bc(k_feat[:, k, P * j:P * j + P].rearrange("p (j t) -> p j t", t=BLK).unsqueeze(1), four),
                                bc(hop[:, k, j].unsqueeze(3), four), ALU.mult).then_inc(kt_ready, 1)

            def b(i, u):
                for h in range(2):
                    dve.wait_ge(s_ps, i * (2 * UNITS) + (2 * u + h + 1))
                    if u >= 2:
                        dve.wait_ge(y_ps, i * UNITS + (u - 1))
                    half = slice(NBLK // 2 * h, NBLK // 2 * (h + 1))
                    v.tensor_tensor(att[:, u % 2, :, half].rearrange("p h n t -> p n h t"), scores(u, h),
                                    bc(g.upto[:, P // 2 * h:P // 2 * (h + 1)]
                                       .rearrange("p (n t) -> p n t", t=BLK).unsqueeze(2), [P, NBLK // 2, GH, BLK]),
                                    ALU.mult).then_inc(att_ready, 1)

            def first():
                link = Links(dve, vec)
                norm_stats_dve(nc, dve, g, n, link, 0)
                norm_apply_dve(nc, dve, g, n, 0)
                gates(0, link)
                spread(0, link)
                assert link.n == VEC_FIRST, link.n

            def group(i, more):
                link = Links(dve, vec, i * (VEC_FIRST + VEC_LAST) + VEC_FIRST)
                a(i, 0)
                for u in range(UNITS):
                    if u + 1 < UNITS:
                        a(i, u + 1)
                    elif more:
                        norm_apply_dve(nc, dve, g, n, i + 1)
                    if u == UNITS // 2 and more:
                        norm_stats_dve(nc, dve, g, n, link, i + 1)
                    b(i, u)
                dve.wait_ge(y_ps, i * UNITS + UNITS)
                v.memset(y_half[:, 0], 0.0)
                for j in range(GROUP):
                    ins = v.bn_stats(y_stats[:, j, :], bank_y[j // 2][:, j % 2, :])
                link(ins)
                merge_stats(v, link, y_stats[:], y_mv, y_half)
                v.tensor_scalar(y_small[:, 0, :], y_mv[:, :, 1], LN_EPS, None, ALU.add).then_inc(y_var, 1)
                dve.wait_ge(y_rstd, i + 1)
                for j in range(GROUP):
                    v.tensor_scalar(y_tok[:, j, :], bank_y[j // 2][:, j % 2, :], y_mv[:, j, 0:1], y_small[:, 1, j:j + 1],
                                    ALU.subtract, ALU.mult).then_inc(y_ready, 1)
                if more:
                    gates(i + 1, link)
                    spread(i + 1, link)
                for h in range(2):
                    dve.wait_ge(o_ps, i * 2 + (h + 1))
                    seqs = bass.ds(i * GROUP + 2 * h, 2)
                    v.tensor_tensor(g.X[:, seqs, :], g.X[:, seqs, :], bank_y[h][:], ALU.add)
                if more:
                    assert link.n == VEC_FIRST + VEC_LAST, link.n
            groups(dve, first, group)


def channel_phase(nc, g):
    SCALE = float(D) ** -0.5
    VEC_STEPS = 7 + GROUP
    with ExitStack() as ctx:
        def sb(name, *shape):
            return ctx.enter_context(nc.sbuf_tensor("c_" + name, list(shape), F32))

        def ps(name, *shape):
            return ctx.enter_context(nc.psum_tensor("c_" + name, list(shape), F32))

        sem = lambda name: g.sem("c_" + name)
        n = norm_buffers(ctx, nc, g, "c_")
        c_tok, c_feat = sb("c_tok", P, 2, GROUP, D), sb("c_feat", P, 2, KD, GROUP, P)
        peak, bias, total, inv = sb("peak", P, 2, KD), sb("bias", P, 2, KD), sb("total", P, 2, KD), sb("inv", P, 2, KD)
        prob = sb("prob", P, 2, KD, D)
        bank_a = [ps(f"bank_a{k}", P, KD, D) for k in range(2)]
        bank_o = [ps(f"bank_o{k}", P, D) for k in range(2)]
        c_loaded, c_used = [sem("c_loaded0"), sem("c_loaded1")], sem("c_used")
        vec, had_ps, inv_ready = sem("vec"), sem("had_ps"), sem("inv_ready")
        a_ps, bias_ready, exp_ready, prob_ready, o_ps, added = (
            sem("a_ps"), sem("bias_ready"), sem("exp_ready"), sem("prob_ready"), sem("o_ps"), sem("added"))
        block = ctx.enter_context(nc.Block())

        def slots(a, b, c):
            for s in range(GROUP + 2):
                for stage, late in ((a, 0), (b, 1), (c, 2)):
                    if 0 <= s - late < GROUP:
                        stage(s - late)

        @block.sync
        def _(sp):
            with sp.Fori(0, GROUPS // 2) as m:
                for b in range(2):
                    sp.wait_ge(c_used, m * 2 + (b + 1))
                    seqs = bass.ds(m * (2 * GROUP) + b * GROUP, GROUP)
                    sp.dma_start(c_tok[:, b], g.dram["ctx"].rearrange("q s d -> s q d")[:, seqs, :]).then_inc(c_loaded[b], 16)
                    for k in range(KD):
                        sp.dma_start(c_feat[:, b, k], g.dram["ctx_feat"][:, k, seqs, :]).then_inc(c_loaded[b], 16)

        @block.gpsimd
        def _(pool):
            norm_pool(nc, pool, g, n, 0)
            with pool.Fori(1, GROUPS) as i:
                norm_pool(nc, pool, g, n, i)

        @block.tensor
        def _(pe):
            pe.wait_ge(g.ffn_loaded, 16 * 3)
            pe.wait_ge(g.folded, 2 * (KF - 1))
            for f in range(KF):
                if f >= 2:
                    pe.wait_ge(g.w2h_ready, f - 1)
                nc.tensor.matmul(bank_o[f % 2][:], g.ffn["had"], g.ffn["w2b"][:, f, :], start=True, stop=True)\
                    .then_inc(had_ps, 1)
            pe.wait_ge(g.w2h_ready, KF)
            with pe.Fori(0, GROUPS // 2) as m:
                for gb in range(2):
                    i = m * 2 + gb
                    pe.wait_ge(c_loaded[gb], m * 48 + 48)

                    def a(j):
                        pe.wait_ge(n.ready, i * GROUP + (j + 1))
                        pe.wait_ge(exp_ready, i * GROUP + (j + 1))
                        for k in range(KD):
                            last = nc.tensor.matmul(bank_a[j % 2][:, k, :], c_tok[:, gb, j, P * k:P * k + P], n.tok[:, j, :],
                                                    start=True, stop=True)
                        last.then_inc(a_ps, 1)

                    def none(j):
                        pass

                    def c(j):
                        pe.wait_ge(prob_ready, i * GROUP + (j + 1))
                        pe.wait_ge(added, i * GROUP + (j + 1))
                        for k in range(KD):
                            last = nc.tensor.matmul(bank_o[j % 2][:], c_feat[:, gb, k, j, :], prob[:, j % 2, k, :],
                                                    start=(k == 0), stop=(k == KD - 1))
                        last.then_inc(o_ps, 1)
                    slots(a, none, c)

        @block.scalar
        def _(act):
            for f in range(KF):
                act.wait_ge(had_ps, f + 1)
                nc.scalar.mul(g.ffn["w2h"][:, f, :], bank_o[f % 2][:], 0.5 / float(FF) ** 0.5).then_inc(g.w2h_ready, 1)
            act.sem_inc(exp_ready, 2)
            with act.Fori(0, GROUPS) as i:
                for j in range(GROUP):
                    act.wait_ge(bias_ready, i * GROUP + (j + 1))
                    for k in range(KD):
                        last = nc.scalar.activation(prob[:, j % 2, k, :], bank_a[j % 2][:, k, :], ACT.Exp, scale=SCALE,
                                                    bias=bias[:, j % 2, k:k + 1], accum_out=total[:, j % 2, k:k + 1])
                    last.then_inc(exp_ready, 1)

        @block.vector
        def _(dve):
            v = nc.vector
            dve.sem_inc(added, 2)
            dve.sem_inc(c_used, 2)

            def first():
                norm_stats_dve(nc, dve, g, n, Links(dve, vec), 0)
                norm_apply_dve(nc, dve, g, n, 0)

            def group(i, more):
                link = Links(dve, vec, i * VEC_STEPS + 7)

                def a(j):
                    dve.wait_ge(a_ps, i * GROUP + (j + 1))
                    if j >= 2:
                        dve.wait_ge(o_ps, i * GROUP + (j - 1))
                    link(v.tensor_reduce(peak[:, j % 2, :], bank_a[j % 2][:], AX.X, ALU.max))
                    v.tensor_scalar(bias[:, j % 2, :], peak[:, j % 2, :], -SCALE, None, ALU.mult).then_inc(bias_ready, 1)
                    if j == 1 and more:
                        norm_stats_dve(nc, dve, g, n, link, i + 1)
                    if j == GROUP - 1 and more:
                        norm_apply_dve(nc, dve, g, n, i + 1)

                def b(j):
                    dve.wait_ge(exp_ready, i * GROUP + (j + 3))
                    v.reciprocal(inv[:, j % 2, :], total[:, j % 2, :]).then_inc(inv_ready, 1)
                    dve.wait_ge(inv_ready, i * GROUP + (j + 1))
                    v.tensor_tensor(prob[:, j % 2], prob[:, j % 2], bc(inv[:, j % 2, :].unsqueeze(2), [P, KD, D]), ALU.mult)\
                        .then_inc(prob_ready, 1)

                def c(j):
                    dve.wait_ge(o_ps, i * GROUP + (j + 1))
                    q = i * GROUP + j
                    v.tensor_tensor(g.X[:, q, :], g.X[:, q, :], bank_o[j % 2][:], ALU.add).then_inc(added, 1)
                slots(a, b, c)
                dve.sem_inc(c_used, 1)
                if more:
                    assert link.n == VEC_STEPS, link.n
            groups(dve, first, group)


def ffn_phase(nc, g):
    VEC_STEPS = 7 + KF
    with ExitStack() as ctx:
        def sb(name, *shape):
            return ctx.enter_context(nc.sbuf_tensor("f_" + name, list(shape), F32))

        def ps(name, *shape):
            return ctx.enter_context(nc.psum_tensor("f_" + name, list(shape), F32))

        sem = lambda name: g.sem("f_" + name)
        n = norm_buffers(ctx, nc, g, "f_")
        w1, w3, w2h = g.ffn["w1"], g.ffn["w3"], g.ffn["w2h"]
        n_feat = sb("n_feat", P, KD, GT)
        tanh, silu = sb("tanh", P, 2, GT), sb("silu", P, 2, GT)
        hid = sb("hid", P, KF, GT)
        bank_t = [ps(f"bank_t{k}", P, GT) for k in range(2)]
        bank_g = [ps(f"bank_g{k}", P, GT) for k in range(2)]
        bank_u = [ps(f"bank_u{k}", P, GT) for k in range(2)]
        bank_o = [ps(f"bank_o{k}", P, D) for k in range(2)]
        vec = sem("vec")
        turned, feat_ready, gu_ps, tanh_ready, hid_ready = (
            sem("turned"), sem("feat_ready"), sem("gu_ps"), sem("tanh_ready"), sem("hid_ready"))
        o_ps, added, stored = sem("o_ps"), sem("added"), sem("stored")
        block = ctx.enter_context(nc.Block())

        @block.sync
        def _(sp):
            with sp.Fori(0, GROUPS) as i:
                sp.wait_ge(added, i * GROUP + (GROUP + 2))
                seqs = bass.ds(i * GROUP, GROUP)
                sp.dma_start(g.dram["out"].rearrange("q t d -> t q d")[:, seqs, :], g.X[:, seqs, :]).then_inc(stored, 16)
            sp.wait_ge(stored, 16 * GROUPS)

        @block.gpsimd
        def _(pool):
            norm_pool(nc, pool, g, n, 0)
            with pool.Fori(1, GROUPS) as i:
                norm_pool(nc, pool, g, n, i)

        @block.tensor
        def _(pe):
            def first():
                turn_pe(nc, pe, g, n, bank_t, turned, 0)

            def group(i, more):
                pe.wait_ge(feat_ready, i * KD + KD)
                for f in range(KF):
                    pe.wait_ge(hid_ready, i * KF + (f + 1))
                    for w, bank in ((w1, bank_g), (w3, bank_u)):
                        for k in range(KD):
                            last = nc.tensor.matmul(bank[f % 2][:], w[:, k, P * f:P * f + P], n_feat[:, k, :],
                                                    start=(k == 0), stop=(k == KD - 1))
                    last.then_inc(gu_ps, 1)
                if more:
                    turn_pe(nc, pe, g, n, bank_t, turned, i + 1)
                for j in range(GROUP):
                    pe.wait_ge(added, i * GROUP + (j + 1))
                    for f in range(KF):
                        if j == 0:
                            pe.wait_ge(hid_ready, i * KF + (f + 3))
                        last = nc.tensor.matmul(bank_o[j % 2][:], hid[:, f, P * j:P * j + P], w2h[:, f, :],
                                                start=(f == 0), stop=(f == KF - 1))
                    last.then_inc(o_ps, 1)
            groups(pe, first, group)

        @block.scalar
        def _(act):
            def feats(i):
                act.wait_ge(turned, i + 1)
                for k in range(KD):
                    nc.scalar.copy(n_feat[:, k, :], bank_t[k][:]).then_inc(feat_ready, 1)

            def group(i, more):
                for f in range(KF):
                    act.wait_ge(gu_ps, i * KF + (f + 1))
                    nc.scalar.activation(tanh[:, f % 2, :], bank_g[f % 2][:], ACT.Tanh, scale=0.5).then_inc(tanh_ready, 1)
                if more:
                    feats(i + 1)
            groups(act, lambda: feats(0), group)

        @block.vector
        def _(dve):
            v = nc.vector
            dve.sem_inc(hid_ready, 2)
            dve.sem_inc(added, 2)

            def first():
                norm_stats_dve(nc, dve, g, n, Links(dve, vec), 0)
                norm_apply_dve(nc, dve, g, n, 0)

            def group(i, more):
                link = Links(dve, vec, i * VEC_STEPS + 7)
                for f in range(KF):
                    dve.wait_ge(tanh_ready, i * KF + (f + 1))
                    link(v.scalar_tensor_tensor(out=silu[:, f % 2, :], in0=tanh[:, f % 2, :], scalar=1.0,
                                                in1=bank_g[f % 2][:], op0=ALU.add, op1=ALU.mult))
                    v.tensor_tensor(hid[:, f, :], silu[:, f % 2, :], bank_u[f % 2][:], ALU.mult).then_inc(hid_ready, 1)
                    if f == 1 and more:
                        norm_stats_dve(nc, dve, g, n, link, i + 1)
                    if f == 4 and more:
                        norm_apply_dve(nc, dve, g, n, i + 1)
                for j in range(GROUP):
                    dve.wait_ge(o_ps, i * GROUP + (j + 1))
                    q = i * GROUP + j
                    v.tensor_tensor(g.X[:, q, :], g.X[:, q, :], bank_o[j % 2][:], ALU.add).then_inc(added, 1)
                if more:
                    assert link.n == VEC_STEPS, link.n
            groups(dve, first, group)


def build_program(nc, dram):
    with ExitStack() as ctx:
        g = Shared()
        g.dram = dram
        g.sem = nc.alloc_semaphore

        def sb(name, *shape):
            return ctx.enter_context(nc.sbuf_tensor(name, list(shape), F32))
        g.X = sb("X", P, SEQS, D)
        g.xm_tok = sb("xm_tok_all", P, SEQS, D)
        g.moe_w2 = sb("moe_w2", P, EXPERTS, KF, D)
        g.xm_feat = g.moe_w2[:, EXPERTS - 2:].rearrange("p a b c -> p (a b c)").rearrange("p (k t) -> p k t", k=KD)
        g.moe_norm_w = sb("moe_norm_w", P, KD)
        g.zeros = sb("zeros", P, D)
        g.slot_in = nc.dram_tensor("slot_in", ((TILES + 1) * P, D), F32, kind="Internal").ap()
        g.slot_out = nc.dram_tensor("slot_out", (TILES * P, D), F32, kind="Internal").ap()
        g.zeroed, g.slots_zero, g.w2_loaded = g.sem("zeroed"), g.sem("slots_zero"), g.sem("w2_loaded")
        g.ident, g.upto, g.after, g.ones = sb("ident", P, P), sb("upto", P, P), sb("after", P, P), sb("ones", P, P)
        g.neg_half = sb("neg_half", P, SEQS)
        g.x_loaded, g.a_exp = g.sem("x_loaded"), g.sem("a_exp")
        g.vec_steps_mamba = 55
        g.iota8 = sb("iota8", P, EXPERTS)
        mamba_phase(nc, g)
        before_moe = nc.snapshot_sems()
        moe_phase(nc, g)
        nc.clear_and_free_semaphores(nc.allocated_since(before_moe))
        nc.all_engine_barrier()
        wkv_phase(nc, g)
        switch_phase(nc, g)
        g.ffn = {m: g.moe_w2[:, n] for n, m in enumerate(("w2", "w2b", "w2h"))}
        g.ffn.update({m: g.moe_w2[:, n].rearrange("p a b -> p (a b)").rearrange("p (k f) -> p k f", k=KD)
                      for n, m in ((3, "w1"), (4, "w3"))})
        g.ffn["had"] = g.moe_w2[:, 5, 0, 0:P]
        g.ffn_w2_loaded, g.ffn_loaded = g.sem("ffn_w2_loaded"), g.sem("ffn_loaded")
        g.folded, g.w2h_ready = g.sem("folded"), g.sem("w2h_ready")
        gla_phase(nc, g)
        channel_phase(nc, g)
        ffn_phase(nc, g)


def _tiles(a):
    return a.reshape((a.shape[0] // P, P) + a.shape[1:]).swapaxes(0, 1)


def hadamard(n):
    h = np.ones((1, 1), np.float32)
    while len(h) < n:
        h = np.block([[h, h], [h, -h]])
    return h


def laid_out(inputs):
    f = {k: np.asarray(v) for k, v in inputs.items()}
    w = lambda name: f[name]
    return {
        "x": w("x"),
        "in_proj_w": _tiles(w("L0_attn_in_proj_w").T),
        "out_proj_w": _tiles(w("L0_attn_out_proj_w").T),
        "norm_mamba_w": _tiles(w("L0_attn_norm_mamba_w")),
        "norm_moe_w": _tiles(w("L0_attn_norm_moe_w")),
        "ssm_norm_w": _tiles(w("L0_attn_ssm_norm_w")),
        "conv_w_inner": _tiles(w("L0_attn_conv_w")[:DI]),
        "conv_b_inner": _tiles(w("L0_attn_conv_b")[:DI]),
        "conv_w_bc": w("L0_attn_conv_w")[DI:].reshape(2, NS, TAPS).swapaxes(0, 1),
        "conv_b_bc": w("L0_attn_conv_b")[DI:].reshape(2, NS).T,
        "dt_bias": w("L0_attn_dt_bias"),
        "gate_w": _tiles(w("L0_attn_gate_w").T),
        "moe_w1": w("L0_attn_w1").transpose(0, 2, 1).reshape(EXPERTS, KD, P, FF).swapaxes(1, 2),
        "moe_w2": w("L0_attn_w2").transpose(0, 2, 1).reshape(EXPERTS, KF, P, D).swapaxes(1, 2),
        "ctx_feat": w("ctx_2048").reshape(SEQS, P, KD, P).transpose(3, 2, 0, 1),
        "time_decay": _tiles(w("L0_xattn_time_decay")),
        "time_first": _tiles(w("L0_xattn_time_first")),
        "router_w": _tiles(w("L0_ffn_router_w").T),
        "switch_w1": _tiles(w("L0_ffn_w1").T),
        "switch_b1": _tiles(w("L0_ffn_b1")),
        "switch_w2": _tiles(w("L0_ffn_w2").T),
        "switch_b2": w("L0_ffn_b2").reshape(1, D),
        "gla_wq": _tiles(w("L1_attn_Wq").T),
        "gla_wk": _tiles(w("L1_attn_Wk").T),
        "gla_wv": _tiles(w("L1_attn_Wv").T),
        "gla_wg": _tiles(w("L1_attn_Wg").T),
        "gla_wo": _tiles(w("L1_attn_Wo").T),
        "gla_gamma": _tiles(w("L1_attn_gamma")),
        "gla_beta": _tiles(w("L1_attn_beta")),
        "ctx": w("ctx_2048"),
        "ffn_w1": _tiles(w("L1_ffn_W1").T),
        "ffn_w3": _tiles(w("L1_ffn_W3").T),
        "ffn_w2": _tiles(w("L1_ffn_W2").T),
        "ffn_had": hadamard(P),
        "A_log": w("L0_attn_A_log"),
        "D": w("L0_attn_D").reshape(CI, 2).T,
    }


def kernel(**inputs):
    import concourse.bacc as bacc
    from concourse.bass_utils import run_bass_kernel_spmd

    nc = bacc.Bacc("TRN2", target_bir_lowering=False, num_devices=1)
    arrays, handles = {}, {}
    for name, a in laid_out(inputs).items():
        a = np.ascontiguousarray(a)
        arrays[f"in_{name}"] = a
        handles[name] = nc.dram_tensor(f"in_{name}", a.shape, mybir.dt.from_np(a.dtype), kind="ExternalInput").ap()
    handles["out"] = nc.dram_tensor("out_x", (SEQS, P, D), F32, kind="ExternalOutput").ap()
    build_program(nc, handles)
    r = run_bass_kernel_spmd(nc, [arrays], core_ids=[0])
    return r.results[0]["out_x"]
```

```python
from contextlib import ExitStack

import numpy as np

import concourse.bass as bass
from concourse import mybir

F32 = mybir.dt.float32
U32 = mybir.dt.uint32
BF16 = mybir.dt.bfloat16
I32 = mybir.dt.int32
ALU = mybir.AluOpType
ACT = mybir.ActivationFunctionType
AX = mybir.AxisListType

P = 128
SEQS, D = 16, 256
KD = D // P
GROUP = 4
GROUPS = SEQS // GROUP
GT = GROUP * P
DI, HEADS, HD, NS = 512, 8, 64, 64
CI = DI // P
TAPS = 4
PAD = TAPS - 1
EXPERTS, FF = 8, 1024
KF = FF // P
TILES = 2 * SEQS + EXPERTS - 1
CAP = 64
BLOCKS = 2 * SEQS
LN_EPS, RMS_EPS = 1e-5, 1e-6


def merge_stats(v, link, stats, mean_var, halves):
    link(v.tensor_tensor(halves[:, 0], stats[:, :, 1], stats[:, :, 4], ALU.add))
    link(v.tensor_tensor(halves[:, 1], stats[:, :, 1], stats[:, :, 4], ALU.subtract))
    link(v.tensor_tensor(halves[:, 2], stats[:, :, 2], stats[:, :, 5], ALU.add))
    link(v.tensor_scalar(mean_var[:, :, 0], halves[:, 0], 0.5, None, ALU.mult))
    link(v.scalar_tensor_tensor(out=halves[:, 3], in0=halves[:, 1], scalar=0.25, in1=halves[:, 1],
                                op0=ALU.mult, op1=ALU.mult))
    link(v.scalar_tensor_tensor(out=mean_var[:, :, 1], in0=halves[:, 2], scalar=1.0 / D, in1=halves[:, 3],
                                op0=ALU.mult, op1=ALU.add))


class Shared:
    pass


class Links:

    def __init__(self, eng, sem, base=0):
        self.eng, self.sem, self.base, self.n = eng, sem, base, 0

    def restart(self, base):
        self.base, self.n = base, 0

    def __call__(self, ins):
        ins.then_inc(self.sem, 1)
        self.n += 1
        self.eng.wait_ge(self.sem, self.base + self.n)


def bc(ap, shape):
    return ap.broadcast_to(shape)


def log1p_terms(n):
    return [1.0 / (2 * k + 1) for k in range(n, 0, -1)]


def mamba_phase(nc, g):
    SS_COL = D
    NCONV = 1 + CI
    NPROJ = NCONV + CI
    VEC_START, VEC_AHEAD, VEC_BEHIND = 21, 30, GROUP
    with ExitStack() as ctx:
        def sb(name, *shape):
            return ctx.enter_context(nc.sbuf_tensor(name, list(shape), F32))

        def ps(name, *shape):
            return ctx.enter_context(nc.psum_tensor(name, list(shape), F32))

        sem = g.sem
        win = sb("win", P, KD, 2 * DI + 2 * NS + HEADS)
        wout = sb("wout", P, CI, D)
        norm_w = sb("norm_w", P, KD)
        gate_w = sb("gate_w", P, KD, EXPERTS)
        moe_w = g.moe_norm_w
        spare = lambda n, a, b: g.moe_w2[:, n].rearrange("p a b -> p (a b)")[:, a:b]
        ssm_w = sb("ssm_w", P, CI)
        conv_w = sb("conv_w", P, CI + 1, TAPS)
        conv_b = sb("conv_b", P, CI + 1)
        dt_bias = sb("dt_bias", P, HEADS)
        a_neg = sb("a_neg", P, HEADS)
        d_skip = sb("d_skip", P, CI)
        stats = sb("stats", P, SEQS, 6)
        mean_var = sb("mean_var", P, SEQS, 2)
        halves = sb("halves", P, 4, SEQS)
        ln_var, ln_rstd, ms_a, ms_b, rms_var, rms_rstd = (sb(n, P, SEQS) for n in (
            "ln_var", "ln_rstd", "ms_a", "ms_b", "rms_var", "rms_rstd"))
        u_tok = [sb("u_tok", P, GROUP, D)[:], spare(2, 0, GROUP * D).rearrange("p (q d) -> p q d", d=D)]
        xs_feat = [sb("xs_feat", P, CI, GT)[:], spare(0, 0, CI * GT).rearrange("p (c t) -> p c t", c=CI)]
        gate = [sb("gate", P, CI, GT)[:], spare(1, 0, CI * GT).rearrange("p (c t) -> p c t", c=CI)]
        bc_feat = [sb("bc_feat", NS, 2, GT)[:], spare(2, GROUP * D, GROUP * D + 2 * GT)[0:NS].rearrange("p (n t) -> p n t", n=2)]
        h_tok = sb("h_tok", P, GROUP, D)
        h_feat = sb("h_feat", P, KD, GT)
        dtw = sb("dtw", P, 6, GROUP * HEADS)
        dt = sb("dt", P, 2, GROUP * HEADS)
        da = sb("da", P, 2, GROUP * HEADS)
        xpad = sb("xpad", P, CI + 1, GROUP, PAD + P)
        conv = sb("conv", P, 2, GROUP, P)
        tanh = sb("tanh", P, 2, GT)
        gate_t = sb("gate_t", P, 2, GT)
        gm = sb("gm", P, 2, P)
        xdt = sb("xdt", P, 2, DI)
        steps_da = sb("steps_da", P, HEADS, P)
        decay = sb("decay", P, 2, HEADS, P)
        y_feat = sb("y_feat", P, CI, P)
        yg = sb("yg", P, 2, CI, P)
        yg2 = sb("yg2", P, 2, CI, P)
        hm = sb("hm", P, 2, D)
        hm_sq = sb("hm_sq", P, D)
        xm_tok = sb("xm_tok", P, GROUP, D)
        sc = sb("sc", P, 2, 4)

        bank_a = [ps(f"bank_a{k}", P, GT) for k in range(2)]
        bank_g, bank_x, bank_o = ps("bank_g", P, P + GROUP * EXPERTS), ps("bank_x", P, DI), ps("bank_o", P, D + 1)
        bank_d = ps("bank_d", P, HEADS, P)
        bank_y = ps("bank_y", P, CI, P)

        loaded_in, loaded, consts = sem("m_loaded_in"), sem("m_loaded"), sem("m_consts")
        x_rest_loaded = sem("m_x_rest_loaded")
        logits_ps, logits_used = sem("m_logits_ps"), sem("m_logits_used")
        vec, pool_done, a_cut, wout_ready = sem("m_vec"), sem("m_pool"), sem("m_a_cut"), sem("m_wout_ready")
        var_ready, rstd_ready = sem("m_var_ready"), sem("m_rstd_ready")
        u_ready, h_ready = sem("m_u_ready"), sem("m_h_ready")
        hT_ps, hT_ready = sem("m_hT_ps"), sem("m_hT_ready")
        dt_ps, dt_abs, dt_exp, dt_ready = sem("m_dt_ps"), sem("m_dt_abs"), sem("m_dt_exp"), sem("m_dt_ready")
        proj_ps, proj_used_a, proj_used_v = sem("m_proj_ps"), sem("m_proj_used_a"), sem("m_proj_used_v")
        pad_ready, conv_ready, ctanh_ready, feat_ready = (
            sem("m_pad_ready"), sem("m_conv_ready"), sem("m_ctanh_ready"), sem("m_feat_ready"))
        ztanh_ready, gate_ready = sem("m_ztanh_ready"), sem("m_gate_ready")
        g_ps, gm_ready = sem("m_g_ps"), sem("m_gm_ready")
        xsT_ps, xdt_ready = sem("m_xsT_ps"), sem("m_xdt_ready")
        steps_ready, d_ps, decay_ready, mix_ready = (
            sem("m_steps_ready"), sem("m_d_ps"), sem("m_decay_ready"), sem("m_mix_ready"))
        y_ps, yg_ready, yg2_ready, out_ps = sem("m_y_ps"), sem("m_yg_ready"), sem("m_yg2_ready"), sem("m_out_ps")
        ms_ready, r_ready, hm_ready, hms_ready = (
            sem("m_ms_ready"), sem("m_r_ready"), sem("m_hm_ready"), sem("m_hms_ready"))
        xm_ready, xmT_ps, xmT_used, xm_stored, x_added = (
            sem("m_xm_ready"), sem("m_xmT_ps"), sem("m_xmT_used"), sem("m_xm_stored"), sem("m_x_added"))

        SLOTS = GROUP + 3

        def groups(eng, ahead, behind, start=None):
            if start:
                start()
            for s in range(SLOTS):
                ahead(0, 0, s, 0)
            behind(0, 0, True, True)
            with eng.Fori(0, GROUPS // 2 - 1) as m:
                behind(m * 2 + 1, 1, False, True)
                behind(m * 2 + 2, 0, False, True)
            behind(GROUPS - 1, 1, False, False)

        def stages(s, *late):
            return [(stage, s - n) for stage, n in late if 0 <= s - n < GROUP]

        block = ctx.enter_context(nc.Block())

        @block.sync
        def _(sp):
            def load(dst, src, done):
                sp.dma_start(dst, src).then_inc(done, 16)

            def load_x(lo, hi, done):
                load(g.X[:, lo:hi, :], g.dram["x"].rearrange("b t d -> t b d")[:, lo:hi, :], done)
            load_x(0, GROUP, g.x_loaded)
            load(norm_w[:], g.dram["norm_mamba_w"], loaded_in)
            load(win[:], g.dram["in_proj_w"], loaded_in)
            load(dt_bias[:], g.dram["dt_bias"].partition_broadcast(P), loaded_in)
            load(a_neg[:], g.dram["A_log"].partition_broadcast(P), loaded_in)
            load(conv_w[:], g.dram["conv_w"], loaded_in)
            load(conv_b[:], g.dram["conv_b"], loaded_in)
            load_x(GROUP, SEQS, x_rest_loaded)
            for h in range(2):
                load(d_skip[HD * h:HD * h + HD, :], g.dram["D"][h].partition_broadcast(HD), loaded)
            load(wout[:], g.dram["out_proj_w"], loaded)
            load(ssm_w[:], g.dram["ssm_norm_w"], loaded)
            load(moe_w[:], g.dram["norm_moe_w"], loaded)
            load(gate_w[:], g.dram["gate_w"], loaded)
            for e in range(3, EXPERTS - 2):
                sp.dma_start(g.moe_w2[:, e], g.dram["moe_w2"][e]).then_inc(g.w2_loaded, 16)
            with sp.Fori(0, GROUPS) as i:
                sp.wait_ge(xm_ready, i * GROUP + GROUP)
                sp.dma_start(g.xm_rows.rearrange("(q p) d -> p q d", p=P)[:, bass.ds(i * GROUP, GROUP), :], xm_tok[:])\
                    .then_inc(xm_stored, 16)
            sp.wait_ge(xm_stored, 16 * GROUPS)
        LOADS_IN, LOADS = 16 * 6, 16 * 6

        @block.gpsimd
        def _(pool):
            nc.gpsimd.memset(g.ident[:], 0.0).then_inc(pool_done, 1)
            nc.gpsimd.memset(g.upto[:], 1.0).then_inc(pool_done, 1)
            nc.gpsimd.memset(g.after[:], 1.0).then_inc(pool_done, 1)
            nc.gpsimd.memset(g.ones[:], 1.0).then_inc(consts, 1)
            nc.gpsimd.memset(g.neg_half[:], -0.5).then_inc(consts, 1)
            for e in range(EXPERTS):
                nc.gpsimd.memset(g.iota8[:, e:e + 1], float(e))
            nc.gpsimd.memset(xpad[:], 0.0).then_inc(consts, 1)
            pool.wait_ge(pool_done, 3)
            nc.gpsimd.affine_select(out=g.ident[:], in_=g.ident[:], compare_op=ALU.not_equal, fill=1.0,
                                    base=0, pattern=[[-1, P]], channel_multiplier=1).then_inc(consts, 1)
            nc.gpsimd.affine_select(out=g.upto[:], in_=g.upto[:], compare_op=ALU.is_ge, fill=0.0,
                                    base=0, pattern=[[1, P]], channel_multiplier=-1).then_inc(consts, 1)
            nc.gpsimd.affine_select(out=g.after[:], in_=g.after[:], compare_op=ALU.is_gt, fill=0.0,
                                    base=0, pattern=[[-1, P]], channel_multiplier=1).then_inc(consts, 1)
            pool.wait_ge(consts, 6)
            p = nc.gpsimd

            def steps(i, b, j):
                p.tensor_tensor(steps_da[:], bc(da[:, b, HEADS * j:HEADS * j + HEADS].unsqueeze(2), [P, HEADS, P]),
                                bc(g.upto[:].unsqueeze(1), [P, HEADS, P]), ALU.mult).then_inc(steps_ready, 1)

            def roots(lo, hi, done):
                for n, (var, rstd) in enumerate(((ln_var, ln_rstd), (rms_var, rms_rstd))):
                    pool.wait_ge(var_ready, done + n + 1)
                    p.tensor_tensor(rstd[:, lo:hi], var[:, lo:hi], bc(g.neg_half[:, 0:1], [P, hi - lo]), ALU.pow)\
                        .then_inc(rstd_ready, 1)

            def ahead(i, b, s, before):
                if s == 0 and not before:
                    roots(0, GROUP, 0)
                    roots(GROUP, SEQS, 2)
                if s == SLOTS - 1:
                    pool.wait_ge(dt_ready, i + 1)
                    steps(i, b, 0)

            def behind(i, b, opening, more):
                for s in range(SLOTS):
                    j = s - 3
                    if j >= 0:
                        pool.wait_ge(ms_ready, i * 2 * GROUP + (2 * j + 1))
                        p.tensor_tensor(sc[:, j % 2, 1:2], sc[:, j % 2, 0:1], g.neg_half[:, 0:1], ALU.pow).then_inc(r_ready, 1)
                        pool.wait_ge(hm_ready, i * GROUP + (j + 1))
                        p.tensor_tensor(g.X[:, i * GROUP + j, :], g.X[:, i * GROUP + j, :], hm[:, j % 2, :],
                                        ALU.add).then_inc(x_added, 1)
                        pool.wait_ge(ms_ready, i * 2 * GROUP + (2 * j + 2))
                        p.tensor_tensor(sc[:, j % 2, 3:4], sc[:, j % 2, 2:3], g.neg_half[:, 0:1], ALU.pow).then_inc(r_ready, 1)
                    if s + 1 < GROUP:
                        pool.wait_ge(d_ps, i * GROUP + (s + 1))
                        steps(i, b, s + 1)
                    if more:
                        ahead(i + 1, 1 - b, s, 1)
            groups(pool, ahead, behind)

        @block.tensor
        def _(pe):
            pe.wait_ge(consts, 6)
            pe.wait_ge(loaded_in, LOADS_IN)

            def project(i, n):
                if n == 1:
                    pe.wait_ge(dt_abs, i + 1)
                elif 2 <= n < 2 + NCONV:
                    pe.wait_ge(proj_used_a, i * NCONV + (n - 1))
                elif n >= 2 + NCONV:
                    pe.wait_ge(proj_used_v, i * CI + (n - 2 - NCONV + 1))
                start = 2 * DI if n == 0 else DI + P * (n - 1) if n < NCONV else P * (n - NCONV)
                for k in range(KD):
                    last = nc.tensor.matmul(bank_a[(n + 1) % 2][:], win[:, k, start:start + P], h_feat[:, k, :],
                                            start=(k == 0), stop=(k == KD - 1))
                last.then_inc(proj_ps, 1)

            def ahead(i, b, s, before, opening=False):
                if s == 1:
                    if before and opening:
                        pe.wait_ge(proj_used_v, CI)
                    elif before:
                        pe.wait_ge(xmT_used, i * KD - KD)
                    for j in range(GROUP):
                        pe.wait_ge(h_ready, i * GROUP + (j + 1))
                        for k in range(KD):
                            last = nc.tensor.transpose(bank_a[k][:, P * j:P * j + P], h_tok[:, j, P * k:P * k + P],
                                                       g.ident[:])
                    last.then_inc(hT_ps, 1)
                    pe.wait_ge(hT_ready, i * KD + KD)
                    for j in range(GROUP):
                        for k in range(KD):
                            last = nc.tensor.matmul(bank_a[0][:, HEADS * j:HEADS * j + HEADS],
                                                    h_feat[:, k, P * j:P * j + P], win[:, k, 2 * DI + 2 * NS:],
                                                    start=(k == 0), stop=(k == KD - 1))
                    last.then_inc(dt_ps, 1)
                for n in {1: (0,), 2: (1, 2), 3: (3, 4), 4: (5, 6), 5: (7,), 6: (8,)}.get(s, ()):
                    project(i, n)

            def behind(i, b, opening, more):
                def stage_a(j):
                    if j == 0:
                        pe.wait_ge(feat_ready, i * (2 + CI) + 2)
                        if not opening:
                            pe.wait_ge(logits_used, i)
                    else:
                        pe.wait_ge(gm_ready, i * GROUP + j)
                    tok = slice(P * j, P * j + P)
                    nc.tensor.matmul(bank_g[:, 0:P], bc_feat[b][:, 0, tok], bc_feat[b][:, 1, tok], start=True, stop=True)\
                        .then_inc(g_ps, 1)
                    if j == 0:
                        pe.wait_ge(feat_ready, i * (2 + CI) + 2 + CI)
                    else:
                        pe.wait_ge(xdt_ready, i * GROUP + j)
                    for c in range(CI):
                        last = nc.tensor.transpose(bank_x[:, P * c:P * c + P], xs_feat[b][:, c, tok], g.ident[:])
                    last.then_inc(xsT_ps, 1)
                    pe.wait_ge(steps_ready, i * GROUP + (j + 1))
                    if j:
                        pe.wait_ge(decay_ready, i * GROUP + j)
                    for n in range(2):
                        hs = slice(HEADS // 2 * n, HEADS // 2 * (n + 1))
                        last = nc.tensor.matmul(bank_d[:, hs, :], g.after[:], steps_da[:, hs, :], start=True, stop=True)
                    last.then_inc(d_ps, 1)

                def stage_b(j):
                    pe.wait_ge(mix_ready, i * GROUP + (j + 1))
                    pe.wait_ge(xdt_ready, i * GROUP + (j + 1))
                    if j:
                        pe.wait_ge(yg_ready, i * GROUP + j)
                    for h in range(HEADS):
                        last = nc.tensor.matmul(bank_y[HD * (h % 2):HD * (h % 2) + HD, h // 2, :],
                                                xdt[:, j % 2, HD * h:HD * h + HD], decay[:, j % 2, h, :],
                                                start=True, stop=True)
                    last.then_inc(y_ps, 1)

                def stage_c(j):
                    pe.wait_ge(yg2_ready, i * GROUP + (j + 1))
                    pe.wait_ge(wout_ready, 1)
                    if j:
                        pe.wait_ge(hm_ready, i * GROUP + j)
                    for c in range(CI):
                        nc.tensor.matmul(bank_o[:, SS_COL:SS_COL + 1], yg2[:, j % 2, c, :], g.ones[:, 0:1],
                                         start=(c == 0), stop=(c == CI - 1))
                    for c in range(CI):
                        last = nc.tensor.matmul(bank_o[:, 0:D], yg[:, j % 2, c, :], wout[:, c, :],
                                                start=(c == 0), stop=(c == CI - 1))
                    last.then_inc(out_ps, 1)
                for s in range(SLOTS):
                    for stage, j in stages(s, (stage_a, 0)):
                        stage(j)
                    if s == 0 and not opening:
                        turn_xm(i - 1, i)
                    if s == 4 and not opening:
                        router(i - 1, i)
                    if more:
                        ahead(i + 1, 1 - b, s, 1, opening)
                    for stage, j in stages(s, (stage_b, 1), (stage_c, 2)):
                        stage(j)
                if not more:
                    turn_xm(i, i)
                    router(i, i)

            def router(i, during):
                pe.wait_ge(gm_ready, during * GROUP + GROUP)
                pe.wait_ge(wout_ready, 1)
                pe.wait_ge(xmT_used, i * KD + KD)
                pe.wait_ge(logits_used, i + 1)
                for j in range(GROUP):
                    for k in range(KD):
                        last = nc.tensor.matmul(bank_g[:, P + EXPERTS * j:P + EXPERTS * (j + 1)],
                                                g.xm_feat[:, k, bass.ds(i * GT + P * j, P)], gate_w[:, k, :],
                                                start=(k == 0), stop=(k == KD - 1))
                last.then_inc(logits_ps, 1)

            def turn_xm(i, ahead_of):
                pe.wait_ge(proj_used_v, ahead_of * CI + CI)
                for j in range(GROUP):
                    pe.wait_ge(xm_ready, i * GROUP + (j + 1))
                    for k in range(KD):
                        last = nc.tensor.transpose(bank_a[k][:, P * j:P * j + P], xm_tok[:, j, P * k:P * k + P], g.ident[:])
                last.then_inc(xmT_ps, 1)
            groups(pe, ahead, behind)

        @block.scalar
        def _(act):
            a = nc.scalar

            def start():
                act.wait_ge(loaded_in, LOADS_IN)
                act.wait_ge(a_cut, 1)
                act.sem_inc(logits_used, 1)
                a.activation(a_neg[:], a_neg[:], ACT.Exp).then_inc(g.a_exp, 1)

            def conv_tanh(i, n):
                act.wait_ge(conv_ready, i * NCONV + (n + 1))
                a.activation(tanh[:, n % 2, :], conv[:, n % 2, :, :].rearrange("p a b -> p (a b)"), ACT.Tanh)\
                    .then_inc(ctanh_ready, 1)

            def softplus_exp(i, n):
                act.wait_ge(dt_abs, i + 1)
                a.activation(dtw[:, 2, :], dtw[:, 1, :], ACT.Exp, scale=-1.0).then_inc(dt_exp, 1)

            def pad(i, n):
                act.wait_ge(proj_ps, i * NPROJ + (n + 1))
                a.activation(xpad[:, n - 1 if n else CI, :, PAD:],
                             bank_a[(n + 1) % 2][:].rearrange("p (a b) -> p a b", a=GROUP), ACT.Copy).then_inc(proj_used_a, 1)

            def gate_tanh(i, c):
                n = NCONV + c
                act.wait_ge(proj_ps, i * NPROJ + (n + 1))
                a.activation(gate_t[:, c % 2, :], bank_a[(n + 1) % 2][:], ACT.Tanh, scale=0.5).then_inc(ztanh_ready, 1)

            def ahead(i, b, s, before):
                if s == 0:
                    act.wait_ge(rstd_ready, 4 if before else 2)
                    for j in range(GROUP):
                        act.wait_ge(u_ready, i * GROUP + (j + 1))
                        a.activation(h_tok[:, j, :], u_tok[b][:, j, :], ACT.Copy,
                                     scale=rms_rstd[:, bass.ds(i * GROUP + j, 1)]).then_inc(h_ready, 1)
                if s == 1:
                    act.wait_ge(hT_ps, i + 1)
                    for k in range(KD):
                        a.activation(h_feat[:, k, :], bank_a[k][:], ACT.Copy, scale=norm_w[:, k:k + 1]).then_inc(hT_ready, 1)
                for kind, n in {1: ((pad, 0), (softplus_exp, 0)),
                                2: ((pad, 1), (pad, 2)),
                                3: ((pad, 3), (pad, 4), (conv_tanh, 0), (conv_tanh, 1)),
                                4: ((gate_tanh, 0), (gate_tanh, 1), (conv_tanh, 2)),
                                5: ((gate_tanh, 2), (conv_tanh, 3)),
                                6: ((gate_tanh, 3), (conv_tanh, 4))}.get(s, ()):
                    kind(i, n)

            def behind(i, b, opening, more):
                if opening:
                    act.wait_ge(loaded, LOADS)

                def stage_a(j):
                    act.wait_ge(d_ps, i * GROUP + (j + 1))
                    a.activation(decay[:, j % 2, :, :], bank_d[:], ACT.Exp).then_inc(decay_ready, 1)

                def stage_c(j):
                    act.wait_ge(yg_ready, i * GROUP + (j + 1))
                    a.activation(yg2[:, j % 2, :, :], yg[:, j % 2, :, :], ACT.Square).then_inc(yg2_ready, 1)

                def stage_d(j):
                    act.wait_ge(hm_ready, i * GROUP + (j + 1))
                    a.activation(hm_sq[:], hm[:, j % 2, :], ACT.Square, accum_out=sc[:, j % 2, 2:3]).then_inc(hms_ready, 1)
                for s in range(SLOTS):
                    for stage, j in stages(s, (stage_a, 0)):
                        stage(j)
                    if s == 0 and not opening:
                        store_xm(i - 1)
                    for stage, j in stages(s, (stage_d, 3), (stage_c, 2)):
                        stage(j)
                    if s == 5 and not opening:
                        keep_logits(i - 1)
                    if more:
                        ahead(i + 1, 1 - b, s, 1)
                if not more:
                    store_xm(i)
                    keep_logits(i)

            def keep_logits(i):
                act.wait_ge(logits_ps, i + 1)
                a.copy(g.moe_logits[:, bass.ds(i * GROUP, GROUP), :].rearrange("p q e -> p (q e)"), bank_g[:, P:])\
                    .then_inc(logits_used, 1)

            def store_xm(i):
                act.wait_ge(xmT_ps, i + 1)
                for k in range(KD):
                    a.activation(g.xm_feat[:, k, bass.ds(i * GT, GT)], bank_a[k][:], ACT.Copy, scale=moe_w[:, k:k + 1])\
                        .then_inc(xmT_used, 1)
            groups(act, ahead, behind, start)

        @block.vector
        def _(dve):
            v = nc.vector
            link = Links(dve, vec)

            def start():
                norm_stats(0, GROUP, g.x_loaded)
                dve.wait_ge(loaded_in, LOADS_IN)
                v.tensor_scalar(a_neg[:], a_neg[:], 80.0, None, ALU.min).then_inc(a_cut, 1)
                dve.wait_ge(g.a_exp, 1)
                v.tensor_scalar(a_neg[:], a_neg[:], -1.0, None, ALU.mult).then_inc(vec, 1)
                v.tensor_scalar(conv_w[:], conv_w[:], 0.5, None, ALU.mult).then_inc(vec, 1)
                link.n += 2
                link(v.tensor_scalar(conv_b[:], conv_b[:], 0.5, None, ALU.mult))
                dve.wait_ge(consts, 6)

            def norm_stats(lo, hi, x_here):
                dve.wait_ge(x_here, 16)
                q = slice(lo, hi)
                for n in range(lo, hi):
                    ins = v.bn_stats(stats[:, n, :], g.X[:, n, :])
                link(ins)
                merge_stats(v, link, stats[:, q], mean_var[:, q], halves[:, :, q])
                v.tensor_scalar(ln_var[:, q], mean_var[:, q, 1], LN_EPS, None, ALU.add).then_inc(var_ready, 1)

            def norm_squares(lo, hi, rstds):
                dve.wait_ge(rstd_ready, rstds)
                q = slice(lo, hi)
                link(v.tensor_tensor(ms_a[:, q], mean_var[:, q, 1], ln_rstd[:, q], ALU.mult))
                link(v.tensor_tensor(ms_b[:, q], ms_a[:, q], ln_rstd[:, q], ALU.mult))
                v.tensor_scalar(rms_var[:, q], ms_b[:, q], RMS_EPS, None, ALU.add).then_inc(var_ready, 1)

            def norm_apply(i, b):
                for j in range(GROUP):
                    seq = bass.ds(i * GROUP + j, 1)
                    v.tensor_scalar(u_tok[b][:, j, :], g.X[:, i * GROUP + j, :],
                                    mean_var[:, seq, 0:1].rearrange("p a b -> p (a b)"), ln_rstd[:, seq],
                                    ALU.subtract, ALU.mult).then_inc(u_ready, 1)

            def softplus(i, b):
                dve.wait_ge(dt_ps, i + 1)
                link(v.tensor_tensor(dtw[:, 0, :].rearrange("p (j h) -> p j h", j=GROUP),
                                     bank_a[0][:, 0:GROUP * HEADS].rearrange("p (j h) -> p j h", j=GROUP),
                                     bc(dt_bias[:].unsqueeze(1), [P, GROUP, HEADS]), ALU.add))
                v.scalar_tensor_tensor(out=dtw[:, 1, :], in0=dtw[:, 0, :], scalar=-1.0, in1=dtw[:, 0, :],
                                       op0=ALU.mult, op1=ALU.max).then_inc(dt_abs, 1)

            def softplus_end(i, b):
                dve.wait_ge(dt_exp, i + 1)
                link(v.tensor_scalar(dtw[:, 3, :], dtw[:, 2, :], 2.0, None, ALU.add))
                link(v.reciprocal(dtw[:, 4, :], dtw[:, 3, :]))
                link(v.tensor_tensor(dtw[:, 3, :], dtw[:, 2, :], dtw[:, 4, :], ALU.mult))
                link(v.tensor_tensor(dtw[:, 4, :], dtw[:, 3, :], dtw[:, 3, :], ALU.mult))
                terms = log1p_terms(8)
                link(v.tensor_scalar(dtw[:, 5, :], dtw[:, 4, :], terms[0], None, ALU.mult))
                for c in terms[1:]:
                    link(v.scalar_tensor_tensor(out=dtw[:, 5, :], in0=dtw[:, 5, :], scalar=c, in1=dtw[:, 4, :],
                                                op0=ALU.add, op1=ALU.mult))
                link(v.scalar_tensor_tensor(out=dtw[:, 5, :], in0=dtw[:, 5, :], scalar=1.0, in1=dtw[:, 3, :],
                                            op0=ALU.add, op1=ALU.mult))
                link(v.tensor_scalar(dtw[:, 3, :], dtw[:, 0, :], 0.0, 0.5, ALU.max, ALU.mult))
                link(v.tensor_tensor(dtw[:, 4, :], dtw[:, 3, :], dtw[:, 5, :], ALU.add))
                link(v.tensor_scalar(dt[:, b, :], dtw[:, 4, :], 2.0, None, ALU.mult))
                link(v.tensor_tensor(dtw[:, 3, :].rearrange("p (j h) -> p j h", j=GROUP),
                                     dt[:, b, :].rearrange("p (j h) -> p j h", j=GROUP),
                                     bc(a_neg[:].unsqueeze(1), [P, GROUP, HEADS]), ALU.mult))
                v.tensor_scalar(da[:, b, :], dtw[:, 3, :], -1e30, None, ALU.max).then_inc(dt_ready, 1)

            def taps(i, *tiles):
                for n in tiles:
                    dve.wait_ge(proj_used_a, i * NCONV + (n + 1))
                    if n >= 2:
                        dve.wait_ge(feat_ready, i * (2 + CI) + n)
                    m = n - 1 if n else CI
                    ins = v.tensor_scalar(conv[:, n % 2], xpad[:, m, :, 0:P], conv_w[:, m, 0:1], conv_b[:, m:m + 1],
                                          ALU.mult, ALU.add)
                link(ins)
                for k in range(1, TAPS):
                    for n in tiles:
                        m = n - 1 if n else CI
                        ins = v.scalar_tensor_tensor(out=conv[:, n % 2], in0=xpad[:, m, :, k:k + P],
                                                     scalar=conv_w[:, m, k:k + 1], in1=conv[:, n % 2],
                                                     op0=ALU.mult, op1=ALU.add)
                        if k == TAPS - 1:
                            ins.then_inc(conv_ready, 1)
                    if k < TAPS - 1:
                        link(ins)

            def silu(i, b, n):
                dve.wait_ge(ctanh_ready, i * NCONV + (n + 1))
                for out, rows in (((bc_feat[b][:, 0, :], slice(0, NS)), (bc_feat[b][:, 1, :], slice(NS, 2 * NS))) if n == 0
                                  else ((xs_feat[b][:, n - 1, :], slice(0, P)),)):
                    v.scalar_tensor_tensor(out=out, in0=tanh[rows, n % 2, :], scalar=1.0,
                                           in1=conv[rows, n % 2, :, :].rearrange("p a b -> p (a b)"),
                                           op0=ALU.add, op1=ALU.mult).then_inc(feat_ready, 1)

            def gates(i, b, c):
                dve.wait_ge(ztanh_ready, i * CI + (c + 1))
                v.scalar_tensor_tensor(out=gate[b][:, c, :], in0=gate_t[:, c % 2, :], scalar=1.0,
                                       in1=bank_a[(NCONV + c + 1) % 2][:], op0=ALU.add, op1=ALU.mult).then_inc(proj_used_v, 1)

            def ahead(i, b, s, before):
                if s == 0:
                    if not before:
                        norm_squares(0, GROUP, 1)
                    norm_apply(i, b)
                    if not before:
                        norm_stats(GROUP, SEQS, x_rest_loaded)
                if s == 1:
                    softplus(i, b)
                    if not before:
                        dve.wait_ge(loaded, LOADS)
                        v.tensor_tensor(wout[:], wout[:], bc(ssm_w[:].unsqueeze(2), [P, CI, D]), ALU.mult)\
                            .then_inc(wout_ready, 1)
                        norm_squares(GROUP, SEQS, 3)
                if s == 2:
                    softplus_end(i, b)
                if s == 3:
                    taps(i, 0, 1)
                if s == 4:
                    silu(i, b, 0)
                    silu(i, b, 1)
                    taps(i, 2)
                    gates(i, b, 0)
                if s == 5:
                    gates(i, b, 1)
                    silu(i, b, 2)
                    taps(i, 3)
                if s == 6:
                    taps(i, 4)
                    gates(i, b, 2)
                    silu(i, b, 3)
                    silu(i, b, 4)
                    gates(i, b, 3)

            def behind(i, b, opening, more):
                if opening:
                    assert link.n == VEC_START + VEC_AHEAD, link.n
                link.restart(i * (VEC_AHEAD + VEC_BEHIND) + (VEC_START + VEC_AHEAD))

                def stage_a(j):
                    dve.wait_ge(g_ps, i * GROUP + (j + 1))
                    v.tensor_tensor(gm[:, j % 2, :], bank_g[:, 0:P], g.upto[:], ALU.mult).then_inc(gm_ready, 1)
                    dve.wait_ge(xsT_ps, i * GROUP + (j + 1))
                    v.tensor_tensor(xdt[:, j % 2, :].rearrange("p (h d) -> p h d", h=HEADS),
                                    bank_x[:].rearrange("p (h d) -> p h d", h=HEADS),
                                    bc(dt[:, b, HEADS * j:HEADS * j + HEADS].unsqueeze(2), [P, HEADS, HD]), ALU.mult)\
                        .then_inc(xdt_ready, 1)

                def stage_b(j):
                    dve.wait_ge(gm_ready, i * GROUP + (j + 1))
                    dve.wait_ge(decay_ready, i * GROUP + (j + 1))
                    v.tensor_tensor(decay[:, j % 2, :, :], decay[:, j % 2, :, :],
                                    bc(gm[:, j % 2, :].unsqueeze(1), [P, HEADS, P]), ALU.mult).then_inc(mix_ready, 1)

                def stage_c(j):
                    tok = slice(P * j, P * j + P)
                    dve.wait_ge(y_ps, i * GROUP + (j + 1))
                    for c in range(CI):
                        ins = v.scalar_tensor_tensor(out=y_feat[:, c, :], in0=xs_feat[b][:, c, tok],
                                                     scalar=d_skip[:, c:c + 1], in1=bank_y[:, c, :],
                                                     op0=ALU.mult, op1=ALU.add)
                    link(ins)
                    v.scalar_tensor_tensor(out=yg[:, j % 2, :, :], in0=y_feat[:], scalar=0.5, in1=gate[b][:, :, tok],
                                           op0=ALU.mult, op1=ALU.mult).then_inc(yg_ready, 1)

                def stage_d(j):
                    dve.wait_ge(out_ps, i * GROUP + (j + 1))
                    v.tensor_scalar(sc[:, j % 2, 0:1], bank_o[:, SS_COL:SS_COL + 1], 1.0 / DI, RMS_EPS,
                                    ALU.mult, ALU.add).then_inc(ms_ready, 1)

                def stage_d2(j):
                    dve.wait_ge(r_ready, i * 2 * GROUP + (2 * j + 1))
                    v.scalar_tensor_tensor(out=hm[:, j % 2, :], in0=bank_o[:, 0:D], scalar=sc[:, j % 2, 1:2],
                                           in1=u_tok[b][:, j, :], op0=ALU.mult, op1=ALU.add).then_inc(hm_ready, 1)

                def stage_d3(j):
                    dve.wait_ge(hms_ready, i * GROUP + (j + 1))
                    v.tensor_scalar(sc[:, j % 2, 2:3], sc[:, j % 2, 2:3], 1.0 / D, RMS_EPS, ALU.mult, ALU.add)\
                        .then_inc(ms_ready, 1)

                def stage_d4(j):
                    if j == 0 and not opening:
                        dve.wait_ge(xm_stored, i * 16)
                    dve.wait_ge(r_ready, i * 2 * GROUP + (2 * j + 2))
                    v.tensor_scalar(xm_tok[:, j, :], hm[:, j % 2, :], sc[:, j % 2, 3:4], None, ALU.mult).then_inc(xm_ready, 1)
                for s in range(SLOTS):
                    for stage, j in stages(s, (stage_b, 1), (stage_a, 0), (stage_c, 2), (stage_d, 3), (stage_d2, 3),
                                           (stage_d3, 3)):
                        stage(j)
                    if more:
                        ahead(i + 1, 1 - b, s, 1)
                    for stage, j in stages(s, (stage_d4, 3)):
                        stage(j)
                assert link.n == VEC_BEHIND + (VEC_AHEAD if more else 0), link.n
            groups(dve, ahead, behind, start)


def route_pe(nc, pe, g, r):
    pe.wait_ge(r.loaded, r.loads)
    for n in range(GROUPS):
        if n >= 2:
            pe.wait_ge(r.logits_used, n - 1)
        for k in range(KD):
            last = nc.tensor.matmul(r.bank_l[n % 2][0:EXPERTS, :], r.gate_w[:, k, :],
                                    g.xm_feat[:, k, GT * n:GT * n + GT], start=(k == 0), stop=(k == KD - 1))
        last.then_inc(r.logits_ps, 1)
    pe.wait_ge(r.logits_used, GROUPS)
    for q in range(SEQS):
        last = nc.tensor.transpose(r.bank_lt[:, q, :], r.logits_e[:, P * q:P * q + P], g.ident[0:EXPERTS, 0:EXPERTS])
    last.then_inc(r.logits_t, 1)


def route_act(nc, act, g, r):
    for n in range(GROUPS):
        act.wait_ge(r.logits_ps, n + 1)
        nc.scalar.copy(r.logits_e[:, GT * n:GT * n + GT], r.bank_l[n % 2][0:EXPERTS, :]).then_inc(r.logits_used, 1)


def route_exps(nc, act, g, r, full):
    act.wait_ge(r.second_less_first, 1)
    nc.scalar.activation(r.work[:, 1, :], r.work[:, 0, :], ACT.Exp).then_inc(r.exps, 1)
    if full:
        nc.scalar.activation(r.all_exp[:], r.logits[:], ACT.Exp).then_inc(r.exps, 1)


def route_dve(nc, dve, g, r, link, full):
    v = nc.vector
    if full:
        dve.wait_ge(r.logits_t, 1)
        link(v.tensor_copy(r.logits[:], r.bank_lt[:]))
    for q in range(SEQS):
        ins = v.max(r.top[:, q, :], r.logits[:, q, :])
    link(ins)
    for q in range(SEQS):
        ins = v.max_index(r.top_at[:, q, :], r.top[:, q, :], r.logits[:, q, :])
    link(ins)
    link(v.tensor_copy(r.at[:], r.top_at[:, :, 0:2]))
    for n in range(2):
        link(v.tensor_tensor(r.hot[:, n], bc(r.at[:, :, n:n + 1], [P, SEQS, EXPERTS]),
                             bc(g.iota8[:].unsqueeze(1), [P, SEQS, EXPERTS]), ALU.is_equal))
    dve.sem_inc(r.hot_ready, 1)
    if full:
        link(v.tensor_tensor(r.logits[:], r.logits[:], bc(r.top[:, :, 0:1], [P, SEQS, EXPERTS]), ALU.subtract))
    v.tensor_tensor(r.work[:, 0, :], r.top[:, :, 1], r.top[:, :, 0], ALU.subtract).then_inc(r.second_less_first, 1)
    dve.wait_ge(r.exps, 2 if full else 1)
    if full:
        link(v.tensor_reduce(r.work[:, 2, :], r.all_exp[:], AX.X, ALU.add))
    else:
        link(v.tensor_scalar(r.work[:, 2, :], r.work[:, 1, :], 1.0, None, ALU.add))
    link(v.reciprocal(r.prob[:, 0, :], r.work[:, 2, :]))
    link(v.tensor_tensor(r.prob[:, 1, :], r.prob[:, 0, :], r.work[:, 1, :], ALU.mult))


def count_buffers(ctx, nc, g, r, tag, bank):
    def sb(name, *shape):
        return ctx.enter_context(nc.sbuf_tensor(tag + name, list(shape), F32))
    r.before = sb("before", P, P)
    r.counts, r.carry, r.offset = (sb(name, P, EXPERTS, BLOCKS + 1) for name in ("counts", "carry", "offset"))
    r.slot = sb("slot", P, BLOCKS, EXPERTS)
    r.bank_c = bank.rearrange("p (a b) -> p a b", a=2)
    r.count_consts, r.hot_ready, r.counts_ps = g.sem(tag + "count_consts"), g.sem(tag + "hot_ready"), g.sem(tag + "counts_ps")


def count_pool(nc, pool, g, r):
    nc.gpsimd.memset(r.counts[:], 0.0).then_inc(r.count_consts, 1)
    nc.gpsimd.memset(r.carry[:], 1.0).then_inc(r.count_consts, 1)
    pool.wait_ge(r.count_consts, 2)
    nc.gpsimd.memset(r.carry[:, :, 0:1], 0.0).then_inc(r.count_consts, 1)
    nc.gpsimd.tensor_tensor(r.before[:], g.upto[:], g.ident[:], ALU.subtract).then_inc(r.count_consts, 1)


def count_pe(nc, pe, g, r):
    pe.wait_ge(r.count_consts, 4)
    pe.wait_ge(r.hot_ready, 1)
    hot = r.hot[:].rearrange("p n q e -> p (n q e)")
    nc.tensor.matmul(r.bank_c[:, 0, :], r.before[:], hot, start=True, stop=True)
    nc.tensor.matmul(r.bank_c[:, 1, :], g.ones[:], hot, start=True, stop=True).then_inc(r.counts_ps, 1)


def count_dve(nc, dve, g, r, link):
    v = nc.vector
    dve.wait_ge(r.counts_ps, 1)
    dve.wait_ge(r.count_consts, 4)
    link(v.tensor_copy(r.counts[:, :, 1:], r.bank_c[:, 1, :].rearrange("p (n e) -> p e n", e=EXPERTS)))
    link(v.tensor_tensor_scan(r.offset[:].rearrange("p e n -> p (e n)"), r.carry[:].rearrange("p e n -> p (e n)"),
                              r.counts[:].rearrange("p e n -> p (e n)"), 0.0, ALU.mult, ALU.add))
    link(v.tensor_tensor(r.slot[:], r.bank_c[:, 0, :].rearrange("p (n e) -> p n e", e=EXPERTS),
                         r.offset[:, :, 0:BLOCKS].rearrange("p e n -> p n e"), ALU.add))


def route_buffers(ctx, nc, g, tag):
    def sb(name, *shape, dt=F32):
        return ctx.enter_context(nc.sbuf_tensor(tag + name, list(shape), dt))
    r = Shared()
    r.top, r.top_at, r.at = sb("top", P, SEQS, 8), sb("top_at", P, SEQS, 8, dt=U32), sb("at", P, SEQS, 2)
    r.hot = sb("hot", P, 2, SEQS, EXPERTS)
    r.work, r.prob = sb("work", P, 3, SEQS), sb("prob", P, 2, SEQS)
    if tag == "s_":
        r.logits_ps, r.logits_used, r.logits_t = g.sem(tag + "logits_ps"), g.sem(tag + "logits_used"), g.sem(tag + "logits_t")
        r.gate_w = sb("gate_w", P, KD, EXPERTS)
        r.logits, r.all_exp = sb("logits", P, SEQS, EXPERTS), sb("all_exp", P, SEQS, EXPERTS)
    r.second_less_first, r.exps, r.link = g.sem(tag + "second_less_first"), g.sem(tag + "exps"), g.sem(tag + "link")
    return r


def moe_phase(nc, g):
    ROUND = float(3 << 22)
    with ExitStack() as ctx:
        def sb(name, *shape, dt=F32):
            return ctx.enter_context(nc.sbuf_tensor("e_" + name, list(shape), dt))

        def ps(name, *shape):
            return ctx.enter_context(nc.psum_tensor("e_" + name, list(shape), F32))

        sem = lambda name: g.sem("e_" + name)
        r = route_buffers(ctx, nc, g, "e_")
        w1 = sb("w1", P, EXPERTS, KD, FF)
        w2 = g.moe_w2
        x_tok, x_feat = sb("x_tok", P, 2, D), sb("x_feat", P, 2, KD, P)
        tanh = sb("tanh", P, 2, FF // 2)
        work = sb("rows", P, 2, FF)
        h_tok, h_feat = work[:, 0, :], work[:, 1, :].rearrange("p (f t) -> p f t", f=KF)
        y_tok = sb("y_tok", P, 2, D)
        fill = sb("fill", P, 6, EXPERTS)
        tile_iota, tile_cmp = sb("tile_iota", P, TILES), sb("tile_cmp", P, TILES, EXPERTS)
        tile_expert = sb("tile_expert", P, TILES, dt=I32)
        tile_end = sb("tile_end", P, TILES)
        dest, dest_tile, dest_row = sb("dest", P, BLOCKS), sb("dest_tile", P, BLOCKS), sb("dest_row", P, BLOCKS)
        seq_block = sb("seq_block", P, BLOCKS)
        row_iota, row_number = sb("row_iota", P, P), sb("row_number", P, 1)
        same = sb("same", P, BLOCKS, P, dt=BF16)
        tile_is = sb("tile_is", P, BLOCKS, TILES, dt=BF16)
        here = sb("here", P, BLOCKS, 2, TILES, dt=BF16)
        assert BLOCKS <= P
        slot_block, slot_token = sb("slot_block", P, TILES), sb("slot_token", P, TILES, dt=U32)
        bank_x = ps("bank_x", P, KD, P)
        bank_u = [ps(f"bank_u{n}", P, FF // 2) for n in range(2)]
        bank_h = [ps(f"bank_h{n}", P, KF // 2, P) for n in range(2)]
        bank_o = ps("bank_o", P, D)
        count_buffers(ctx, nc, g, r, "e_", ps("bank_c", P, 2 * BLOCKS * EXPERTS)[:])
        r.logits = g.moe_logits
        half_loaded, experts_here = [sem("half_loaded0"), sem("half_loaded1")], sem("experts_here")
        rows_asked = sem("rows_asked")
        iota_ready, table_ready = sem("iota_ready"), sem("table_ready")
        tile_is_ready, same_ready, slots_ready = sem("tile_is_ready"), sem("same_ready"), sem("slots_ready")
        rows_ps, here_ready, tokens_ps = sem("rows_ps"), sem("here_ready"), sem("tokens_ps")
        SAME = 8
        x_loaded = [sem("x_loaded0"), sem("x_loaded1")]
        xT_ps, x_ready, u_ps, tanh_ready, h_ready = sem("xT_ps"), sem("x_ready"), sem("u_ps"), sem("tanh_ready"), sem("h_ready")
        hT_ps, hT_ready_a, hT_ready_v, o_ps = sem("hT_ps"), sem("hT_ready_a"), sem("hT_ready_v"), sem("o_ps")
        y_ready, stored = sem("y_ready"), [sem("stored0"), sem("stored1")]
        PAIRS = (TILES - 1) // 2
        assert TILES == 2 * PAIRS + 1
        block = ctx.enter_context(nc.Block())

        def steps(eng, step):
            step(0, 0, True, False)
            with eng.Fori(0, PAIRS) as m:
                for b in range(2):
                    step(m * 2 + (b + 1), (b + 1) % 2, False, False)
            step(TILES, TILES % 2, False, True)

        @block.sync
        def _(sp):
            for half in range(2):
                if half:
                    sp.wait_ge(rows_asked, 1)
                loads = 0
                for e in range(EXPERTS // 2 * half, EXPERTS // 2 * (half + 1)):
                    sp.dma_start(w1[:, e], g.dram["moe_w1"][e]).then_inc(half_loaded[half], 16)
                    loads += 16
                    if e < 3 or e >= EXPERTS - 2:
                        sp.dma_start(w2[:, e], g.dram["moe_w2"][e]).then_inc(half_loaded[half], 16)
                        loads += 16
                sp.wait_ge(half_loaded[half], loads)
                if not half:
                    sp.wait_ge(g.w2_loaded, 16 * (EXPERTS - 5))
                sp.sem_inc(experts_here, EXPERTS // 2)

            def store(t, b):
                sp.wait_ge(y_ready, t + 2)
                sp.dma_start(g.slot_out[bass.ds(t * P, P), :], y_tok[:, b, :]).then_inc(stored[b], 16)
            with sp.Fori(0, PAIRS) as m:
                for b in range(2):
                    store(m * 2 + b, b)
            store(TILES - 1, 0)
            for b in range(2):
                sp.wait_ge(stored[b], 16 * ((TILES + 1 - b) // 2) + 16)

        @block.gpsimd
        def _(pool):
            p = nc.gpsimd
            count_pool(nc, pool, g, r)
            for t in range(TILES):
                p.memset(tile_iota[:, t:t + 1], float(t)).then_inc(iota_ready, 1)
            for n in range(BLOCKS):
                p.memset(seq_block[:, n:n + 1], float(n % SEQS)).then_inc(iota_ready, 1)
            pool.wait_ge(tile_is_ready, 1)
            p.tensor_tensor(here[:, :, 0, :], tile_is[:], bc(seq_block[:].unsqueeze(2), [P, BLOCKS, TILES]), ALU.mult)\
                .then_inc(here_ready, 1)
            pool.wait_ge(slots_ready, 1)
            for t in range(TILES + 1):
                if t >= 2:
                    pool.wait_ge(xT_ps, t - 1)
                p.indirect_dma_start(x_tok[:, t % 2, :], None, g.xm_rows,
                                     bass.IndirectOffsetOnAxis(ap=slot_token[:, t % TILES:t % TILES + 1], axis=0))\
                    .then_inc(x_loaded[t % 2], 16)
                if t == 2:
                    pool.sem_inc(rows_asked, 1)

        @block.tensor
        def _(pe):
            pe.wait_ge(r.count_consts, 4)
            nc.tensor.matmul(bank_x[:, 0, :], g.ones[:], r.before[:], start=True, stop=True)
            nc.tensor.matmul(bank_x[:, 1, 0:1], r.before[:], g.ones[:, 0:1], start=True, stop=True).then_inc(rows_ps, 1)
            count_pe(nc, pe, g, r)
            pe.wait_ge(here_ready, 2)
            for n in range(BLOCKS):
                if n % SAME == 0:
                    pe.wait_ge(same_ready, n // SAME + 1)
                last = nc.tensor.matmul(bank_o[:, 0:2 * TILES], same[:, n, :],
                                        here[:, n].rearrange("p a t -> p (a t)"), start=(n == 0), stop=(n == BLOCKS - 1))
            last.then_inc(tokens_ps, 1)
            pe.wait_ge(table_ready, 1)

            def turn_x(t, b, loads):
                pe.wait_ge(x_loaded[b], loads)
                for k in range(KD):
                    last = nc.tensor.transpose(bank_x[:, k, :], x_tok[:, b, P * k:P * k + P], g.ident[:])
                last.then_inc(xT_ps, 1)
            turn_x(0, 0, 16)

            def step(s, b, first, last_step):
                if not first:
                    pe.wait_ge(h_ready, s * 2)
                    for f in range(KF):
                        last = nc.tensor.transpose(bank_h[f // (KF // 2)][:, f % (KF // 2), :], h_tok[:, P * f:P * f + P],
                                                   g.ident[:])
                        if f % (KF // 2) == KF // 2 - 1:
                            last.then_inc(hT_ps, 1)
                if not last_step:
                    pe.wait_ge(x_ready, s + 1)
                    e = pe.value_load(tile_expert[0:1, bass.ds(s, 1)], min_val=0, max_val=EXPERTS - 1)
                    pe.wait_ge(experts_here, e + 1)
                    for n in range(2):
                        for k in range(KD):
                            last = nc.tensor.matmul(bank_u[n][:], x_feat[:, b, k, :],
                                                    w1[:, bass.ds(e, 1), k, FF // 2 * n:FF // 2 * (n + 1)]
                                                    .rearrange("p a f -> p (a f)"),
                                                    start=(k == 0), stop=(k == KD - 1))
                        last.then_inc(u_ps, 1)
                    turn_x(s + 1, 1 - b, (s + 1) // 2 * 16 + 16 if first else (s + (1 + b) - 1) * 8 + 16)
                if not first:
                    e = pe.value_load(tile_expert[0:1, bass.ds(s - 1, 1)], min_val=0, max_val=EXPERTS - 1)
                    pe.wait_ge(hT_ready_a, s)
                    for f in range(KF):
                        if f == KF // 2:
                            pe.wait_ge(hT_ready_v, s)
                        if f == 0:
                            pe.wait_ge(y_ready, s)
                        last = nc.tensor.matmul(bank_o[:], h_feat[:, f, :],
                                                w2[:, bass.ds(e, 1), f, :].rearrange("p a d -> p (a d)"),
                                                start=(f == 0), stop=(f == KF - 1))
                    last.then_inc(o_ps, 1)
            steps(pe, step)

        @block.scalar
        def _(act):
            route_exps(nc, act, g, r, False)

            def x_evac(t, b):
                act.wait_ge(xT_ps, t + 1)
                for k in range(KD):
                    last = nc.scalar.activation(x_feat[:, b, k, :], bank_x[:, k, :], ACT.Copy, scale=g.moe_norm_w[:, k:k + 1])
                last.then_inc(x_ready, 1)
            x_evac(0, 0)

            def step(s, b, first, last_step):
                if not first:
                    act.wait_ge(hT_ps, s * 2 - 1)
                    nc.scalar.copy(h_feat[:, 0:KF // 2, :], bank_h[0][:]).then_inc(hT_ready_a, 1)
                if not last_step:
                    for n in range(2):
                        act.wait_ge(u_ps, s * 2 + (n + 1))
                        nc.scalar.activation(tanh[:, n, :], bank_u[n][:], ACT.Tanh, scale=0.5).then_inc(tanh_ready, 1)
                    x_evac(s + 1, 1 - b)
            steps(act, step)

        @block.vector
        def _(dve):
            v = nc.vector
            link = Links(dve, r.link)
            route_dve(nc, dve, g, r, link, False)
            dve.wait_ge(rows_ps, 1)
            link(v.tensor_copy(row_iota[:], bank_x[:, 0, :]))
            link(v.tensor_copy(row_number[:], bank_x[:, 1, 0:1]))
            dve.wait_ge(iota_ready, TILES + BLOCKS)
            count_dve(nc, dve, g, r, link)
            number, tiles, end, base, ones = (fill[:, n, :] for n in range(5))
            link(v.tensor_scalar(number, r.offset[:, :, BLOCKS], 1.0 / P, (P - 1) / (2.0 * P), ALU.mult, ALU.add))
            link(v.tensor_scalar(tiles, number, ROUND, None, ALU.add))
            link(v.tensor_scalar(tiles, tiles, ROUND, None, ALU.subtract))
            link(v.memset(ones, 1.0))
            link(v.tensor_tensor_scan(end, ones, tiles, 0.0, ALU.mult, ALU.add))
            link(v.tensor_tensor(base, end, tiles, ALU.subtract))
            link(v.tensor_scalar(base, base, float(P), None, ALU.mult))
            link(v.tensor_tensor(r.slot[:], r.slot[:], bc(base.unsqueeze(1), [P, BLOCKS, EXPERTS]), ALU.add))
            link(v.tensor_tensor(r.slot[:], r.slot[:], r.hot[:].rearrange("p n q e -> p (n q) e"), ALU.mult))
            link(v.tensor_reduce(dest[:], r.slot[:], AX.X, ALU.add))
            link(v.tensor_scalar(dest_tile[:], dest[:], 1.0 / P, -(P - 1) / (2.0 * P), ALU.mult, ALU.add))
            link(v.tensor_scalar(dest_tile[:], dest_tile[:], ROUND, None, ALU.add))
            link(v.tensor_scalar(dest_tile[:], dest_tile[:], ROUND, None, ALU.subtract))
            link(v.scalar_tensor_tensor(out=dest_row[:], in0=dest_tile[:], scalar=-float(P), in1=dest[:],
                                        op0=ALU.mult, op1=ALU.add))
            link(v.tensor_tensor(tile_is[:], bc(dest_tile[:].unsqueeze(2), [P, BLOCKS, TILES]),
                                 bc(tile_iota[:].unsqueeze(1), [P, BLOCKS, TILES]), ALU.is_equal))
            dve.sem_inc(tile_is_ready, 1)
            v.tensor_scalar(here[:, :, 1, :], tile_is[:], row_number[:, 0:1], None, ALU.mult).then_inc(here_ready, 1)
            for n in range(0, BLOCKS, SAME):
                v.tensor_tensor(same[:, n:n + SAME, :], bc(dest_row[:, n:n + SAME].unsqueeze(2), [P, SAME, P]),
                                bc(row_iota[:].unsqueeze(1), [P, SAME, P]), ALU.is_equal).then_inc(same_ready, 1)
            link(v.tensor_copy(g.dest_at[:], dest[:]))
            dve.wait_ge(tokens_ps, 1)
            link(v.tensor_copy(slot_block[:], bank_o[:, 0:TILES]))
            link(v.scalar_tensor_tensor(out=slot_token[:], in0=slot_block[:], scalar=float(P),
                                        in1=bank_o[:, TILES:2 * TILES], op0=ALU.mult, op1=ALU.add))
            dve.sem_inc(slots_ready, 1)
            link(v.tensor_tensor(tile_cmp[:], bc(tile_iota[:].unsqueeze(2), [P, TILES, EXPERTS]),
                                 bc(end.unsqueeze(1), [P, TILES, EXPERTS]), ALU.is_ge))
            link(v.tensor_reduce(tile_end[:], tile_cmp[:], AX.X, ALU.add))
            link(v.tensor_scalar(tile_end[:], tile_end[:], float(EXPERTS - 1), None, ALU.min))
            link(v.tensor_copy(tile_expert[:], tile_end[:]))
            link(v.tensor_scalar(g.moe_prob[:], r.prob[:], 0.5, None, ALU.mult))
            dve.sem_inc(table_ready, 1)
            dve.sem_inc(y_ready, 1)
            for b in range(2):
                dve.sem_inc(stored[b], 16)

            def step(s, b, first, last_step):
                if not first:
                    dve.wait_ge(hT_ps, s * 2)
                    v.tensor_copy(h_feat[:, KF // 2:, :], bank_h[1][:]).then_inc(hT_ready_v, 1)
                if not last_step:
                    for n in range(2):
                        dve.wait_ge(tanh_ready, s * 2 + (n + 1))
                        v.scalar_tensor_tensor(out=h_tok[:, FF // 2 * n:FF // 2 * (n + 1)], in0=tanh[:, n, :], scalar=1.0,
                                               in1=bank_u[n][:], op0=ALU.add, op1=ALU.mult).then_inc(h_ready, 1)
                if not first:
                    dve.wait_ge(o_ps, s)
                    dve.wait_ge(stored[1 - b], ((s - 1) // 2 * 16 + 16) if last_step else (s - 1 - (1 - b)) * 8 + 16)
                    v.tensor_copy(y_tok[:, 1 - b, :], bank_o[:]).then_inc(y_ready, 1)
            steps(dve, step)


def wkv_switch_phase(nc, g):
    SP1 = P + 1
    with ExitStack() as ctx:
        def sb(name, *shape):
            return ctx.enter_context(nc.sbuf_tensor(name, list(shape), F32))

        def ps(name, *shape):
            return ctx.enter_context(nc.psum_tensor(name, list(shape), F32))

        sem = g.sem
        stats, mean_var, halves = sb("k_stats", P, GROUP, 6), sb("k_mean_var", P, GROUP, 2), sb("k_halves", P, 4, GROUP)
        small = sb("k_small", P, 4, GROUP)
        n_tok, n2_tok = sb("k_n_tok", P, GROUP, D), sb("k_n2_tok", P, GROUP, D)
        v_feat = sb("k_v_feat", P, KD, GROUP, P)
        time_decay, time_first = sb("k_time_decay", P, KD), sb("k_time_first", P, KD)
        fac = sb("k_fac", P, 4, KD)
        keep = sb("k_keep", P, KD, GROUP, SP1)
        ek, ekv = sb("k_ek", P, KD, GROUP, SP1), sb("k_ekv", P, KD, GROUP, SP1)
        eu, euv = sb("k_eu", P, KD, GT), sb("k_euv", P, KD, GT)
        den_sum, num_sum = sb("k_den_sum", P, KD, GROUP, SP1), sb("k_num_sum", P, KD, GROUP, SP1)
        den, num = sb("k_den", P, KD, GT), sb("k_num", P, KD, GT)
        bank_t = [ps(f"k_bank_t{k}", P, GT) for k in range(KD)]
        bank_y = [ps(f"k_bank_y{j}", P, 2, D) for j in range(2)]
        bank_up = [ps(f"s_bank_up{n}", P, GT) for n in range(2)]
        bank_out = [ps(f"s_bank_out{n}", P, D) for n in range(2)]

        back = sb("k_back", P, 2, GROUP, D)
        out = sb("s_out", P, SEQS, D)
        r = route_buffers(ctx, nc, g, "s_")
        w1, w2 = sb("s_w1", P, KD, FF), sb("s_w2", P, KF, D)
        b1, b2 = sb("s_b1", P, KF), sb("s_b2", 1, D)
        hid = sb("s_hid", P, KF, GT)
        kept = sb("s_kept", P, 2, SEQS)
        weight = sb("s_weight", P, SEQS)
        r.bank_l = bank_up
        r.bank_lt = bank_t[0][:, 0:SEQS * EXPERTS].rearrange("p (q e) -> p q e", e=EXPERTS)
        count_buffers(ctx, nc, g, r, "s_", bank_t[1][:])
        r.logits_e = sb("s_logits_e", EXPERTS, SEQS * P)
        r.loaded, r.loads = sem("s_loaded"), 16 * 5

        loaded, consts, vec, v_loaded = sem("k_loaded"), sem("k_consts"), sem("k_vec"), sem("k_v_loaded")
        var_ready, rstd_ready, n_ready = sem("k_var_ready"), sem("k_rstd_ready"), sem("k_n_ready")
        kT_ps, ek_ready, v_used = sem("k_kT_ps"), sem("k_ek_ready"), sem("k_v_used")
        ekv_ready, y_ready, y_ps = sem("k_ekv_ready"), sem("k_y_ready"), sem("k_y_ps")
        n2_ready, nT_ps, nT_used = sem("k_n2_ready"), sem("k_nT_ps"), sem("k_nT_used")
        gathered, moe_added = sem("k_gathered"), sem("k_moe_added")
        up_ps, hid_ready, out_ps, out_used = sem("s_up_ps"), sem("s_hid_ready"), sem("s_out_ps"), sem("s_out_used")
        VEC_START, VEC_NORM, VEC_STEPS = 5, 7, 26
        block = ctx.enter_context(nc.Block())

        def bodies(eng, body):
            body(0, False, True)
            with eng.Fori(1, GROUPS - 1) as i:
                body(i, True, True)
            body(GROUPS - 1, True, False)

        @block.sync
        def _(sp):
            sp.dma_start(time_decay[:], g.dram["time_decay"]).then_inc(loaded, 16)
            sp.dma_start(time_first[:], g.dram["time_first"]).then_inc(loaded, 16)

            def load_v(i):
                sp.dma_start(v_feat[:], g.dram["ctx_feat"][:, :, bass.ds(i * GROUP, GROUP), :]).then_inc(v_loaded, 16)
            load_v(0)
            for dst, src in ((w1, "switch_w1"), (b1, "switch_b1"), (w2, "switch_w2"), (b2, "switch_b2"), (r.gate_w, "router_w")):
                sp.dma_start(dst[:], g.dram[src]).then_inc(r.loaded, 16)
            with sp.Fori(1, GROUPS) as i:
                sp.wait_ge(v_used, i)
                load_v(i)

        @block.gpsimd
        def _(pool):
            p = nc.gpsimd

            def root(n):
                pool.wait_ge(var_ready, n)
                p.tensor_tensor(small[:, 1, :], small[:, 0, :], g.neg_half[:, 0:GROUP], ALU.pow).then_inc(rstd_ready, 1)

            def gather(i):
                if i:
                    pool.wait_ge(moe_added, 2 * GROUP * i)
                for c in range(2):
                    for j in range(GROUP):
                        n = SEQS * c + GROUP * i + j
                        p.indirect_dma_start(back[:, c, j, :], None, g.slot_out,
                                             bass.IndirectOffsetOnAxis(ap=g.dest_at[:, n:n + 1], axis=0)).then_inc(gathered, 16)
            gather(0)
            root(1)

            def body(i, more):
                pool.wait_ge(v_loaded, i * 16 + 16)
                for k in range(KD):
                    pool.wait_ge(ek_ready, i * 4 + (2 * k + 1))
                    p.tensor_tensor(ekv[:, k, :, 1:], ek[:, k, :, 1:], v_feat[:, k], ALU.mult).then_inc(ekv_ready, 1)
                    pool.wait_ge(ek_ready, i * 4 + (2 * k + 2))
                    p.tensor_tensor(euv[:, k, :], eu[:, k, :], v_feat[:, k].rearrange("p a b -> p (a b)"), ALU.mult)\
                        .then_inc(ekv_ready, 1)
                pool.wait_ge(ekv_ready, i * 4 + 4)
                pool.sem_inc(v_used, 1)
                if more:
                    gather(i + 1)
                root(i * 2 + 2)
                if more:
                    root(i * 2 + 3)
            for i in range(GROUPS):
                body(i, i < GROUPS - 1)
            count_pool(nc, pool, g, r)

        @block.tensor
        def _(pe):
            def turn(src, ready, i, done):
                for j in range(GROUP):
                    pe.wait_ge(ready, i * GROUP + (j + 1))
                    for k in range(KD):
                        last = nc.tensor.transpose(bank_t[k][:, P * j:P * j + P], src[:, j, P * k:P * k + P], g.ident[:])
                last.then_inc(done, 1)

            def up(i):
                for f in range(KF):
                    pe.wait_ge(hid_ready, i * KF + (f + 1))
                    for k in range(KD):
                        last = nc.tensor.matmul(bank_up[f % 2][:], w1[:, k, P * f:P * f + P],
                                                g.xm_feat[:, k, bass.ds(i * GT, GT)], start=(k == 0), stop=(k == KD - 1))
                    last.then_inc(up_ps, 1)

            def down(i, j):
                pe.wait_ge(out_used, i * GROUP + (j + 1))
                nc.tensor.matmul(bank_out[j % 2][:], g.ones[0:1, :], b2[:], start=True, stop=False)
                for f in range(KF):
                    if j == 0:
                        pe.wait_ge(hid_ready, i * KF + (f + 3))
                    last = nc.tensor.matmul(bank_out[j % 2][:], hid[:, f, P * j:P * j + P], w2[:, f, :],
                                            start=False, stop=(f == KF - 1))
                last.then_inc(out_ps, 1)

            def body(i, ffn, more):
                if ffn:
                    pe.wait_ge(nT_used, i * KD)
                turn(n_tok, n_ready, i, kT_ps)
                if ffn:
                    up(i - 1)
                for k in range(KD):
                    pe.wait_ge(y_ready, i * KD + (k + 1))
                    for j in range(GROUP):
                        last = nc.tensor.transpose(bank_y[j // 2][:, j % 2, P * k:P * k + P],
                                                   num[:, k, P * j:P * j + P], g.ident[:])
                last.then_inc(y_ps, 1)
                if ffn:
                    down(i - 1, 0)
                    down(i - 1, 1)
                pe.wait_ge(ek_ready, i * (2 * KD) + 2 * KD)
                turn(n2_tok, n2_ready, i, nT_ps)
                if ffn:
                    down(i - 1, 2)
                    down(i - 1, 3)
                else:
                    pe.wait_ge(r.loaded, r.loads)
            bodies(pe, body)
            pe.wait_ge(nT_used, GROUPS * KD)
            pe.wait_ge(hid_ready, (GROUPS - 1) * KF + 2)
            route_pe(nc, pe, g, r)
            up(GROUPS - 1)
            count_pe(nc, pe, g, r)
            for j in range(GROUP):
                down(GROUPS - 1, j)

        @block.scalar
        def _(act):
            s = nc.scalar
            act.wait_ge(loaded, 32)
            s.activation(fac[:, 1, :], time_decay[:], ACT.Exp).then_inc(vec, 1)
            act.wait_ge(vec, 1)
            s.activation(fac[:, 0, :], fac[:, 1, :], ACT.Exp, scale=-1.0).then_inc(vec, 1)
            act.wait_ge(vec, 4)
            s.activation(fac[:, 3, :], fac[:, 3, :], ACT.Exp).then_inc(vec, 1)
            act.wait_ge(consts, 3)
            act.sem_inc(hid_ready, 2)
            act.sem_inc(out_used, 2)
            act.wait_ge(r.loaded, r.loads)

            def gelu(i):
                for f in range(KF):
                    act.wait_ge(up_ps, i * KF + (f + 1))
                    s.activation(hid[:, f, :], bank_up[f % 2][:], ACT.Gelu, bias=b1[:, f:f + 1]).then_inc(hid_ready, 1)

            def keep_out(i, j):
                act.wait_ge(out_ps, i * GROUP + (j + 1))
                s.copy(out[:, i * GROUP + j, :], bank_out[j % 2][:]).then_inc(out_used, 1)

            def body(i, ffn, more):
                act.wait_ge(kT_ps, i + 1)
                for k in range(KD):
                    s.activation(ek[:, k, :, 1:], bank_t[k][:].rearrange("p (a b) -> p a b", a=GROUP), ACT.Exp)\
                        .then_inc(ek_ready, 1)
                    s.activation(eu[:, k, :], bank_t[k][:], ACT.Exp, bias=fac[:, 2, k:k + 1]).then_inc(ek_ready, 1)
                if ffn:
                    gelu(i - 1)
                    keep_out(i - 1, 0)
                    keep_out(i - 1, 1)
                act.wait_ge(nT_ps, i + 1)
                for k in range(KD):
                    s.copy(g.xm_feat[:, k, bass.ds(i * GT, GT)], bank_t[k][:]).then_inc(nT_used, 1)
                if ffn:
                    keep_out(i - 1, 2)
                    keep_out(i - 1, 3)
            bodies(act, body)
            route_act(nc, act, g, r)
            gelu(GROUPS - 1)
            route_exps(nc, act, g, r, True)
            for j in range(GROUP):
                keep_out(GROUPS - 1, j)

        @block.vector
        def _(dve):
            v = nc.vector
            v.memset(keep[:], 0.0).then_inc(consts, 1)
            v.memset(ek[:], 0.0).then_inc(consts, 1)
            v.memset(ekv[:], 0.0).then_inc(consts, 1)
            dve.wait_ge(loaded, 32)
            dve.wait_ge(vec, 2)
            v.tensor_scalar(fac[:, 2, :], time_first[:], 0.0, None, ALU.min).then_inc(vec, 1)
            v.tensor_scalar(fac[:, 3, :], time_first[:], 0.0, -1.0, ALU.max, ALU.mult).then_inc(vec, 1)
            dve.wait_ge(vec, 5)
            dve.wait_ge(consts, 3)
            for k in range(KD):
                ins = v.tensor_scalar(keep[:, k, :, 1:], keep[:, k, :, 1:], fac[:, 0, k:k + 1], None, ALU.add)
            ins.then_inc(consts, 1)
            dve.wait_ge(consts, 4)
            link = Links(dve, vec, VEC_START)

            def layer_norm(i, part, out, ready):
                for j in range(GROUP):
                    ins = v.bn_stats(stats[:, j, :], g.X[:, i * GROUP + j, :])
                link(ins)
                merge_stats(v, link, stats[:], mean_var, halves)
                v.tensor_scalar(small[:, 0, :], mean_var[:, :, 1], LN_EPS, None, ALU.add).then_inc(var_ready, 1)
                dve.wait_ge(rstd_ready, i * 2 + (part + 1))
                for j in range(GROUP):
                    v.tensor_scalar(out[:, j, :], g.X[:, i * GROUP + j, :], mean_var[:, j, 0:1],
                                    small[:, 1, j:j + 1], ALU.subtract, ALU.mult).then_inc(ready, 1)

            def add_moe(i):
                dve.wait_ge(gathered, i * (16 * 2 * GROUP) + 16 * 2 * GROUP)
                for c in range(2):
                    if c:
                        dve.wait_ge(moe_added, i * (2 * GROUP) + GROUP)
                    for j in range(GROUP):
                        q = i * GROUP + j
                        prob = g.moe_prob[:, c, bass.ds(q, 1)]
                        v.scalar_tensor_tensor(out=g.X[:, q, :], in0=back[:, c, j, :], scalar=prob, in1=g.X[:, q, :],
                                               op0=ALU.mult, op1=ALU.add).then_inc(moe_added, 1)
                dve.wait_ge(moe_added, i * (2 * GROUP) + 2 * GROUP)
                v.memset(small[:, 3, :], 0.0)
            add_moe(0)
            layer_norm(0, 0, n_tok, n_ready)

            def body(i, ffn, more):
                link.restart(i * VEC_STEPS + (VEC_START + VEC_NORM))
                for k in range(KD):
                    dve.wait_ge(ek_ready, i * 4 + (2 * k + 1))
                    link(v.tensor_tensor_scan(den_sum[:, k].rearrange("p a b -> p (a b)"),
                                              keep[:, k].rearrange("p a b -> p (a b)"),
                                              ek[:, k].rearrange("p a b -> p (a b)"), 0.0, ALU.mult, ALU.add))
                    dve.wait_ge(ek_ready, i * 4 + (2 * k + 2))
                    link(v.scalar_tensor_tensor(out=den[:, k].rearrange("p (a b) -> p a b", a=GROUP),
                                                in0=den_sum[:, k, :, 0:P], scalar=fac[:, 3, k:k + 1],
                                                in1=eu[:, k].rearrange("p (a b) -> p a b", a=GROUP),
                                                op0=ALU.mult, op1=ALU.add))
                    link(v.reciprocal(den[:, k], den[:, k]))
                    dve.wait_ge(ekv_ready, i * 4 + (2 * k + 1))
                    link(v.tensor_tensor_scan(num_sum[:, k].rearrange("p a b -> p (a b)"),
                                              keep[:, k].rearrange("p a b -> p (a b)"),
                                              ekv[:, k].rearrange("p a b -> p (a b)"), 0.0, ALU.mult, ALU.add))
                    dve.wait_ge(ekv_ready, i * 4 + (2 * k + 2))
                    link(v.scalar_tensor_tensor(out=num[:, k].rearrange("p (a b) -> p a b", a=GROUP),
                                                in0=num_sum[:, k, :, 0:P], scalar=fac[:, 3, k:k + 1],
                                                in1=euv[:, k].rearrange("p (a b) -> p a b", a=GROUP),
                                                op0=ALU.mult, op1=ALU.add))
                    v.tensor_tensor(num[:, k], num[:, k], den[:, k], ALU.mult).then_inc(y_ready, 1)
                dve.wait_ge(y_ps, i + 1)
                for h in range(2):
                    seqs = bass.ds(i * GROUP + 2 * h, 2)
                    link(v.tensor_tensor(g.X[:, seqs, :], g.X[:, seqs, :], bank_y[h][:], ALU.add))
                v.memset(small[:, 3, :], 0.0)
                layer_norm(i, 1, n2_tok, n2_ready)
                if more:
                    add_moe(i + 1)
                    layer_norm(i + 1, 0, n_tok, n_ready)
                assert link.n == VEC_STEPS - (0 if more else VEC_NORM), link.n
            bodies(dve, body)
            link = Links(dve, r.link)
            route_dve(nc, dve, g, r, link, True)
            count_dve(nc, dve, g, r, link)
            slot = r.slot
            link(v.tensor_scalar(slot[:], slot[:], CAP - 0.5, None, ALU.is_lt))
            link(v.tensor_tensor(slot[:], slot[:], r.hot[:].rearrange("p n q e -> p (n q) e"), ALU.mult))
            link(v.tensor_reduce(kept[:].rearrange("p n q -> p (n q)"), slot[:], AX.X, ALU.add))
            link(v.tensor_tensor(kept[:], kept[:], r.prob[:], ALU.mult))
            link(v.tensor_tensor(weight[:], kept[:, 0], kept[:, 1], ALU.add))
            for q in range(SEQS):
                dve.wait_ge(out_used, q + 3)
                v.scalar_tensor_tensor(out=g.X[:, q, :], in0=out[:, q, :], scalar=weight[:, q:q + 1],
                                       in1=g.X[:, q, :], op0=ALU.mult, op1=ALU.add)


def norm_buffers(ctx, nc, g, tag):
    def sb(name, *shape):
        return ctx.enter_context(nc.sbuf_tensor(tag + name, list(shape), F32))
    n = Shared()
    n.stats, n.mean_var, n.halves = sb("stats", P, GROUP, 6), sb("mean_var", P, GROUP, 2), sb("halves", P, 4, GROUP)
    n.small, n.tok = sb("small", P, 2, GROUP), sb("n_tok", P, GROUP, D)
    n.var_ready, n.rstd_ready, n.ready = g.sem(tag + "var_ready"), g.sem(tag + "rstd_ready"), g.sem(tag + "n_ready")
    return n


def groups(eng, first, group):
    first()
    with eng.Fori(0, GROUPS - 1) as i:
        group(i, True)
    group(GROUPS - 1, False)


def norm_stats_dve(nc, dve, g, n, link, i):
    v = nc.vector
    for j in range(GROUP):
        ins = v.bn_stats(n.stats[:, j, :], g.X[:, i * GROUP + j, :])
    link(ins)
    norm_merge_dve(nc, g, n, link)


def norm_merge_dve(nc, g, n, link):
    v = nc.vector
    merge_stats(v, link, n.stats[:], n.mean_var, n.halves)
    v.tensor_scalar(n.small[:, 0, :], n.mean_var[:, :, 1], LN_EPS, None, ALU.add).then_inc(n.var_ready, 1)


def norm_apply_dve(nc, dve, g, n, i):
    dve.wait_ge(n.rstd_ready, i + 1)
    for j in range(GROUP):
        nc.vector.tensor_scalar(n.tok[:, j, :], g.X[:, i * GROUP + j, :], n.mean_var[:, j, 0:1], n.small[:, 1, j:j + 1],
                                ALU.subtract, ALU.mult).then_inc(n.ready, 1)


def norm_pool(nc, pool, g, n, i):
    pool.wait_ge(n.var_ready, i + 1)
    nc.gpsimd.tensor_tensor(n.small[:, 1, :], n.small[:, 0, :], g.neg_half[:, 0:GROUP], ALU.pow)\
        .then_inc(n.rstd_ready, 1)


def turn_pe(nc, pe, g, n, banks, turned, i):
    for j in range(GROUP):
        pe.wait_ge(n.ready, i * GROUP + (j + 1))
        for k in range(KD):
            last = nc.tensor.transpose(banks[k][:, P * j:P * j + P], n.tok[:, j, P * k:P * k + P], g.ident[:])
    last.then_inc(turned, 1)


BLK = 16
NBLK = P // BLK
LIMIT = 1e17
GH = 8
HK = P // GH


def gla_phase(nc, g):
    UNITS = GROUP * KD
    VEC_FIRST = 7 + 3
    VEC_LAST = 7
    with ExitStack() as ctx:
        def sb(name, *shape):
            return ctx.enter_context(nc.sbuf_tensor("g_" + name, list(shape), F32))

        def ps(name, *shape):
            return ctx.enter_context(nc.psum_tensor("g_" + name, list(shape), F32))

        sem = lambda name: g.sem("g_" + name)
        n = norm_buffers(ctx, nc, g, "g_")
        w = {m: sb("w" + m, P, KD, D) for m in "qkvgo"}
        gamma, beta = sb("gamma", P, KD), sb("beta", P, KD)
        n_feat = sb("n_feat", P, KD, GT)
        k_feat, q_feat, v_tok = sb("k_feat", P, KD, GT), sb("q_feat", P, KD, GT), sb("v_tok", P, GROUP, D)
        absx, soft = sb("absx", P, KD, GT), sb("soft", P, KD, GT)
        logg, run = sb("logg", P, KD, GT), sb("run", P, KD, GT)
        mid = sb("mid", P, KD, GROUP, NBLK)
        dist = sb("dist", P, KD, GT)
        ek, eq = sb("ek", P, KD, GT), sb("eq", P, KD, GT)
        hop = sb("hop", P, KD, GROUP, NBLK, NBLK)
        later = sb("later", P, NBLK, NBLK)
        reset = sb("reset", P, GROUP, P)
        head = sb("head", P, GH)
        kt = sb("kt", P, 2, NBLK, P)
        qbd = sb("qbd", P, 2, NBLK, GH, BLK)
        att = sb("att", P, 2, GH, NBLK, BLK)
        y_stats, y_mv, y_half = sb("y_stats", P, GROUP, 6), sb("y_mv", P, GROUP, 2), sb("y_half", P, 4, GROUP)
        y_small = sb("y_small", P, 2, GROUP)
        y_tok = sb("y_tok", P, GROUP, D)
        y_feat = sb("y_feat", P, KD, GT)
        bank_t = [ps(f"bank_t{k}", P, GT) for k in range(2)]
        bank_p = [ps(f"bank_p{k}", P, GT) for k in range(2)]
        bank_s = [ps(f"bank_s{k}", P, GT) for k in range(2)]
        bank_y = [ps(f"bank_y{k}", P, 2, D) for k in range(2)]

        loaded, consts, vec = sem("loaded"), sem("consts"), sem("vec")
        turned, feat_ready = sem("turned"), sem("feat_ready")
        g_ps, k_ps, q_ps, v_ps = sem("g_ps"), sem("k_ps"), sem("q_ps"), sem("v_ps")
        soft_ready, gates_read, exponents, decays, k_ready, q_ready, v_ready = (
            sem("soft_ready"), sem("gates_read"), sem("exponents"), sem("decays"), sem("k_ready"), sem("q_ready"),
            sem("v_ready"))
        kt_ready, qbd_ready = sem("kt_ready"), sem("qbd_ready")
        s_ps, att_ready, y_ps = sem("s_ps"), sem("att_ready"), sem("y_ps")
        y_var, y_rstd, y_ready, yT_ps, yT_ready, o_ps = (
            sem("y_var"), sem("y_rstd"), sem("y_ready"), sem("yT_ps"), sem("yT_ready"), sem("o_ps"))
        block = ctx.enter_context(nc.Block())

        def scores(u, h):
            return (bank_p if u % 2 else bank_s)[h][:].rearrange("p (b h t) -> p b h t", b=NBLK // 2, h=GH)

        @block.sync
        def _(sp):
            for m in "gkqvo":
                sp.dma_start(w[m][:], g.dram["gla_w" + m]).then_inc(loaded, 16)
            sp.dma_start(gamma[:], g.dram["gla_gamma"]).then_inc(loaded, 16)
            sp.dma_start(beta[:], g.dram["gla_beta"]).then_inc(loaded, 16)
            for m in ("w2", "had", "w1", "w3"):
                sp.dma_start(g.ffn[m], g.dram["ffn_" + m]).then_inc(g.ffn_w2_loaded if m == "w2" else g.ffn_loaded, 16)

        @block.gpsimd
        def _(pool):
            p = nc.gpsimd
            p.memset(reset[:], 1.0).then_inc(consts, 1)
            p.memset(head[:], float(HK) ** -0.5).then_inc(consts, 1)
            p.memset(later[:], 0.0).then_inc(consts, 1)
            pool.wait_ge(consts, 3)
            p.affine_select(out=later[:], in_=later[:], compare_op=ALU.is_ge, fill=-1000.0, base=0,
                            pattern=[[1, NBLK], [-1, NBLK]], channel_multiplier=0).then_inc(consts, 1)
            p.memset(reset[:, :, 0:1], 0.0).then_inc(consts, 1)
            p.affine_select(out=head[:], in_=head[:], compare_op=ALU.is_ge, fill=0.0, base=0,
                            pattern=[[-HK, GH]], channel_multiplier=1).then_inc(consts, 1)
            pool.wait_ge(consts, 6)
            p.affine_select(out=head[:], in_=head[:], compare_op=ALU.is_ge, fill=0.0, base=HK - 1,
                            pattern=[[HK, GH]], channel_multiplier=-1).then_inc(consts, 1)
            pool.wait_ge(consts, 7)

            def first():
                norm_pool(nc, pool, g, n, 0)
                pool.wait_ge(g.ffn_w2_loaded, 16)
                src, dst = g.ffn["w2"], g.ffn["w2b"]
                for m in range(3):
                    h = 1 << m
                    a = src.rearrange("p (n two h) d -> p n two h d", two=2, h=h)
                    o = dst.rearrange("p (n two h) d -> p n two h d", two=2, h=h)
                    for x in range(KF // (2 * h)):
                        p.tensor_tensor(o[:, x, 0], a[:, x, 0], a[:, x, 1], ALU.add).then_inc(g.folded, 1)
                        p.tensor_tensor(o[:, x, 1], a[:, x, 0], a[:, x, 1], ALU.subtract).then_inc(g.folded, 1)
                    pool.wait_ge(g.folded, sum(2 * (KF >> (q + 1)) for q in range(m + 1)))
                    src, dst = dst, src

            def group(i, more):
                for u in range(UNITS):
                    j, k = u // KD, u % KD
                    tok = slice(P * j, P * j + P)
                    if u < KD:
                        pool.wait_ge(q_ready, i * KD + (k + 1))
                    else:
                        pool.wait_ge(s_ps, i * (2 * UNITS) + (2 * (u - 1)))
                    p.tensor_tensor(qbd[:, u % 2],
                                    bc(q_feat[:, k, tok].rearrange("p (n t) -> p n t", n=NBLK).unsqueeze(2), [P, NBLK, GH, BLK]),
                                    bc(head[:].unsqueeze(1).unsqueeze(3), [P, NBLK, GH, BLK]), ALU.mult)\
                        .then_inc(qbd_ready, 1)
                    if u == UNITS - 2 and more:
                        norm_pool(nc, pool, g, n, i + 1)
                pool.wait_ge(y_var, i + 1)
                p.tensor_tensor(y_small[:, 1, :], y_small[:, 0, :], g.neg_half[:, 0:GROUP], ALU.pow).then_inc(y_rstd, 1)
            groups(pool, first, group)

        @block.tensor
        def _(pe):
            pe.wait_ge(loaded, 16 * 7)

            def project(what, banks, done, tiles=range(KD)):
                for c in tiles:
                    for k in range(KD):
                        last = nc.tensor.matmul(banks[c][:], w[what][:, k, P * c:P * c + P], n_feat[:, k, :],
                                                start=(k == 0), stop=(k == KD - 1))
                    last.then_inc(done, 1)

            def project_v(i):
                pe.wait_ge(gates_read, i * KD + KD)
                for j in range(GROUP):
                    for k in range(KD):
                        last = nc.tensor.matmul(bank_s[j // 2][:, D * (j % 2):D * (j % 2) + D],
                                                n_feat[:, k, P * j:P * j + P], w["v"][:, k, :],
                                                start=(k == 0), stop=(k == KD - 1))
                    if j % 2:
                        last.then_inc(v_ps, 1)

            def first():
                turn_pe(nc, pe, g, n, bank_t, turned, 0)
                pe.wait_ge(feat_ready, KD)
                project("g", bank_s, g_ps)
                project("k", bank_t, k_ps)
                project("q", bank_p, q_ps)
                project_v(0)

            def a(i, u):
                pe.wait_ge(qbd_ready, i * UNITS + (u + 1))
                pe.wait_ge(kt_ready, i * UNITS + (u + 1))
                if u == 0:
                    pe.wait_ge(v_ready, i * 2 + 2)
                for h in range(2):
                    if u >= 2:
                        pe.wait_ge(att_ready, i * (2 * UNITS) + (2 * (u - 2) + h + 1))
                    for b in range(NBLK // 2):
                        blk = NBLK // 2 * h + b
                        last = nc.tensor.matmul(scores(u, h)[:, b], kt[:, u % 2, blk, :], qbd[:, u % 2, blk],
                                                start=True, stop=True)
                    last.then_inc(s_ps, 1)

            def b(i, u):
                j, k = u // KD, u % KD
                pe.wait_ge(att_ready, i * (2 * UNITS) + (2 * u + 2))
                for h in range(GH):
                    col = P * k + HK * h
                    last = nc.tensor.matmul(bank_y[j // 2][:, j % 2, col:col + HK],
                                            att[:, u % 2, h].rearrange("p n t -> p (n t)"),
                                            v_tok[:, j, col:col + HK], start=True, stop=True)
                last.then_inc(y_ps, 1)

            def group(i, more):
                for u in range(UNITS):
                    a(i, u)
                    if u == UNITS - 1 and more:
                        turn_pe(nc, pe, g, n, bank_t, turned, i + 1)
                    if u >= 2:
                        b(i, u - 2)
                if more:
                    pe.wait_ge(feat_ready, i * KD + 2 * KD)
                    pe.wait_ge(att_ready, i * (2 * UNITS) + (2 * UNITS - 2))
                    project("g", bank_s, g_ps, range(1))
                b(i, UNITS - 2)
                if more:
                    project("g", bank_s, g_ps, range(1, KD))
                b(i, UNITS - 1)
                if more:
                    project("k", bank_t, k_ps)
                for j in range(GROUP):
                    pe.wait_ge(y_ready, i * GROUP + (j + 1))
                    for k in range(KD):
                        last = nc.tensor.transpose(bank_p[k][:, P * j:P * j + P], y_tok[:, j, P * k:P * k + P], g.ident[:])
                last.then_inc(yT_ps, 1)
                if more:
                    project_v(i + 1)
                pe.wait_ge(yT_ready, i * KD + KD)
                if more:
                    project("q", bank_p, q_ps)
                for j in range(GROUP):
                    for k in range(KD):
                        last = nc.tensor.matmul(bank_y[j // 2][:, j % 2, :], y_feat[:, k, P * j:P * j + P], w["o"][:, k, :],
                                                start=(k == 0), stop=(k == KD - 1))
                    if j % 2:
                        last.then_inc(o_ps, 1)
            groups(pe, first, group)

        @block.scalar
        def _(act):
            s = nc.scalar
            act.wait_ge(loaded, 16 * 7)

            def feats(i):
                act.wait_ge(turned, i + 1)
                for k in range(KD):
                    s.copy(n_feat[:, k, :], bank_t[k][:]).then_inc(feat_ready, 1)

            def gates(i):
                for k in range(KD):
                    act.wait_ge(g_ps, i * KD + (k + 1))
                    s.activation(absx[:, k, :], bank_s[k][:], ACT.Abs).then_inc(soft_ready, 1)
                for k in range(KD):
                    act.wait_ge(soft_ready, i * (3 * KD) + (k + 1))
                    s.activation(soft[:, k, :], absx[:, k, :], ACT.Exp, scale=-1.0).then_inc(soft_ready, 1)
                for k in range(KD):
                    act.wait_ge(soft_ready, i * (3 * KD) + (KD + k + 1))
                    s.activation(soft[:, k, :], soft[:, k, :], ACT.Ln, bias=1.0).then_inc(soft_ready, 1)

            def spread(i):
                for x, (out, sign) in enumerate(((ek, -1.0), (eq, 1.0))):
                    for k in range(KD):
                        act.wait_ge(exponents, i * (2 * KD) + (k + 1))
                        s.activation(out[:, k, :], dist[:, k, :], ACT.Exp, scale=sign).then_inc(decays, 1)
                for k in range(KD):
                    act.wait_ge(exponents, i * (2 * KD) + (KD + k + 1))
                    s.activation(hop[:, k], hop[:, k], ACT.Exp).then_inc(decays, 1)
                for h in range(2):
                    act.wait_ge(v_ps, i * 2 + (h + 1))
                    s.copy(v_tok[:, 2 * h:2 * h + 2, :].rearrange("p a d -> p (a d)"), bank_s[h][:]).then_inc(v_ready, 1)

            def first():
                feats(0)
                gates(0)
                spread(0)

            def group(i, more):
                if more:
                    feats(i + 1)
                    gates(i + 1)
                act.wait_ge(yT_ps, i + 1)
                for k in range(KD):
                    s.activation(y_feat[:, k, :], bank_p[k][:], ACT.Identity, scale=gamma[:, k:k + 1],
                                 bias=beta[:, k:k + 1]).then_inc(yT_ready, 1)
                if more:
                    spread(i + 1)
            groups(act, first, group)

        @block.vector
        def _(dve):
            v = nc.vector
            dve.wait_ge(consts, 7)

            def gates(i, link):
                for k in range(KD):
                    dve.wait_ge(soft_ready, i * (3 * KD) + (2 * KD + k + 1))
                    v.scalar_tensor_tensor(out=logg[:, k, :], in0=bank_s[k][:], scalar=0.0, in1=soft[:, k, :],
                                           op0=ALU.min, op1=ALU.subtract).then_inc(gates_read, 1)
                for k in range(KD):
                    dve.wait_ge(gates_read, i * KD + (k + 1))
                    ins = v.tensor_tensor_scan(run[:, k, :], reset[:].rearrange("p a b -> p (a b)"), logg[:, k, :], 0.0,
                                               ALU.mult, ALU.add)
                link(ins)
                for k in range(KD):
                    ins = v.tensor_copy(mid[:, k].rearrange("p a n -> p (a n)"), run[:, k, BLK // 2 - 1:GT:BLK])
                link(ins)
                for k in range(KD):
                    v.tensor_tensor(dist[:, k, :].rearrange("p (n t) -> p n t", t=BLK),
                                    run[:, k, :].rearrange("p (n t) -> p n t", t=BLK),
                                    bc(mid[:, k].rearrange("p a n -> p (a n)").unsqueeze(2), [P, GROUP * NBLK, BLK]),
                                    ALU.subtract).then_inc(exponents, 1)
                square = [P, GROUP, NBLK, NBLK]
                for k in range(KD):
                    ins = v.tensor_tensor(hop[:, k], bc(mid[:, k].unsqueeze(3), square), bc(mid[:, k].unsqueeze(2), square),
                                          ALU.subtract)
                link(ins)
                for k in range(KD):
                    v.scalar_tensor_tensor(out=hop[:, k], in0=hop[:, k], scalar=0.0, in1=bc(later[:].unsqueeze(1), square),
                                           op0=ALU.min, op1=ALU.add).then_inc(exponents, 1)

            def spread(i, link):
                for x, (e, banks, ps_ready, out, ready) in enumerate(((ek, bank_t, k_ps, k_feat, k_ready),
                                                                      (eq, bank_p, q_ps, q_feat, q_ready))):
                    for k in range(KD):
                        dve.wait_ge(ps_ready, i * KD + (k + 1))
                        dve.wait_ge(decays, i * (3 * KD) + (KD * x + k + 1))
                        ins = v.scalar_tensor_tensor(out=out[:, k, :], in0=e[:, k, :], scalar=LIMIT, in1=banks[k][:],
                                                     op0=ALU.min, op1=ALU.mult)
                        ins.then_inc(ready, 1)
                    dve.wait_ge(ready, i * KD + KD)

            def a(i, u):
                j, k = u // KD, u % KD
                if u >= 2:
                    dve.wait_ge(s_ps, i * (2 * UNITS) + 2 * (u - 1))
                if u == 0:
                    dve.wait_ge(decays, i * (3 * KD) + 3 * KD)
                four = [P, NBLK, NBLK, BLK]
                v.tensor_tensor(kt[:, u % 2].rearrange("p i (j t) -> p i j t", t=BLK),
                                bc(k_feat[:, k, P * j:P * j + P].rearrange("p (j t) -> p j t", t=BLK).unsqueeze(1), four),
                                bc(hop[:, k, j].unsqueeze(3), four), ALU.mult).then_inc(kt_ready, 1)

            def b(i, u):
                for h in range(2):
                    dve.wait_ge(s_ps, i * (2 * UNITS) + (2 * u + h + 1))
                    if u >= 2:
                        dve.wait_ge(y_ps, i * UNITS + (u - 1))
                    half = slice(NBLK // 2 * h, NBLK // 2 * (h + 1))
                    v.tensor_tensor(att[:, u % 2, :, half].rearrange("p h n t -> p n h t"), scores(u, h),
                                    bc(g.upto[:, P // 2 * h:P // 2 * (h + 1)]
                                       .rearrange("p (n t) -> p n t", t=BLK).unsqueeze(2), [P, NBLK // 2, GH, BLK]),
                                    ALU.mult).then_inc(att_ready, 1)

            def first():
                link = Links(dve, vec)
                norm_stats_dve(nc, dve, g, n, link, 0)
                norm_apply_dve(nc, dve, g, n, 0)
                gates(0, link)
                spread(0, link)
                a(0, 0)
                assert link.n == VEC_FIRST, link.n

            def group(i, more):
                link = Links(dve, vec, i * (VEC_FIRST + VEC_LAST) + VEC_FIRST)
                for u in range(UNITS):
                    if u + 1 < UNITS:
                        a(i, u + 1)
                    if u == UNITS - 2 and more:
                        norm_apply_dve(nc, dve, g, n, i + 1)
                    if u in (1, 2) and more:
                        for q in (2 * u - 2, 2 * u - 1):
                            ins = v.bn_stats(n.stats[:, q, :], g.X[:, (i + 1) * GROUP + q, :])
                    if u == 2 and more:
                        link(ins)
                    if u == 4 and more:
                        norm_merge_dve(nc, g, n, link)
                    b(i, u)
                    if u == UNITS // 2 + 1:
                        for j in range(2):
                            v.bn_stats(y_stats[:, j, :], bank_y[0][:, j, :])
                dve.wait_ge(y_ps, i * UNITS + UNITS)
                v.memset(y_half[:, 0], 0.0)
                for j in range(2, GROUP):
                    ins = v.bn_stats(y_stats[:, j, :], bank_y[j // 2][:, j % 2, :])
                link(ins)
                merge_stats(v, link, y_stats[:], y_mv, y_half)
                v.tensor_scalar(y_small[:, 0, :], y_mv[:, :, 1], LN_EPS, None, ALU.add).then_inc(y_var, 1)
                dve.wait_ge(y_rstd, i + 1)
                for j in range(GROUP):
                    v.tensor_scalar(y_tok[:, j, :], bank_y[j // 2][:, j % 2, :], y_mv[:, j, 0:1], y_small[:, 1, j:j + 1],
                                    ALU.subtract, ALU.mult).then_inc(y_ready, 1)
                if more:
                    gates(i + 1, link)
                    spread(i + 1, link)
                    a(i + 1, 0)
                for h in range(2):
                    dve.wait_ge(o_ps, i * 2 + (h + 1))
                    seqs = bass.ds(i * GROUP + 2 * h, 2)
                    v.tensor_tensor(g.X[:, seqs, :], g.X[:, seqs, :], bank_y[h][:], ALU.add)
                if more:
                    assert link.n == VEC_FIRST + VEC_LAST, link.n
            groups(dve, first, group)


def channel_phase(nc, g):
    SCALE = float(D) ** -0.5
    VEC_FIRST = 14 + GROUP
    with ExitStack() as ctx:
        def sb(name, *shape):
            return ctx.enter_context(nc.sbuf_tensor("c_" + name, list(shape), F32))

        def ps(name, *shape):
            return ctx.enter_context(nc.psum_tensor("c_" + name, list(shape), F32))

        sem = lambda name: g.sem("c_" + name)
        stats, mean_var, halves = sb("stats", P, SEQS, 6), sb("mean_var", P, SEQS, 2), sb("halves", P, 4, SEQS)
        var, rstd, n_tok = sb("var", P, SEQS), sb("rstd", P, SEQS), sb("n_tok", P, GROUP, D)
        c_tok, c_feat = sb("c_tok", P, 2, GROUP, D), sb("c_feat", P, 2, KD, GROUP, P)
        peak, bias, total, inv = sb("peak", P, 2, KD), sb("bias", P, 2, KD), sb("total", P, 2, KD), sb("inv", P, 2, KD)
        prob = sb("prob", P, GROUP, KD, D)
        bank_a = [ps(f"bank_a{k}", P, KD, D) for k in range(2)]
        bank_o = [ps(f"bank_o{k}", P, D) for k in range(2)]
        c_loaded, c_used = [sem("c_loaded0"), sem("c_loaded1")], sem("c_used")
        var_ready, rstd_ready, n_ready = sem("var_ready"), sem("rstd_ready"), sem("n_ready")
        vec, had_ps, inv_ready = sem("vec"), sem("had_ps"), sem("inv_ready")
        a_ps, bias_ready, exp_ready, prob_ready, o_ps, added = (
            sem("a_ps"), sem("bias_ready"), sem("exp_ready"), sem("prob_ready"), sem("o_ps"), sem("added"))
        block = ctx.enter_context(nc.Block())

        def pipeline(eng, a, b, c):
            def group(i, buf, loads, opening, more):
                for j in range(GROUP):
                    a(i, j, buf, loads, opening, more)
                    if not opening or j >= 1:
                        b(i * GROUP + (j - 1), (j - 1) % GROUP)
                    if not opening or j >= 2:
                        c(i * GROUP + (j - 2), (j - 2) % GROUP, buf if j >= 2 else 1 - buf)
            group(0, 0, 48, True, True)
            with eng.Fori(0, GROUPS // 2 - 1) as m:
                group(m * 2 + 1, 1, m * 48 + 48, False, True)
                group(m * 2 + 2, 0, m * 48 + 96, False, True)
            group(GROUPS - 1, 1, GROUPS // 2 * 48, False, False)
            b(SEQS - 1, GROUP - 1)
            c(SEQS - 2, GROUP - 2, 1)
            c(SEQS - 1, GROUP - 1, 1)

        @block.sync
        def _(sp):
            with sp.Fori(0, GROUPS // 2) as m:
                for b in range(2):
                    sp.wait_ge(c_used, m * 2 + (b + 1))
                    seqs = bass.ds(m * (2 * GROUP) + b * GROUP, GROUP)
                    sp.dma_start(c_tok[:, b], g.dram["ctx"].rearrange("q s d -> s q d")[:, seqs, :]).then_inc(c_loaded[b], 16)
                    for k in range(KD):
                        sp.dma_start(c_feat[:, b, k], g.dram["ctx_feat"][:, k, seqs, :]).then_inc(c_loaded[b], 16)

        @block.gpsimd
        def _(pool):
            for n, q in enumerate((slice(0, GROUP), slice(GROUP, SEQS))):
                pool.wait_ge(var_ready, n + 1)
                nc.gpsimd.tensor_tensor(rstd[:, q], var[:, q], bc(g.neg_half[:, 0:1], [P, q.stop - q.start]), ALU.pow)\
                    .then_inc(rstd_ready, 1)

        @block.tensor
        def _(pe):
            pe.wait_ge(g.ffn_loaded, 16 * 3)
            pe.wait_ge(g.folded, 2 * (KF - 1))
            for f in range(KF):
                if f >= 2:
                    pe.wait_ge(g.w2h_ready, f - 1)
                nc.tensor.matmul(bank_o[f % 2][:], g.ffn["had"], g.ffn["w2b"][:, f, :], start=True, stop=True)\
                    .then_inc(had_ps, 1)
            pe.wait_ge(g.w2h_ready, KF)

            def a(i, j, buf, loads, opening, more):
                if j == 0:
                    pe.wait_ge(c_loaded[buf], loads)
                pe.wait_ge(n_ready, i * GROUP + (j + 1))
                pe.wait_ge(exp_ready, i * GROUP + (j + 1))
                for k in range(KD):
                    last = nc.tensor.matmul(bank_a[j % 2][:, k, :], c_tok[:, buf, j, P * k:P * k + P], n_tok[:, j, :],
                                            start=True, stop=True)
                last.then_inc(a_ps, 1)

            def none(n, j):
                pass

            def c(n, j, buf):
                pe.wait_ge(prob_ready, n + 1)
                pe.wait_ge(added, n + 1)
                for k in range(KD):
                    last = nc.tensor.matmul(bank_o[j % 2][:], c_feat[:, buf, k, j, :], prob[:, j, k, :],
                                            start=(k == 0), stop=(k == KD - 1))
                last.then_inc(o_ps, 1)
            pipeline(pe, a, none, c)

        @block.scalar
        def _(act):
            for f in range(KF):
                act.wait_ge(had_ps, f + 1)
                nc.scalar.mul(g.ffn["w2h"][:, f, :], bank_o[f % 2][:], 0.5 / float(FF) ** 0.5).then_inc(g.w2h_ready, 1)
            act.sem_inc(exp_ready, 2)
            with act.Fori(0, GROUPS) as i:
                for j in range(GROUP):
                    act.wait_ge(bias_ready, i * GROUP + (j + 1))
                    for k in range(KD):
                        last = nc.scalar.activation(prob[:, j, k, :], bank_a[j % 2][:, k, :], ACT.Exp, scale=SCALE,
                                                    bias=bias[:, j % 2, k:k + 1], accum_out=total[:, j % 2, k:k + 1])
                    last.then_inc(exp_ready, 1)

        @block.vector
        def _(dve):
            v = nc.vector
            dve.sem_inc(added, 2)
            dve.sem_inc(c_used, 2)
            link = Links(dve, vec)

            def row_stats(lo, hi):
                for q in range(lo, hi):
                    ins = v.bn_stats(stats[:, q, :], g.X[:, q, :])
                return ins

            def variances(lo, hi):
                q = slice(lo, hi)
                merge_stats(v, link, stats[:, q], mean_var[:, q], halves[:, :, q])
                v.tensor_scalar(var[:, q], mean_var[:, q, 1], LN_EPS, None, ALU.add).then_inc(var_ready, 1)

            def norm_apply(i, rstds):
                dve.wait_ge(rstd_ready, rstds)
                for j in range(GROUP):
                    q = bass.ds(i * GROUP + j, 1)
                    v.tensor_scalar(n_tok[:, j, :], g.X[:, i * GROUP + j, :],
                                    mean_var[:, q, 0:1].rearrange("p a b -> p (a b)"), rstd[:, q],
                                    ALU.subtract, ALU.mult).then_inc(n_ready, 1)

            def a(i, j, buf, loads, opening, more):
                if j == 0 and not opening:
                    link.restart((i - 1) * GROUP + VEC_FIRST)
                dve.wait_ge(a_ps, i * GROUP + (j + 1))
                link(v.tensor_reduce(peak[:, j % 2, :], bank_a[j % 2][:], AX.X, ALU.max))
                v.tensor_scalar(bias[:, j % 2, :], peak[:, j % 2, :], -SCALE, None, ALU.mult).then_inc(bias_ready, 1)
                if opening and j < 3:
                    ins = row_stats(GROUP * (j + 1), GROUP * (j + 2))
                if opening and j == 2:
                    link(ins)
                    variances(GROUP, SEQS)
                if j == GROUP - 1 and more:
                    norm_apply(i + 1, 2)

            def b(n, j):
                dve.wait_ge(exp_ready, n + 3)
                v.reciprocal(inv[:, j % 2, :], total[:, j % 2, :]).then_inc(inv_ready, 1)
                dve.wait_ge(inv_ready, n + 1)
                v.tensor_tensor(prob[:, j], prob[:, j], bc(inv[:, j % 2, :].unsqueeze(2), [P, KD, D]), ALU.mult)\
                    .then_inc(prob_ready, 1)

            def c(n, j, buf):
                dve.wait_ge(o_ps, n + 1)
                if j == GROUP - 1:
                    dve.sem_inc(c_used, 1)
                v.tensor_tensor(g.X[:, n, :], g.X[:, n, :], bank_o[j % 2][:], ALU.add).then_inc(added, 1)
            assert SEQS == 4 * GROUP
            link(row_stats(0, GROUP))
            variances(0, GROUP)
            norm_apply(0, 1)
            pipeline(dve, a, b, c)


def ffn_phase(nc, g):
    VEC_STEPS = 7 + KF
    with ExitStack() as ctx:
        def sb(name, *shape):
            return ctx.enter_context(nc.sbuf_tensor("f_" + name, list(shape), F32))

        def ps(name, *shape):
            return ctx.enter_context(nc.psum_tensor("f_" + name, list(shape), F32))

        sem = lambda name: g.sem("f_" + name)
        n = norm_buffers(ctx, nc, g, "f_")
        w1, w3, w2h = g.ffn["w1"], g.ffn["w3"], g.ffn["w2h"]
        n_feat = sb("n_feat", P, KD, GT)
        tanh, silu = sb("tanh", P, 2, GT), sb("silu", P, 2, GT)
        hid = sb("hid", P, KF, GT)
        bank_t = [ps(f"bank_t{k}", P, GT) for k in range(2)]
        bank_g = [ps(f"bank_g{k}", P, GT) for k in range(2)]
        bank_u = [ps(f"bank_u{k}", P, GT) for k in range(2)]
        bank_o = [ps(f"bank_o{k}", P, D) for k in range(2)]
        vec = sem("vec")
        turned, feat_ready, gu_ps, tanh_ready, hid_ready = (
            sem("turned"), sem("feat_ready"), sem("gu_ps"), sem("tanh_ready"), sem("hid_ready"))
        o_ps, added, stored = sem("o_ps"), sem("added"), sem("stored")
        block = ctx.enter_context(nc.Block())

        @block.sync
        def _(sp):
            with sp.Fori(0, GROUPS) as i:
                sp.wait_ge(added, i * GROUP + (GROUP + 2))
                seqs = bass.ds(i * GROUP, GROUP)
                sp.dma_start(g.dram["out"].rearrange("q t d -> t q d")[:, seqs, :], g.X[:, seqs, :]).then_inc(stored, 16)
            sp.wait_ge(stored, 16 * GROUPS)

        @block.gpsimd
        def _(pool):
            norm_pool(nc, pool, g, n, 0)
            with pool.Fori(1, GROUPS) as i:
                norm_pool(nc, pool, g, n, i)

        @block.tensor
        def _(pe):
            def first():
                turn_pe(nc, pe, g, n, bank_t, turned, 0)

            def group(i, more):
                pe.wait_ge(feat_ready, i * KD + KD)
                for f in range(KF):
                    pe.wait_ge(hid_ready, i * KF + (f + 1))
                    for w, bank in ((w1, bank_g), (w3, bank_u)):
                        for k in range(KD):
                            last = nc.tensor.matmul(bank[f % 2][:], w[:, k, P * f:P * f + P], n_feat[:, k, :],
                                                    start=(k == 0), stop=(k == KD - 1))
                    last.then_inc(gu_ps, 1)
                if more:
                    turn_pe(nc, pe, g, n, bank_t, turned, i + 1)
                for j in range(GROUP):
                    pe.wait_ge(added, i * GROUP + (j + 1))
                    for f in range(KF):
                        if j == 0:
                            pe.wait_ge(hid_ready, i * KF + (f + 3))
                        last = nc.tensor.matmul(bank_o[j % 2][:], hid[:, f, P * j:P * j + P], w2h[:, f, :],
                                                start=(f == 0), stop=(f == KF - 1))
                    last.then_inc(o_ps, 1)
            groups(pe, first, group)

        @block.scalar
        def _(act):
            def feats(i):
                act.wait_ge(turned, i + 1)
                for k in range(KD):
                    nc.scalar.copy(n_feat[:, k, :], bank_t[k][:]).then_inc(feat_ready, 1)

            def group(i, more):
                for f in range(KF):
                    act.wait_ge(gu_ps, i * KF + (f + 1))
                    nc.scalar.activation(tanh[:, f % 2, :], bank_g[f % 2][:], ACT.Tanh, scale=0.5).then_inc(tanh_ready, 1)
                if more:
                    feats(i + 1)
            groups(act, lambda: feats(0), group)

        @block.vector
        def _(dve):
            v = nc.vector
            dve.sem_inc(hid_ready, 2)
            dve.sem_inc(added, 2)

            def first():
                norm_stats_dve(nc, dve, g, n, Links(dve, vec), 0)
                norm_apply_dve(nc, dve, g, n, 0)

            def group(i, more):
                link = Links(dve, vec, i * VEC_STEPS + 7)
                for f in range(KF):
                    dve.wait_ge(tanh_ready, i * KF + (f + 1))
                    link(v.scalar_tensor_tensor(out=silu[:, f % 2, :], in0=tanh[:, f % 2, :], scalar=1.0,
                                                in1=bank_g[f % 2][:], op0=ALU.add, op1=ALU.mult))
                    v.tensor_tensor(hid[:, f, :], silu[:, f % 2, :], bank_u[f % 2][:], ALU.mult).then_inc(hid_ready, 1)
                    if f == 1 and more:
                        norm_stats_dve(nc, dve, g, n, link, i + 1)
                    if f == 4 and more:
                        norm_apply_dve(nc, dve, g, n, i + 1)
                for j in range(GROUP):
                    dve.wait_ge(o_ps, i * GROUP + (j + 1))
                    q = i * GROUP + j
                    v.tensor_tensor(g.X[:, q, :], g.X[:, q, :], bank_o[j % 2][:], ALU.add).then_inc(added, 1)
                if more:
                    assert link.n == VEC_STEPS, link.n
            groups(dve, first, group)


def build_program(nc, dram):
    with ExitStack() as ctx:
        g = Shared()
        g.dram = dram
        g.sem = nc.alloc_semaphore

        def sb(name, *shape):
            return ctx.enter_context(nc.sbuf_tensor(name, list(shape), F32))
        g.X = sb("X", P, SEQS, D)
        g.moe_w2 = sb("moe_w2", P, EXPERTS, KF, D)
        g.xm_feat = g.moe_w2[:, EXPERTS - 2:].rearrange("p a b c -> p (a b c)").rearrange("p (k t) -> p k t", k=KD)
        g.moe_norm_w = sb("moe_norm_w", P, KD)
        g.moe_logits = ctx.enter_context(nc.sbuf_tensor("moe_logits", [P, SEQS, EXPERTS], F32))
        g.dest_at = ctx.enter_context(nc.sbuf_tensor("dest_at", [P, BLOCKS], U32))
        g.moe_prob = sb("moe_prob", P, 2, SEQS)
        g.xm_rows = nc.dram_tensor("xm_rows", (SEQS * P, D), F32, kind="Internal").ap()
        g.slot_out = nc.dram_tensor("slot_out", (TILES * P, D), F32, kind="Internal").ap()
        g.w2_loaded = g.sem("w2_loaded")
        g.ident, g.upto, g.after, g.ones = sb("ident", P, P), sb("upto", P, P), sb("after", P, P), sb("ones", P, P)
        g.neg_half = sb("neg_half", P, SEQS)
        g.x_loaded, g.a_exp = g.sem("x_loaded"), g.sem("a_exp")
        g.iota8 = sb("iota8", P, EXPERTS)
        mamba_phase(nc, g)
        before_moe = nc.snapshot_sems()
        moe_phase(nc, g)
        nc.clear_and_free_semaphores(nc.allocated_since(before_moe))
        nc.all_engine_barrier()
        wkv_switch_phase(nc, g)
        g.ffn = {m: g.moe_w2[:, n] for n, m in enumerate(("w2", "w2b", "w2h"))}
        g.ffn.update({m: g.moe_w2[:, n].rearrange("p a b -> p (a b)").rearrange("p (k f) -> p k f", k=KD)
                      for n, m in ((3, "w1"), (4, "w3"))})
        g.ffn["had"] = g.moe_w2[:, 5, 0, 0:P]
        g.ffn_w2_loaded, g.ffn_loaded = g.sem("ffn_w2_loaded"), g.sem("ffn_loaded")
        g.folded, g.w2h_ready = g.sem("folded"), g.sem("w2h_ready")
        gla_phase(nc, g)
        channel_phase(nc, g)
        ffn_phase(nc, g)


def _tiles(a):
    return a.reshape((a.shape[0] // P, P) + a.shape[1:]).swapaxes(0, 1)


def hadamard(n):
    h = np.ones((1, 1), np.float32)
    while len(h) < n:
        h = np.block([[h, h], [h, -h]])
    return h


def laid_out(inputs):
    f = {k: np.asarray(v) for k, v in inputs.items()}
    w = lambda name: f[name]
    return {
        "x": w("x"),
        "in_proj_w": _tiles(w("L0_attn_in_proj_w").T),
        "out_proj_w": _tiles(w("L0_attn_out_proj_w").T),
        "norm_mamba_w": _tiles(w("L0_attn_norm_mamba_w")),
        "norm_moe_w": _tiles(w("L0_attn_norm_moe_w")),
        "ssm_norm_w": _tiles(w("L0_attn_ssm_norm_w")),
        "conv_w": _tiles(w("L0_attn_conv_w")),
        "conv_b": _tiles(w("L0_attn_conv_b")),
        "dt_bias": w("L0_attn_dt_bias"),
        "gate_w": _tiles(w("L0_attn_gate_w").T),
        "moe_w1": w("L0_attn_w1").transpose(0, 2, 1).reshape(EXPERTS, KD, P, FF).swapaxes(1, 2),
        "moe_w2": w("L0_attn_w2").transpose(0, 2, 1).reshape(EXPERTS, KF, P, D).swapaxes(1, 2),
        "ctx_feat": w("ctx_2048").reshape(SEQS, P, KD, P).transpose(3, 2, 0, 1),
        "time_decay": _tiles(w("L0_xattn_time_decay")),
        "time_first": _tiles(w("L0_xattn_time_first")),
        "router_w": _tiles(w("L0_ffn_router_w").T),
        "switch_w1": _tiles(w("L0_ffn_w1").T),
        "switch_b1": _tiles(w("L0_ffn_b1")),
        "switch_w2": _tiles(w("L0_ffn_w2").T),
        "switch_b2": w("L0_ffn_b2").reshape(1, D),
        "gla_wq": _tiles(w("L1_attn_Wq").T),
        "gla_wk": _tiles(w("L1_attn_Wk").T),
        "gla_wv": _tiles(w("L1_attn_Wv").T),
        "gla_wg": _tiles(w("L1_attn_Wg").T),
        "gla_wo": _tiles(w("L1_attn_Wo").T),
        "gla_gamma": _tiles(w("L1_attn_gamma")),
        "gla_beta": _tiles(w("L1_attn_beta")),
        "ctx": w("ctx_2048"),
        "ffn_w1": _tiles(w("L1_ffn_W1").T),
        "ffn_w3": _tiles(w("L1_ffn_W3").T),
        "ffn_w2": _tiles(w("L1_ffn_W2").T),
        "ffn_had": hadamard(P),
        "A_log": w("L0_attn_A_log"),
        "D": w("L0_attn_D").reshape(CI, 2).T,
    }


def kernel(**inputs):
    import concourse.bacc as bacc
    from concourse.bass_utils import run_bass_kernel_spmd

    nc = bacc.Bacc("TRN2", target_bir_lowering=False, num_devices=1)
    arrays, handles = {}, {}
    for name, a in laid_out(inputs).items():
        a = np.ascontiguousarray(a)
        arrays[f"in_{name}"] = a
        handles[name] = nc.dram_tensor(f"in_{name}", a.shape, mybir.dt.from_np(a.dtype), kind="ExternalInput").ap()
    handles["out"] = nc.dram_tensor("out_x", (SEQS, P, D), F32, kind="ExternalOutput").ap()
    build_program(nc, handles)
    r = run_bass_kernel_spmd(nc, [arrays], core_ids=[0])
    return r.results[0]["out_x"]
```
